# Optimizing a Trainium2 kernel written in Bass

```python
import numpy as np
import jax
import jax.numpy as jnp

def _softmax(x, axis=-1):
    return jax.nn.softmax(x, axis=axis)

def _gelu(x):
    return jax.nn.gelu(x, approximate=True)

def _silu(x):
    return jax.nn.silu(x)

def _sigmoid(x):
    return jax.nn.sigmoid(x)

def _layernorm(x, axis=-1, eps=1e-05):
    m = jnp.mean(x, axis=axis, keepdims=True)
    v = jnp.var(x, axis=axis, keepdims=True)
    return (x - m) / jnp.sqrt(v + eps)

def _scatter_add(tgt, idx, src, axis=0):
    return tgt.at[idx].add(src)

def _segment_sum(src, seg, n):
    return jax.ops.segment_sum(src, seg, n)
kernel_name = 'mk_xattn_ffn_d1_seqx_r4_74fbb5'

def setup_inputs(seed: int=0):
    np.random.seed(seed)
    _w = jnp.asarray

    def _rec_inputs():
        import jax
        import jax.numpy as jnp
        _rk = jax.random.key(seed)
        x = -0.000929 + 1 * jax.random.normal(jax.random.fold_in(_rk, 1), (4, 512, 256), jnp.float32)
        _lenS = 512 - jax.random.randint(jax.random.fold_in(_rk, 7), (4,), 0, max(1, 512 // 4) + 1, jnp.int32)
        _lenS2 = 1024 - jax.random.randint(jax.random.fold_in(_rk, 8), (4,), 0, max(1, 1024 // 4) + 1, jnp.int32)
        _ctx_1024P = jax.random.normal(jax.random.fold_in(_rk, 11), (4, 16, 256), jnp.float32)
        _ctx_1024c = jax.random.dirichlet(jax.random.fold_in(_rk, 511), 0.3 * jnp.ones((16,), jnp.float32), (4, 1024))
        _ctx_1024t = jnp.einsum('bsk,bkd->bsd', _ctx_1024c, _ctx_1024P)
        _ctx_1024t = _ctx_1024t * jax.lax.rsqrt(jnp.mean(jnp.square(_ctx_1024t)) + 1e-12) * 0.953939
        ctx_1024 = -1.52775e-05 + 0.999936 * (_ctx_1024t + 0.3 * jax.random.normal(jax.random.fold_in(_rk, 611), (4, 1024, 256), jnp.float32))
        return (x, ctx_1024)
    x, ctx_1024 = _rec_inputs()

    def _L0_xattn_setup():
        import jax, jax.numpy as jnp
        import numpy as np
        DIM = 256
        H = 16
        D = 64
        INNER = H * D
        EPS = 1e-05

        def layernorm(x, w, b):
            mu = jnp.mean(x, axis=-1, keepdims=True)
            var = jnp.var(x, axis=-1, keepdims=True)
            return (x - mu) * jax.lax.rsqrt(var + EPS) * w + b
        key = jax.random.key(seed)
        ks = jax.random.split(key, 8)
        B, N, S = (4, 64, 2048)
        s = 1.0 / np.sqrt(DIM)
        return {'latents': jax.random.normal(ks[0], (B, N, DIM), jnp.float32), 'context': jax.random.normal(ks[1], (B, S, DIM), jnp.float32), 'ln_l_w': jnp.ones((DIM,), jnp.float32), 'ln_l_b': jnp.zeros((DIM,), jnp.float32), 'ln_c_w': jnp.ones((DIM,), jnp.float32), 'ln_c_b': jnp.zeros((DIM,), jnp.float32), 'Wq': jax.random.normal(ks[2], (DIM, INNER), jnp.float32) * s, 'Wkv': jax.random.normal(ks[3], (DIM, 2 * INNER), jnp.float32) * s, 'Wo': jax.random.normal(ks[4], (INNER, DIM), jnp.float32) * (1.0 / np.sqrt(INNER)), 'bo': jnp.zeros((DIM,), jnp.float32)}
    _L0_xattn_all = _L0_xattn_setup()
    _L0_xattn_in = {k: v for k, v in _L0_xattn_all.items() if k in ('ln_l_w', 'ln_l_b', 'ln_c_w', 'ln_c_b', 'Wq', 'Wkv', 'Wo', 'bo')}
    del _L0_xattn_all

    def _L0_ffn_setup():
        import jax, jax.numpy as jnp
        import numpy as np
        TOP_K = 2
        LN_EPS = 1e-05
        B, S, H, E, F = (2, 512, 256, 8, 1024)

        def _layernorm(x, w, b):
            mu = jnp.mean(x, axis=-1, keepdims=True)
            var = jnp.mean(jnp.square(x - mu), axis=-1, keepdims=True)
            return (x - mu) * jax.lax.rsqrt(var + LN_EPS) * w + b
        key = jax.random.key(seed)
        ks = jax.random.split(key, 6)
        x = jax.random.normal(ks[0], (B, S, H), dtype=jnp.float32)
        Wg = jax.random.normal(ks[1], (H, E), dtype=jnp.float32) * 0.02
        alpha = jax.random.normal(ks[2], (E,), dtype=jnp.float32)
        ln_w = jnp.ones((E, H), dtype=jnp.float32)
        ln_b = jnp.zeros((E, H), dtype=jnp.float32)
        fc1_w = jax.random.normal(ks[3], (E, H, F), dtype=jnp.float32) * 0.02
        fc1_b = jnp.zeros((E, F), dtype=jnp.float32)
        fc2_w = jax.random.normal(ks[4], (E, F, H), dtype=jnp.float32) * 0.02
        fc2_b = jnp.zeros((E, H), dtype=jnp.float32)
        return {'x': x, 'Wg': Wg, 'alpha': alpha, 'ln_w': ln_w, 'ln_b': ln_b, 'fc1_w': fc1_w, 'fc1_b': fc1_b, 'fc2_w': fc2_w, 'fc2_b': fc2_b}
    _L0_ffn_all = _L0_ffn_setup()
    _L0_ffn_in = {k: v for k, v in _L0_ffn_all.items() if k in ('Wg', 'alpha', 'ln_w', 'ln_b', 'fc1_w', 'fc1_b', 'fc2_w', 'fc2_b')}
    del _L0_ffn_all
    return {'x': x, 'ctx_1024': ctx_1024, 'L0_xattn_ln_l_w': _L0_xattn_in['ln_l_w'], 'L0_xattn_ln_l_b': _L0_xattn_in['ln_l_b'], 'L0_xattn_ln_c_w': _L0_xattn_in['ln_c_w'], 'L0_xattn_ln_c_b': _L0_xattn_in['ln_c_b'], 'L0_xattn_Wq': _L0_xattn_in['Wq'], 'L0_xattn_Wkv': _L0_xattn_in['Wkv'], 'L0_xattn_Wo': _L0_xattn_in['Wo'], 'L0_xattn_bo': _L0_xattn_in['bo'], 'L0_ffn_Wg': _L0_ffn_in['Wg'], 'L0_ffn_alpha': _L0_ffn_in['alpha'], 'L0_ffn_ln_w': _L0_ffn_in['ln_w'], 'L0_ffn_ln_b': _L0_ffn_in['ln_b'], 'L0_ffn_fc1_w': _L0_ffn_in['fc1_w'], 'L0_ffn_fc1_b': _L0_ffn_in['fc1_b'], 'L0_ffn_fc2_w': _L0_ffn_in['fc2_w'], 'L0_ffn_fc2_b': _L0_ffn_in['fc2_b']}

def reference(x, ctx_1024, L0_xattn_ln_l_w, L0_xattn_ln_l_b, L0_xattn_ln_c_w, L0_xattn_ln_c_b, L0_xattn_Wq, L0_xattn_Wkv, L0_xattn_Wo, L0_xattn_bo, L0_ffn_Wg, L0_ffn_alpha, L0_ffn_ln_w, L0_ffn_ln_b, L0_ffn_fc1_w, L0_ffn_fc1_b, L0_ffn_fc2_w, L0_ffn_fc2_b):
    import jax
    import jax.numpy as jnp

    def _L0_xattn_ref(latents, context, ln_l_w, ln_l_b, ln_c_w, ln_c_b, Wq, Wkv, Wo, bo):
        import jax, jax.numpy as jnp
        import numpy as np
        DIM = 256
        H = 16
        D = 64
        INNER = H * D
        EPS = 1e-05

        def layernorm(x, w, b):
            mu = jnp.mean(x, axis=-1, keepdims=True)
            var = jnp.var(x, axis=-1, keepdims=True)
            return (x - mu) * jax.lax.rsqrt(var + EPS) * w + b
        b, n, _ = latents.shape
        s = context.shape[1]
        lat = layernorm(latents, ln_l_w, ln_l_b)
        ctx = layernorm(context, ln_c_w, ln_c_b)
        q = (lat @ Wq).reshape(b, n, H, D).transpose(0, 2, 1, 3)
        kv = ctx @ Wkv
        k, v = jnp.split(kv, 2, axis=-1)
        k = k.reshape(b, s, H, D).transpose(0, 2, 1, 3)
        v = v.reshape(b, s, H, D).transpose(0, 2, 1, 3)
        scale = D ** (-0.5)
        attn = jnp.einsum('bhnd,bhsd->bhns', q, k) * scale
        attn = jnp.clip(attn, -11.0, 11.0)
        attn = jax.nn.softmax(attn, axis=-1)
        out = jnp.einsum('bhns,bhsd->bhnd', attn, v)
        out = out.transpose(0, 2, 1, 3).reshape(b, n, INNER)
        return out @ Wo + bo

    def _L0_ffn_ref(x, Wg, alpha, ln_w, ln_b, fc1_w, fc1_b, fc2_w, fc2_b):
        import jax, jax.numpy as jnp
        import numpy as np
        TOP_K = 2
        LN_EPS = 1e-05
        B, S, H, E, F = (2, 512, 256, 8, 1024)

        def _layernorm(x, w, b):
            mu = jnp.mean(x, axis=-1, keepdims=True)
            var = jnp.mean(jnp.square(x - mu), axis=-1, keepdims=True)
            return (x - mu) * jax.lax.rsqrt(var + LN_EPS) * w + b
        b, s, h = x.shape
        xf = x.reshape(-1, h)
        logits = xf @ Wg
        top_vals, top_idx = jax.lax.top_k(logits, TOP_K)
        gate_score = jax.nn.softmax(top_vals, axis=-1)
        one_hot = jax.nn.one_hot(top_idx, Wg.shape[1], dtype=xf.dtype)
        comb = jnp.einsum('tke,tk->te', one_hot, gate_score) * alpha
        out = jnp.zeros_like(xf)
        for e in range(Wg.shape[1]):
            hdn = _layernorm(xf, ln_w[e], ln_b[e])
            a = jax.nn.gelu(hdn @ fc1_w[e] + fc1_b[e], approximate=True)
            y = a @ fc2_w[e] + fc2_b[e]
            out = out + y * comb[:, e:e + 1]
        return out.reshape(b, s, h)
    x = x + _L0_xattn_ref(_layernorm(x, axis=-1), ctx_1024, L0_xattn_ln_l_w, L0_xattn_ln_l_b, L0_xattn_ln_c_w, L0_xattn_ln_c_b, L0_xattn_Wq, L0_xattn_Wkv, L0_xattn_Wo, L0_xattn_bo)
    x = x + _L0_ffn_ref(_layernorm(x, axis=-1), L0_ffn_Wg, L0_ffn_alpha, L0_ffn_ln_w, L0_ffn_ln_b, L0_ffn_fc1_w, L0_ffn_fc1_b, L0_ffn_fc2_w, L0_ffn_fc2_b)
    return x

_drawn_inputs = setup_inputs


def setup_inputs(seed=0):
    import zlib

    import numpy as np

    out = dict(_drawn_inputs(seed))
    spreads = {'L0_xattn_ln_l_w': (1.0, 0.2),
     'L0_xattn_ln_l_b': (0.0, 0.445),
     'L0_xattn_ln_c_w': (1.0, 0.2),
     'L0_xattn_ln_c_b': (0.0, 0.1),
     'L0_xattn_bo': (0.0, 0.1),
     'L0_ffn_ln_w': (1.0, 0.6),
     'L0_ffn_ln_b': (0.0, 0.8),
     'L0_ffn_fc1_b': (0.0, 0.469),
     'L0_ffn_fc2_b': (0.0, 0.1)}
    factors = {}
    for name, (base, spread) in spreads.items():
        noise = np.random.default_rng([zlib.crc32(name.encode()), seed]).standard_normal(out[name].shape)
        drawn = base * np.exp(spread * noise) if base else spread * noise
        out[name] = jnp.asarray(drawn.astype(out[name].dtype))
    for name, factor in factors.items():
        out[name] = (out[name] * factor).astype(out[name].dtype)
    return out
```

```python
from contextlib import ExitStack
import math

import concourse.bass as bass
from concourse import mybir

F32 = mybir.dt.float32
F16 = mybir.dt.float16
U32 = mybir.dt.uint32
ALU = mybir.AluOpType
ACT = mybir.ActivationFunctionType

P = 128
B = 4
N = 512
S = 1024
D = 256
KD = D // P
H = 16
DH = 64
INNER = H * DH
KI = INNER // P
NT = N // P
ST = S // P
EPS = 1e-5
CLIP = 11.0
W_SCALE = 16.0
LO_SCALE = 2048.0
VW = 130
UNITS = 8
LEAD = 3
E_RING = 4
P_RING = 4
TT = B * NT

E = 8
F = 1024
KF = F // P
F_SCALE = 64.0
G_LEAD = 2
A_RING = 4
H_BANKS = 3
BLOCKS = TT // NT
STEPS = BLOCKS * KF

ROW_B1, ROW_LNW, ROW_LNB, ROW_LW, ROW_LB, ROW_CW, ROW_CB = 0, 64, 80, 96, 98, 100, 102


def attention_block(nc, A, T):
    with ExitStack() as ctx:
        def sb(name, shape, dt):
            return ctx.enter_context(nc.sbuf_tensor(name, shape, dt))

        def sem(name):
            return ctx.enter_context(nc.semaphore(name))

        x1, ident, vec_t = T["x1"], T["ident"], T["vec_t"]
        wq_hi, wq_lo = sb("wq_hi", [P, KD, INNER], F16), sb("wq_lo", [P, KD, INNER], F16)
        wkv_hi, wkv_lo = sb("wkv_hi", [P, KD, 2 * INNER], F16), sb("wkv_lo", [P, KD, 2 * INNER], F16)
        wo_hi, wo_lo = sb("wo_hi", [P, KI, D], F16), sb("wo_lo", [P, KI, D], F16)
        stage = sb("stage", [P, 8192], F32)
        vec_rows = sb("vec_rows", [P, P], F32)
        bo_all = sb("bo_all", [P, D], F32)
        ctx_in = sb("ctx_in", [P, ST, D], F32)
        x_in = sb("x_in", [P, NT, D], F32)
        lat = sb("lat", [P, NT, D], F32)
        stats = sb("stats", [P, ST, 6], F32)
        mean_var = sb("mean_var", [P, 16, 2], F32)
        var_eps = sb("var_eps", [P, 16], F32)
        rstd = sb("rstd", [P, 16], F32)
        minus_half = sb("minus_half", [P, 16], F32)
        eps = sb("eps", [P, 16], F32)
        ln_lo_scale = sb("ln_lo_scale", [P, 1], F32)
        warm = sb("warm", [P, 1], F32)
        affine = sb("affine", [P, 2, N], F32)
        ctx_hi, ctx_lo = sb("ctx_hi", [P, KD, S], F16), sb("ctx_lo", [P, KD, S], F16)
        lat_hi, lat_lo = sb("lat_hi", [P, KD, N], F16), sb("lat_lo", [P, KD, N], F16)
        keys = sb("keys", [P, 2, 2, S], F16)
        qrys = sb("qrys", [P, 2, 2, 2, N], F16)
        vals = sb("vals", [P, 2, ST, 2, VW], F16)
        vals_s = sb("vals_s", [P, 2, ST, 2, 66], F16)
        expo = sb("expo", [P, E_RING, 2 * N], F32)
        p_hi, p_lo = sb("p_hi", [P, P_RING, 2 * N], F16), sb("p_lo", [P, P_RING, 2 * N], F16)
        o_lo = sb("o_lo", [P, NT, DH], F32)
        o_sum = sb("o_sum", [P, 2, NT, DH], F32)
        o_rec = sb("o_rec", [P, 2, NT], F32)
        attn = stage[:, 0:NT * INNER].rearrange("p (n i) -> p n i", n=NT)
        attn_t = stage[:, NT * INNER:].bitcast(F16).rearrange("p (c j n) -> p c j n", c=2, j=KI)
        wkv_in = stage[:, 0:KD * 2 * INNER].rearrange("p (k n) -> p k n", k=KD)
        wq_in = stage[:, 4096:6144].rearrange("p (k n) -> p k n", k=KD)
        wo_in = stage[:, 6144:8192].rearrange("p (k n) -> p k n", k=KI)

        ps = T["ps"]
        S_BANK, O_BANK, J_BANK = 0, 4, 6

        def o_ps(n):
            return ps[:, O_BANK + n // 2, (n % 2) * 256:(n % 2) * 256 + 129]

        o_all = ps[:, O_BANK:O_BANK + 2, :].rearrange("p b (h c) -> p (b h) c", h=2)

        w_in, ctx_loaded, x_loaded = sem("w_in"), sem("ctx_loaded"), sem("x_loaded")
        vec_in, consts, vec_turned, vec_done = sem("vec_in"), sem("consts"), sem("vec_turned"), sem("vec_done")
        wait_taken, bo_in = sem("wait_taken"), sem("bo_in")
        ident_done, pool_chain, dve_chain = sem("ident_done"), sem("pool_chain"), sem("dve_chain")
        w_hi_done, w_lo_done = sem("w_hi_done"), sem("w_lo_done")
        moments, rstd_done, residual_done = sem("moments"), sem("rstd_done"), sem("residual_done")
        normed, turned, affine_done, split_done = sem("normed"), sem("turned"), sem("affine_done"), sem("split_done")
        proj_ready, proj_hi, proj_free, q_twice = sem("proj_ready"), sem("proj_hi"), sem("proj_free"), sem("q_twice")
        scores_ready, exp_done, clip_done, hi_done, lo_done = (
            sem("scores_ready"), sem("exp_done"), sem("clip_done"), sem("hi_done"), sem("lo_done"))
        pv_done, o_lo_done, o_free, o_step, attn_done = (
            sem("pv_done"), sem("o_lo_done"), sem("o_free"), sem("o_step"), sem("attn_done"))
        at_ready, at_hi, at_lo, y_ready, x1_done = (
            sem("at_ready"), sem("at_hi"), sem("at_lo"), sem("y_ready"), sem("x1_done"))
        FREE = {exp_done: 2, lo_done: E_RING, pv_done: P_RING, o_free: 1, attn_done: 2, proj_free: 1,
                split_done: 2, x1_done: NT}

        block = ctx.enter_context(nc.Block())

        def pair_loop(eng, b, pair):
            with eng.Fori(0, KI // 2 - 1) as mm:
                pair(b, 2 * mm, 0, False)
                pair(b, 2 * mm + 1, 1, False)
            pair(b, KI - 2, 0, False)
            pair(b, KI - 1, 1, True)

        @block.sync
        def _(sp):
            ctx_v = A["ctx_1024"].rearrange("b (t p) d -> b p t d", p=P)
            x_v = A["x"].rearrange("b (t p) d -> b p t d", p=P)
            sp.dma_start(ctx_in[:], ctx_v[0]).then_inc(ctx_loaded, 16)
            sp.dma_start(x_in[:], x_v[0]).then_inc(x_loaded, 16)
            sp.dma_start(wkv_in, A["L0_xattn_Wkv"].rearrange("(k p) n -> p k n", p=P)).then_inc(w_in, 16)
            sp.dma_start(wq_in, A["L0_xattn_Wq"].rearrange("(k p) n -> p k n", p=P)).then_inc(w_in, 16)
            sp.dma_start(wo_in, A["L0_xattn_Wo"].rearrange("(k p) n -> p k n", p=P)).then_inc(w_in, 16)

            def q_to_upper(pairs_before, parity):
                sp.wait_ge(proj_free, pairs_before * 5 + 1 + FREE[proj_free])
                sp.dma_start(qrys[DH:P, parity], qrys[0:DH, parity]).then_inc(q_twice, 16)

            def batch(b, load_next):
                q_to_upper(b * KI, 0)
                if load_next:
                    sp.wait_ge(turned, (b + 1) * 6)
                    sp.dma_start(ctx_in[:], ctx_v[bass.ds(b + 1, 1)].rearrange("o p t d -> (o p) t d")).then_inc(ctx_loaded, 16)
                    sp.wait_ge(residual_done, b + 1)
                    sp.dma_start(x_in[:], x_v[bass.ds(b + 1, 1)].rearrange("o p t d -> (o p) t d")).then_inc(x_loaded, 16)

                def pair(b, m, parity, last):
                    if not last:
                        q_to_upper(b * KI + m + 1, 1 - parity)
                pair_loop(sp, b, pair)

            with sp.Fori(0, B - 1) as b:
                batch(b, True)
            batch(B - 1, False)

        @block.gpsimd
        def _(pool):
            chain = [0]

            def link(ins):
                chain[0] += 1
                ins.then_inc(pool_chain, 1)
                pool.wait_ge(pool_chain, chain[0])

            pool.sem_inc(attn_done, FREE[attn_done])
            link(pool.memset(ident[:], 0.0))
            pool.affine_select(out=ident[:], in_=ident[:], compare_op=ALU.not_equal, fill=1.0, base=0,
                               pattern=[[-1, P]], channel_multiplier=1).then_inc(ident_done, 1)
            link(pool.memset(minus_half[:], -0.5))
            link(pool.memset(eps[:], EPS))
            pool.dma_start(bo_all[:], A["L0_xattn_bo"].partition_broadcast(P)).then_inc(bo_in, 16)
            PER_BATCH = 3

            def root(b, nth, a, z):
                pool.wait_ge(moments, b * 3 + nth + 1)
                pool.tensor_tensor(var_eps[:, a:z], mean_var[:, a:z, 1], eps[:, a:z], ALU.add).then_inc(pool_chain, 1)
                pool.wait_ge(pool_chain, b * PER_BATCH + nth + 1 + chain[0])
                pool.tensor_tensor(rstd[:, a:z], var_eps[:, a:z], minus_half[:, a:z], ALU.pow).then_inc(rstd_done, 1)

            with pool.Fori(0, B) as b:
                root(b, 0, 0, 8)
                root(b, 1, 8, 12)
                root(b, 2, 12, 16)
                pool.wait_ge(x_loaded, b * 16 + 16)
                pool.wait_ge(bo_in, 16)
                pool.tensor_tensor(x1[:, bass.ds(b * NT, NT), :], x_in[:],
                                   bo_all[:].unsqueeze(1).broadcast_to([P, NT, D]), ALU.add).then_inc(residual_done, 1)

                def pair(b, m, parity, last):
                    for h in range(2):
                        pool.wait_ge(o_free, b * H + m * 2 + h + 1 + FREE[o_free])
                        pool.tensor_tensor(attn[:, :, bass.ds(m * P + h * DH, DH)], o_sum[:, h],
                                           o_rec[:, h].unsqueeze(2).broadcast_to([P, NT, DH]),
                                           ALU.mult).then_inc(attn_done, 1)
                pair_loop(pool, b, pair)

        @block.scalar
        def _(act):
            act.sem_inc(exp_done, FREE[exp_done])
            for view, row in ((A["L0_ffn_fc1_b"].rearrange("e (f p) -> (e f) p", p=P), ROW_B1),
                              (A["L0_ffn_ln_w"].rearrange("e (k p) -> (e k) p", p=P), ROW_LNW),
                              (A["L0_ffn_ln_b"].rearrange("e (k p) -> (e k) p", p=P), ROW_LNB),
                              (A["L0_xattn_ln_l_w"].rearrange("(k p) -> k p", p=P), ROW_LW),
                              (A["L0_xattn_ln_l_b"].rearrange("(k p) -> k p", p=P), ROW_LB),
                              (A["L0_xattn_ln_c_w"].rearrange("(k p) -> k p", p=P), ROW_CW),
                              (A["L0_xattn_ln_c_b"].rearrange("(k p) -> k p", p=P), ROW_CB)):
                if row == ROW_B1:
                    act.wait_ge(consts, 1)
                act.dma_start(vec_rows[row:row + view.shape[0], :], view).then_inc(vec_in, 16)
            act.wait_ge(consts, 2)
            act.activation(warm[:], ln_lo_scale[:], ACT.Exp)
            act.wait_ge(w_in, 48)
            for k in range(KD):
                act.activation(wkv_hi[:, k], wkv_in[:, k], ACT.Copy, scale=W_SCALE).then_inc(w_hi_done, 1)
            act.activation(wq_hi[:], wq_in, ACT.Copy, scale=W_SCALE).then_inc(w_hi_done, 1)
            act.activation(wo_hi[:], wo_in, ACT.Copy, scale=W_SCALE).then_inc(w_hi_done, 1)

            def proj_hi_part(pairs_before, c, parity):
                act.wait_ge(proj_ready, pairs_before * 5 + c + 1)
                if c == 0:
                    act.activation(qrys[0:DH, parity, 0, 0], ps[0:DH, J_BANK], ACT.Copy, scale=1 / W_SCALE)
                    act.activation(qrys[0:DH, parity, 1, 0], ps[DH:P, J_BANK], ACT.Copy,
                                   scale=1 / W_SCALE).then_inc(proj_hi, 1)
                elif c < 3:
                    bank, t = J_BANK + c % 2, slice((c - 1) * 512, c * 512)
                    act.activation(keys[0:DH, parity, 0, t], ps[0:DH, bank], ACT.Copy, scale=1 / W_SCALE)
                    act.activation(keys[DH:P, parity, 1, t], ps[DH:P, bank], ACT.Copy,
                                   scale=1 / W_SCALE).then_inc(proj_hi, 1)
                else:
                    bank, t = J_BANK + c % 2, slice((c - 3) * 4, (c - 2) * 4)
                    act.activation(vals[:, parity, t, :, DH:2 * DH].rearrange("p t h d -> p (t h) d"),
                                   ps[:, bank, :].rearrange("p (t d) -> p t d", d=DH),
                                   ACT.Copy, scale=1 / W_SCALE).then_inc(proj_hi, 1)

            def exp(unit, j):
                act.wait_ge(scores_ready, unit + 1)
                act.wait_ge(lo_done, unit + 1)
                act.activation(expo[:, j % E_RING],
                               ps[:, S_BANK + 2 * (j % 2):S_BANK + 2 * (j % 2) + 2, :].rearrange("p a b -> p (a b)"),
                               ACT.Exp, scale=DH ** -0.5, bias=ln_lo_scale[:, 0:1]).then_inc(exp_done, 1)

            def hi(unit, j):
                act.wait_ge(clip_done, unit + 1)
                act.wait_ge(pv_done, unit + 1)
                act.activation(p_hi[:, j % P_RING], expo[:, j % E_RING], ACT.Copy,
                               scale=1 / LO_SCALE).then_inc(hi_done, 1)

            def out_lo(head):
                act.wait_ge(pv_done, head * 4 + 4 + FREE[pv_done])
                act.wait_ge(o_free, head + FREE[o_free])
                act.activation(o_lo[:], o_all[:, :, 0:DH], ACT.Copy).then_inc(o_lo_done, 1)

            with act.Fori(0, B) as b:
                for i in range(6):
                    row_w, row_b, k = (ROW_CW, ROW_CB, i // 2) if i < 4 else (ROW_LW, ROW_LB, i - 4)
                    act.wait_ge(turned, b * 6 + i + 1)
                    if i == 0:
                        act.wait_ge(vec_done, 1)
                    act.wait_ge(split_done, b * 6 + i + 1)
                    act.activation(affine[:, i % 2], ps[:, i], ACT.Identity, bias=vec_t[:, row_b + k:row_b + k + 1],
                                   scale=vec_t[:, row_w + k:row_w + k + 1]).then_inc(affine_done, 1)
                for c in range(5):
                    proj_hi_part(b * KI, c, 0)
                first = b * (KI * UNITS)
                exp(first, 0)
                exp(first + 1, 1)
                hi(first, 0)
                exp(first + 2, 2)
                hi(first + 1, 1)

                def pair(b, m, parity, last):
                    unit, head = (b * KI + m) * UNITS, (b * KI + m) * 2
                    for j in range(UNITS):
                        if j == UNITS // 2:
                            out_lo(head)
                        if not last or j + LEAD < UNITS:
                            exp(unit + j + LEAD, j + LEAD)
                        if not last or j + LEAD - 1 < UNITS:
                            hi(unit + j + LEAD - 1, j + LEAD - 1)
                        if not last and j < 5:
                            proj_hi_part(b * KI + m + 1, j, 1 - parity)
                    out_lo(head + 1)
                pair_loop(act, b, pair)
                for j in range(KI):
                    act.wait_ge(at_ready, b * KI + j + 1)
                    act.activation(attn_t[:, 0, j], ps[:, j], ACT.Copy).then_inc(at_hi, 1)

        @block.vector
        def _(dve):
            for s in (lo_done, o_free, proj_free, split_done, x1_done):
                dve.sem_inc(s, FREE[s])
            dve.memset(vec_rows[:], 0.0).then_inc(consts, 1)
            dve.memset(ln_lo_scale[:], math.log(LO_SCALE)).then_inc(consts, 1)
            dve.memset(vals[:, :, :, :, 2 * DH:VW].rearrange("p a t h d -> p (a t h) d"), 1.0)
            dve.memset(vals_s[:, :, :, :, DH:DH + 2].rearrange("p a t h d -> p (a t h) d"), 1 / LO_SCALE)

            def lo_of(out, full, hi, scale):
                return dve.scalar_tensor_tensor(out=out, in0=full, scalar=scale, in1=hi, op0=ALU.mult, op1=ALU.subtract)

            dve.wait_ge(vec_turned, 1)
            dve.tensor_copy(vec_t[:], ps[:, 7, 0:P]).then_inc(vec_done, 1)
            for k in range(KD):
                dve.wait_ge(w_hi_done, k + 1)
                lo_of(wkv_lo[:, k], wkv_in[:, k], wkv_hi[:, k], W_SCALE).then_inc(w_lo_done, 1)
            dve.wait_ge(w_hi_done, KD + 1)
            lo_of(wq_lo[:], wq_in, wq_hi[:], W_SCALE).then_inc(w_lo_done, 1)
            dve.wait_ge(w_hi_done, KD + 2)
            lo_of(wo_lo[:], wo_in, wo_hi[:], W_SCALE).then_inc(w_lo_done, 1)

            def proj_lo_part(pairs_before, c, parity):
                dve.wait_ge(proj_hi, pairs_before * 5 + c + 1)
                if c == 0:
                    lo_of(qrys[0:DH, parity, 0, 1], ps[0:DH, J_BANK], qrys[0:DH, parity, 0, 0], 1 / W_SCALE)
                    lo_of(qrys[0:DH, parity, 1, 1], ps[DH:P, J_BANK], qrys[0:DH, parity, 1, 0],
                          1 / W_SCALE).then_inc(proj_free, 1)
                elif c < 3:
                    bank, t = J_BANK + c % 2, slice((c - 1) * 512, c * 512)
                    lo_of(keys[DH:P, parity, 0, t], ps[0:DH, bank], keys[0:DH, parity, 0, t], 1 / W_SCALE)
                    lo_of(keys[0:DH, parity, 1, t], ps[DH:P, bank], keys[DH:P, parity, 1, t],
                          1 / W_SCALE).then_inc(proj_free, 1)
                else:
                    bank, t = J_BANK + c % 2, slice((c - 3) * 4, (c - 2) * 4)
                    v = vals[:, parity, t].rearrange("p t h d -> p (t h) d")
                    dve.tensor_scalar(vals_s[:, parity, t, :, 0:DH].rearrange("p t h d -> p (t h) d"),
                                      v[:, :, DH:2 * DH], 1 / LO_SCALE, None, ALU.mult)
                    lo_of(v[:, :, 0:DH], ps[:, bank, :].rearrange("p (t d) -> p t d", d=DH),
                          v[:, :, DH:2 * DH], 1 / W_SCALE).then_inc(proj_free, 1)

            def clip(unit, j):
                dve.wait_ge(exp_done, unit + 1 + FREE[exp_done])
                e = expo[:, j % E_RING]
                dve.tensor_scalar(e, e, LO_SCALE * math.exp(CLIP), LO_SCALE * math.exp(-CLIP),
                                  ALU.min, ALU.max).then_inc(clip_done, 1)

            def lo(unit, j):
                dve.wait_ge(hi_done, unit + 1)
                dve.scalar_tensor_tensor(out=p_lo[:, j % P_RING], in0=p_hi[:, j % P_RING], scalar=-LO_SCALE,
                                         in1=expo[:, j % E_RING], op0=ALU.mult, op1=ALU.add).then_inc(lo_done, 1)

            def out_sum(head, h):
                dve.wait_ge(o_lo_done, head + 1)
                dve.wait_ge(attn_done, head + 1)
                dve.reciprocal(o_rec[:, h], o_all[:, :, 2 * DH])
                dve.tensor_tensor(o_sum[:, h], o_all[:, :, DH:2 * DH], o_lo[:], ALU.add).then_inc(o_free, 1)

            CHAIN = 4

            with dve.Fori(0, B) as b:
                steps = [0]

                def link(ins):
                    steps[0] += 1
                    ins.then_inc(dve_chain, 1)
                    dve.wait_ge(dve_chain, b * CHAIN + steps[0])

                def tile_moments(tokens, tiles, at):
                    for t in range(tiles):
                        ins = dve.bn_stats(stats[:, t, :], tokens[:, t, :])
                    link(ins)
                    dve.sem_inc(wait_taken, 1)
                    for t in range(tiles):
                        ins = dve.bn_aggr(mean_var[:, at + t, :], stats[:, t, :])
                    return ins

                def normalise(out, tokens, tiles, at):
                    for t in range(tiles):
                        ins = dve.tensor_scalar(out[:, t, :], tokens[:, t, :], mean_var[:, at + t, 0:1],
                                                rstd[:, at + t:at + t + 1], ALU.subtract, ALU.mult)
                    return ins

                dve.wait_ge(ctx_loaded, b * 16 + 16)
                tile_moments(ctx_in, ST, 0).then_inc(moments, 1)
                dve.wait_ge(x_loaded, b * 16 + 16)
                dve.wait_ge(moments, b * 3 + 1)
                tile_moments(x_in, NT, 8).then_inc(moments, 1)
                dve.wait_ge(rstd_done, b * 3 + 1)
                normalise(ctx_in, ctx_in, ST, 0).then_inc(normed, 1)
                dve.wait_ge(rstd_done, b * 3 + 2)
                link(normalise(lat, x_in, NT, 8))
                tile_moments(lat, NT, 12).then_inc(moments, 1)
                dve.wait_ge(rstd_done, b * 3 + 3)
                normalise(lat, lat, NT, 12).then_inc(normed, 1)
                for i in range(6):
                    hi_, lo_, k = (ctx_hi, ctx_lo, i // 2) if i < 4 else (lat_hi, lat_lo, i - 4)
                    t = slice((i % 2) * N, (i % 2) * N + N) if i < 4 else slice(0, N)
                    dve.wait_ge(affine_done, b * 6 + i + 1)
                    dve.tensor_copy(hi_[:, k, t], affine[:, i % 2]).then_inc(o_step, 1)
                    dve.wait_ge(o_step, b * 6 + i + 1)
                    dve.tensor_tensor(lo_[:, k, t], affine[:, i % 2], hi_[:, k, t], ALU.subtract).then_inc(split_done, 1)
                for c in range(5):
                    proj_lo_part(b * KI, c, 0)
                first = b * (KI * UNITS)
                clip(first, 0)
                clip(first + 1, 1)
                lo(first, 0)
                clip(first + 2, 2)
                lo(first + 1, 1)

                def pair(b, m, parity, last):
                    unit, head = (b * KI + m) * UNITS, (b * KI + m) * 2
                    for j in range(UNITS):
                        if j == UNITS // 2:
                            out_sum(head, 0)
                        if not last or j + LEAD < UNITS:
                            clip(unit + j + LEAD, j + LEAD)
                        if not last or j + LEAD - 1 < UNITS:
                            lo(unit + j + LEAD - 1, j + LEAD - 1)
                        if not last and j < 5:
                            proj_lo_part(b * KI + m + 1, j, 1 - parity)
                    out_sum(head + 1, 1)
                pair_loop(dve, b, pair)
                for j in range(KI):
                    dve.wait_ge(at_hi, b * KI + j + 1)
                    dve.tensor_tensor(attn_t[:, 1, j], ps[:, j], attn_t[:, 0, j], ALU.subtract).then_inc(at_lo, 1)
                for n in range(NT):
                    dve.wait_ge(y_ready, b * NT + n + 1)
                    tile = x1[:, bass.ds(b * NT + n, 1), :].rearrange("p o d -> p (o d)")
                    if n == 0:
                        dve.wait_ge(residual_done, b + 1)
                    dve.scalar_tensor_tensor(out=tile, in0=ps[:, n, 0:D], scalar=1 / W_SCALE, in1=tile,
                                             op0=ALU.mult, op1=ALU.add).then_inc(x1_done, 1)

        @block.tensor
        def _(pe):
            pe.sem_inc(pv_done, FREE[pv_done])
            pe.wait_ge(ident_done, 1)
            pe.wait_ge(vec_in, 16 * 7)
            pe.transpose(ps[:, 7, 0:P], vec_rows[:], ident[:]).then_inc(vec_turned, 1)
            pe.wait_ge(w_lo_done, KD + 2)

            def pairs3(out, w_hi, w_lo, x_hi, x_lo, first, last):
                pe.matmul(out, w_hi, x_hi, start=first, stop=False, skip_group_check=True)
                pe.matmul(out, w_hi, x_lo, start=False, stop=False, skip_group_check=True)
                return pe.matmul(out, w_lo, x_hi, start=False, stop=last, skip_group_check=True)

            def project(pairs_before, m, c, parity):
                pe.wait_ge(proj_free, pairs_before * 5 + c + (FREE[proj_free] if c == 0 else 0))
                out = ps[:, J_BANK + c % 2, :]
                if c < 3:
                    w_hi, w_lo = (wq_hi, wq_lo) if c == 0 else (wkv_hi, wkv_lo)
                    x_hi, x_lo = (lat_hi, lat_lo) if c == 0 else (ctx_hi, ctx_lo)
                    t = slice(0, N) if c == 0 else slice((c - 1) * 512, c * 512)
                    for k in range(KD):
                        w = bass.ds(m * P, P)
                        ins = pairs3(out, w_hi[:, k, w], w_lo[:, k, w], x_hi[:, k, t], x_lo[:, k, t],
                                     k == 0, k == KD - 1)
                else:
                    for t4 in range(4):
                        t = slice(((c - 3) * 4 + t4) * P, ((c - 3) * 4 + t4 + 1) * P)
                        for k in range(KD):
                            w = bass.ds(m * P + INNER, P)
                            ins = pairs3(out[:, t4 * P:(t4 + 1) * P], ctx_hi[:, k, t], ctx_lo[:, k, t],
                                         wkv_hi[:, k, w], wkv_lo[:, k, w], k == 0 and t4 == 0, k == KD - 1)
                ins.then_inc(proj_ready, 1)

            def scores(unit, j, parity):
                h, u = j // 4, j % 4
                pe.wait_ge(exp_done, unit + 1)
                for t in range(2):
                    k = keys[:, parity, h, (2 * u + t) * P:(2 * u + t + 1) * P]
                    out = ps[:, S_BANK + 2 * (j % 2) + t, :]
                    pe.matmul(out, k, qrys[:, parity, h, 0], start=True, stop=False)
                    ins = pe.matmul(out, k, qrys[:, parity, h, 1], start=False, stop=True)
                ins.then_inc(scores_ready, 1)

            def values(unit, head, j, parity):
                h, u = j // 4, j % 4
                pe.wait_ge(lo_done, unit + 1 + FREE[lo_done])
                if u == 0:
                    pe.wait_ge(o_free, head + FREE[o_free])
                for t in range(2):
                    st = 2 * u + t
                    for n in range(NT):
                        w = slice(t * N + n * P, t * N + (n + 1) * P)
                        pe.matmul(o_ps(n), p_hi[:, j % P_RING, w], vals[:, parity, st, h, 0:129],
                                  start=st == 0 and n % 2 == 0, stop=False, skip_group_check=True)
                        ins = pe.matmul(o_ps(n)[:, DH:129], p_lo[:, j % P_RING, w], vals_s[:, parity, st, h, 0:65],
                                        start=False, stop=st == ST - 1, skip_group_check=True)
                ins.then_inc(pv_done, 1)

            def need(pairs_before, chunks):
                pe.wait_ge(proj_free, pairs_before * 5 + chunks + FREE[proj_free])
                if chunks == 2:
                    pe.wait_ge(q_twice, (pairs_before + 1) * 16)

            with pe.Fori(0, B) as b:
                pe.wait_ge(x1_done, b * NT + NT)
                pe.wait_ge(normed, b * 2 + 1)
                for i in range(6):
                    if i == 4:
                        pe.wait_ge(normed, b * 2 + 2)
                    src, k, t0 = (ctx_in, i // 2, (i % 2) * 4) if i < 4 else (lat, i - 4, 0)
                    for t in range(4):
                        ins = pe.transpose(ps[:, i, t * P:(t + 1) * P], src[:, t0 + t, k * P:(k + 1) * P], ident[:])
                    ins.then_inc(turned, 1)
                pe.wait_ge(split_done, b * 6 + 6 + FREE[split_done])
                for c in range(5):
                    project(b * KI, 0, c, 0)
                need(b * KI, 2)
                need(b * KI, 3)
                first = b * (KI * UNITS)
                for j in range(LEAD):
                    scores(first + j, j, 0)

                def pair(b, m, parity, last):
                    before = b * KI + m
                    unit, head = before * UNITS, before * 2
                    for j in range(UNITS):
                        if j + LEAD < UNITS:
                            scores(unit + j + LEAD, j + LEAD, parity)
                        elif not last:
                            if j + LEAD == UNITS:
                                need(before + 1, 2)
                                need(before + 1, 3)
                            scores(unit + j + LEAD, j + LEAD - UNITS, 1 - parity)
                        if not last and j < 5:
                            project(before + 1, m + 1, j, 1 - parity)
                        if j == 0:
                            need(before, 5)
                        values(unit + j, head + j // 4, j, parity)
                pair_loop(pe, b, pair)

                pe.wait_ge(attn_done, b * H + H + FREE[attn_done])
                for j in range(KI):
                    for n in range(NT):
                        ins = pe.transpose(ps[:, j, n * P:(n + 1) * P], attn[:, n, j * P:(j + 1) * P], ident[:])
                    ins.then_inc(at_ready, 1)
                pe.wait_ge(at_lo, b * KI + KI)
                for n in range(NT):
                    t = slice(n * P, (n + 1) * P)
                    for j in range(KI):
                        ins = pairs3(ps[:, n, 0:D], attn_t[:, 0, j, t], attn_t[:, 1, j, t],
                                     wo_hi[:, j], wo_lo[:, j], j == 0, j == KI - 1)
                    ins.then_inc(y_ready, 1)


def experts_block(nc, A, T, out):
    with ExitStack() as ctx:
        def sb(name, shape, dt):
            return ctx.enter_context(nc.sbuf_tensor(name, shape, dt))

        def sem(name):
            return ctx.enter_context(nc.semaphore(name))

        x1, ident, vec_t, ps = T["x1"], T["ident"], T["vec_t"], T["ps"]
        stats, mean_var = sb("g_stats", [P, NT, 6], F32), sb("g_mean_var", [P, 2 * NT, 2], F32)
        var_eps, rstd = sb("g_var_eps", [P, 2 * NT], F32), sb("g_rstd", [P, 2 * NT], F32)
        minus_half, eps = sb("g_minus_half", [P, 2 * NT], F32), sb("g_eps", [P, 2 * NT], F32)
        xf, xh = sb("xf", [P, NT, D], F32), sb("xh", [P, NT, D], F32)
        xf_t = sb("xf_t", [P, KD, N], F32)
        wg = sb("wg", [P, KD, E], F32)
        alpha = sb("alpha", [P, E], F32)
        expert_no = sb("expert_no", [P, E], F32)
        logits, top = sb("logits", [P, NT, E], F32), sb("top", [P, NT, E], F32)
        top_at, top_no = sb("top_at", [P, NT, E], U32), sb("top_no", [P, NT, E], F32)
        gap, gap_exp = sb("gap", [P, NT], F32), sb("gap_exp", [P, NT], F32)
        share = sb("share", [P, 2, NT], F32)
        part = sb("part", [P, 2, NT, E], F32)
        mix_wide = sb("mix_wide", [P, NT, P], F32)
        mix_t = sb("mix_t", [P, NT, P], F32)
        b2_wide = sb("b2_wide", [P, D], F32)
        mix = sb("mix", [P, TT, E], F32)
        mix_now = sb("mix_now", [P, NT], F32)
        xt_hi, xt_lo = sb("xt_hi", [P, KD, TT * P], F16), sb("xt_lo", [P, KD, TT * P], F16)
        w1_in, w2_in = sb("w1_in", [P, KD, F], F32), sb("w2_in", [P, KF, D], F32)
        w1_hi, w1_lo = sb("w1_hi", [P, 2, KD, F], F16), sb("w1_lo", [P, 2, KD, F], F16)
        w2_hi, w2_lo = sb("w2_hi", [P, 2, KF, D], F16), sb("w2_lo", [P, 2, KF, D], F16)
        lnw_all = sb("lnw_all", [P, E * KD], F32)
        lnw_now, lnb_now = sb("lnw_now", [P, KD], F32), sb("lnb_now", [P, KD], F32)
        b1 = sb("b1", [P, 2, KF], F32)
        hid = sb("hid", [P, A_RING, N], F32)
        hid_hi, hid_lo = sb("hid_hi", [P, A_RING, N], F16), sb("hid_lo", [P, A_RING, N], F16)
        H_BANK, Y_BANK, BIAS_BANK = 0, 2, 6
        flat = "p k n -> p (k n)"

        gate_in, b2_cleared, consts, pool_chain = sem("gate_in"), sem("b2_cleared"), sem("g_consts"), sem("g_pool_chain")
        dve_chain, wait_taken, moments, rstd_done = sem("g_dve_chain"), sem("wait_taken"), sem("g_moments"), sem("g_rstd")
        normed, turned, turned_hi, turned_lo = sem("g_normed"), sem("g_turned"), sem("g_turned_hi"), sem("g_turned_lo")
        logits_ready, gap_done, gap_exp_done, mix_done = sem("logits_ready"), sem("gap_done"), sem("gap_exp_done"), sem("mix_done")
        mix_turned, mix_copied, b2_ready, b2_added = sem("mix_turned"), sem("mix_copied"), sem("b2_ready"), sem("b2_added")
        w_loaded, ln_now, w_hi_done, w_lo_done = sem("w_loaded"), sem("ln_now"), sem("e_w_hi"), sem("e_w_lo")
        bias_ready, bias_done = sem("bias_ready"), sem("bias_done")
        h_ready, gelu_done, hid_hi_done, hid_done = sem("h_ready"), sem("gelu_done"), sem("hid_hi_done"), sem("hid_done")
        hid_used, y_ready, mix_now_done, y_free, stored = (
            sem("hid_used"), sem("e_y_ready"), sem("mix_now_done"), sem("y_free"), sem("stored"))
        FREE = {hid_used: A_RING, hid_done: A_RING, gelu_done: 2, y_free: NT, b2_added: 1}
        PIECES = 4

        block = ctx.enter_context(nc.Block())

        def expert_loop(eng, expert):
            with eng.Fori(0, E // 2 - 1) as ee:
                expert(2 * ee, 0, False)
                expert(2 * ee + 1, 1, False)
            expert(E - 2, 0, False)
            expert(E - 1, 1, True)

        def block_loop(eng, one_block):
            with eng.Fori(0, BLOCKS - 1) as i:
                one_block(i, False)
            one_block(BLOCKS - 1, True)

        @block.sync
        def _(sp):
            sp.dma_start(wg[:], A["L0_ffn_Wg"].rearrange("(k p) e -> p k e", p=P)).then_inc(gate_in, 16)
            sp.wait_ge(b2_cleared, 1)
            sp.dma_start(b2_wide[0:E, :], A["L0_ffn_fc2_b"]).then_inc(gate_in, 16)
            sp.dma_start(alpha[:], A["L0_ffn_alpha"].partition_broadcast(P)).then_inc(gate_in, 16)
            w1_v = A["L0_ffn_fc1_w"].rearrange("e (k p) f -> e p k f", p=P)
            w2_v = A["L0_ffn_fc2_w"].rearrange("e (f p) d -> e p f d", p=P)
            sp.dma_start(w1_in[:], w1_v[0]).then_inc(w_loaded, 16)
            sp.dma_start(w2_in[:], w2_v[0]).then_inc(w_loaded, 16)
            with sp.Fori(0, E - 1) as e:
                sp.wait_ge(w_lo_done, (e + 1) * PIECES)
                sp.wait_ge(bias_ready, e + 1)
                sp.dma_start(w1_in[:], w1_v[bass.ds(e + 1, 1)].rearrange("o p k f -> (o p) k f")).then_inc(w_loaded, 16)
                sp.dma_start(w2_in[:], w2_v[bass.ds(e + 1, 1)].rearrange("o p f d -> (o p) f d")).then_inc(w_loaded, 16)
            for i in range(BLOCKS):
                sp.wait_ge(y_free, ((E - 1) * BLOCKS + i + 1) * NT + FREE[y_free])
                sp.dma_start(out[i].rearrange("(t p) d -> p t d", p=P), x1[:, i * NT:(i + 1) * NT, :]).then_inc(stored, 16)
            sp.wait_ge(stored, BLOCKS * 16)

        @block.gpsimd
        def _(pool):
            pool.memset(b2_wide[:], 0.0).then_inc(b2_cleared, 1)
            pool.memset(eps[:], EPS).then_inc(pool_chain, 1)
            pool.memset(minus_half[:], -0.5).then_inc(pool_chain, 1)
            pool.wait_ge(pool_chain, 2)
            with pool.Fori(0, BLOCKS) as g:
                for nth in range(2):
                    t = slice(nth * NT, (nth + 1) * NT)
                    pool.wait_ge(moments, g * 2 + nth + 1)
                    pool.tensor_tensor(var_eps[:, t], mean_var[:, t, 1], eps[:, t], ALU.add).then_inc(pool_chain, 1)
                    pool.wait_ge(pool_chain, g * 2 + nth + 3)
                    pool.tensor_tensor(rstd[:, t], var_eps[:, t], minus_half[:, t], ALU.pow).then_inc(rstd_done, 1)

        @block.scalar
        def _(act):
            act.sem_inc(gelu_done, FREE[gelu_done])
            with act.Fori(0, BLOCKS) as g:
                act.wait_ge(turned, g + 1)
                for k in range(KD):
                    act.activation(xf_t[:, k], ps[:, k], ACT.Copy)
                for k in range(KD):
                    ins = act.activation(xt_hi[:, k, bass.ds(g * N, N)], ps[:, KD + k], ACT.Copy)
                ins.then_inc(turned_hi, 1)
                act.wait_ge(gap_done, g + 1)
                act.activation(gap_exp[:], gap[:], ACT.Exp).then_inc(gap_exp_done, 1)
                act.wait_ge(mix_turned, g + 1)
                act.activation(mix_t[:].rearrange("p t n -> p (t n)"), ps[:, 5], ACT.Copy).then_inc(mix_copied, 1)

            def weights_hi(e, parity, i):
                if i == 0:
                    act.wait_ge(w_loaded, (e + 1) * 32)
                    act.wait_ge(ln_now, e + 1)
                if i < KD:
                    ins = act.activation(w1_hi[:, parity, i], w1_in[:, i], ACT.Identity, scale=lnw_now[:, i:i + 1])
                else:
                    f = slice((i - 2) * 4, (i - 1) * 4)
                    ins = act.activation(w2_hi[:, parity, f], w2_in[:, f], ACT.Copy, scale=F_SCALE)
                ins.then_inc(w_hi_done, 1)

            def gelu(e, step, f, parity):
                act.wait_ge(h_ready, step + 1)
                act.wait_ge(hid_done, step + 1)
                if f == 0:
                    act.wait_ge(bias_done, e + 1)
                act.activation(hid[:, f % A_RING], ps[:, H_BANK + f % 2], ACT.Gelu_apprx_tanh,
                               bias=b1[:, parity, f:f + 1], scale=1 / F_SCALE).then_inc(gelu_done, 1)

            for i in range(PIECES):
                weights_hi(0, 0, i)
            for f in range(G_LEAD):
                gelu(0, f, f, 0)

            def expert(e, parity, last):
                def one_block(i, last_block):
                    step = e * STEPS + i * KF
                    for f in range(KF):
                        if last_block and not last and f < PIECES:
                            if f == 0:
                                act.wait_ge(hid_used, e * STEPS + FREE[hid_used])
                            weights_hi(e + 1, 1 - parity, f)
                        if f + G_LEAD < KF or not last_block:
                            gelu(e, step + f + G_LEAD, (f + G_LEAD) % KF, parity)
                        elif not last:
                            gelu(e + 1, step + f + G_LEAD, (f + G_LEAD) % KF, 1 - parity)
                block_loop(act, one_block)
            expert_loop(act, expert)

        @block.vector
        def _(dve):
            for s in (hid_done, y_free, b2_added):
                dve.sem_inc(s, FREE[s])
            dve.memset(mix_wide[:], 0.0)
            for e in range(E):
                dve.memset(expert_no[:, e:e + 1], float(e))
            dve.tensor_scalar(lnw_all[:], vec_t[:, ROW_LNW:ROW_LNW + E * KD], F_SCALE, None, ALU.mult).then_inc(consts, 1)
            dve.wait_ge(consts, 1)
            dve.wait_ge(gate_in, 48)
            CHAIN = 12

            with dve.Fori(0, BLOCKS) as g:
                steps = [0]

                def link(ins):
                    steps[0] += 1
                    ins.then_inc(dve_chain, 1)
                    dve.wait_ge(dve_chain, g * CHAIN + steps[0])

                def tile_moments(tokens, at):
                    for t in range(NT):
                        ins = dve.bn_stats(stats[:, t, :], tokens(t))
                    link(ins)
                    dve.sem_inc(wait_taken, 1)
                    for t in range(NT):
                        ins = dve.bn_aggr(mean_var[:, at + t, :], stats[:, t, :])
                    ins.then_inc(moments, 1)

                def normalise(out, tokens, at):
                    for t in range(NT):
                        ins = dve.tensor_scalar(out[:, t, :], tokens(t), mean_var[:, at + t, 0:1],
                                                rstd[:, at + t:at + t + 1], ALU.subtract, ALU.mult)
                    return ins

                def x1_tile(t):
                    return x1[:, bass.ds(g * NT + t, 1), :].rearrange("p o d -> p (o d)")

                dve.wait_ge(b2_added, g + FREE[b2_added])
                dve.sem_inc(wait_taken, 1)
                tile_moments(x1_tile, 0)
                dve.wait_ge(rstd_done, g * 2 + 1)
                link(normalise(xf, x1_tile, 0))
                tile_moments(lambda t: xf[:, t, :], NT)
                dve.wait_ge(rstd_done, g * 2 + 2)
                normalise(xh, lambda t: xf[:, t, :], NT).then_inc(normed, 1)
                dve.wait_ge(turned_hi, g + 1)
                for k in range(KD):
                    t = bass.ds(g * N, N)
                    ins = dve.tensor_tensor(xt_lo[:, k, t], ps[:, KD + k], xt_hi[:, k, t], ALU.subtract)
                ins.then_inc(turned_lo, 1)
                dve.wait_ge(logits_ready, g + 1)
                link(dve.tensor_copy(logits[:].rearrange("p t e -> p (t e)"), ps[:, 4, 0:NT * E]))
                dve.sem_inc(wait_taken, 1)
                for t in range(NT):
                    ins = dve.max(top[:, t, :], logits[:, t, :])
                link(ins)
                dve.sem_inc(wait_taken, 1)
                for t in range(NT):
                    ins = dve.max_index(top_at[:, t, :], top[:, t, :], logits[:, t, :])
                link(ins)
                dve.tensor_copy(top_no[:], top_at[:])
                dve.tensor_tensor(gap[:], top[:, :, 1], top[:, :, 0], ALU.subtract).then_inc(gap_done, 1)
                dve.wait_ge(gap_exp_done, g + 1)
                link(dve.tensor_scalar(gap[:], gap_exp[:], 1.0, None, ALU.add))
                link(dve.reciprocal(share[:, 0], gap[:]))
                link(dve.tensor_tensor(share[:, 1], gap_exp[:], share[:, 0], ALU.mult))
                for c in range(2):
                    for t in range(NT):
                        ins = dve.tensor_scalar(part[:, c, t], expert_no[:], top_no[:, t, c:c + 1],
                                                share[:, c, t:t + 1], ALU.is_equal, ALU.mult)
                link(ins)
                link(dve.tensor_tensor(part[:, 0], part[:, 0], part[:, 1], ALU.add))
                mixed = mix_wide[:, :, 0:E]
                link(dve.tensor_tensor(mixed, part[:, 0], alpha[:].unsqueeze(1).broadcast_to([P, NT, E]), ALU.mult))
                dve.tensor_scalar(mix[:, bass.ds(g * NT, NT), :], mixed, 1 / F_SCALE, None, ALU.mult).then_inc(mix_done, 1)
                dve.wait_ge(b2_ready, g + 1)
                dve.sem_inc(wait_taken, 1)
                for t in range(NT):
                    y = ps[:, 6 + t // 2, (t % 2) * D:(t % 2 + 1) * D]
                    ins = dve.tensor_tensor(x1_tile(t), y, x1_tile(t), ALU.add)
                ins.then_inc(b2_added, 1)
                assert steps[0] == CHAIN, steps

            def ln_of(e):
                dve.tensor_copy(lnw_now[:], lnw_all[:, bass.ds(e * KD, KD)])
                dve.tensor_copy(lnb_now[:], vec_t[:, bass.ds(e * KD + ROW_LNB, KD)]).then_inc(ln_now, 1)

            def weights_lo(e, parity, i):
                dve.wait_ge(w_hi_done, e * PIECES + i + 1)
                if i < KD:
                    dve.scalar_tensor_tensor(out=w1_lo[:, parity, i], in0=w1_in[:, i], scalar=lnw_now[:, i:i + 1],
                                             in1=w1_hi[:, parity, i], op0=ALU.mult, op1=ALU.subtract).then_inc(w_lo_done, 1)
                else:
                    f = slice((i - 2) * 4, (i - 1) * 4)
                    dve.scalar_tensor_tensor(out=w2_lo[:, parity, f].rearrange(flat), in0=w2_in[:, f].rearrange(flat),
                                             scalar=F_SCALE, in1=w2_hi[:, parity, f].rearrange(flat),
                                             op0=ALU.mult, op1=ALU.subtract).then_inc(w_lo_done, 1)

            def bias(e, parity):
                dve.wait_ge(bias_ready, e + 1)
                dve.tensor_tensor(b1[:, parity], ps[:, BIAS_BANK, 0:KF], vec_t[:, bass.ds(e * KF + ROW_B1, KF)],
                                  ALU.add).then_inc(bias_done, 1)

            def split(step, f):
                dve.wait_ge(gelu_done, step + 1 + FREE[gelu_done])
                dve.wait_ge(hid_used, step + 1)
                dve.tensor_copy(hid_hi[:, f % A_RING], hid[:, f % A_RING]).then_inc(hid_hi_done, 1)
                dve.wait_ge(hid_hi_done, step + 1)
                dve.tensor_tensor(hid_lo[:, f % A_RING], hid[:, f % A_RING], hid_hi[:, f % A_RING],
                                  ALU.subtract).then_inc(hid_done, 1)

            ln_of(0)
            for i in range(PIECES):
                weights_lo(0, 0, i)
            bias(0, 0)
            for f in range(G_LEAD):
                split(f, f)

            def expert(e, parity, last):
                def one_block(i, last_block):
                    blocks, step = e * BLOCKS + i, e * STEPS + i * KF
                    dve.wait_ge(y_free, blocks * NT + FREE[y_free])
                    dve.tensor_copy(mix_now[:], mix[:, bass.ds(i * NT, NT), bass.ds(e, 1)].rearrange("p t o -> p (t o)"))\
                       .then_inc(mix_now_done, 1)
                    if last_block and not last:
                        ln_of(e + 1)
                    for f in range(KF):
                        if last_block and not last and f < PIECES:
                            weights_lo(e + 1, 1 - parity, f)
                        if last_block and not last and f == 2:
                            bias(e + 1, 1 - parity)
                        if f + G_LEAD < KF or not (last_block and last):
                            split(step + f + G_LEAD, (f + G_LEAD) % KF)
                    for n in range(NT):
                        tile = x1[:, bass.ds(i * NT + n, 1), :].rearrange("p o d -> p (o d)")
                        if n == 0:
                            dve.wait_ge(mix_now_done, blocks + 1)
                        if n < NT - 1:
                            dve.wait_ge(y_ready, blocks * (NT - 1) + n + 1)
                        else:
                            dve.wait_ge(hid_used, blocks * KF + KF + FREE[hid_used])
                        dve.scalar_tensor_tensor(out=tile, in0=ps[:, Y_BANK + n, 0:D], scalar=mix_now[:, n:n + 1],
                                                 in1=tile, op0=ALU.mult, op1=ALU.add).then_inc(y_free, 1)
                block_loop(dve, one_block)
            expert_loop(dve, expert)

        @block.tensor
        def _(pe):
            pe.sem_inc(hid_used, FREE[hid_used])
            pe.wait_ge(gate_in, 48)
            with pe.Fori(0, BLOCKS) as g:
                pe.wait_ge(normed, g + 1)
                for i in range(2 * KD):
                    src, k = (xf, i) if i < KD else (xh, i - KD)
                    for t in range(NT):
                        ins = pe.transpose(ps[:, i, t * P:(t + 1) * P], src[:, t, k * P:(k + 1) * P], ident[:])
                ins.then_inc(turned, 1)
                pe.wait_ge(turned_hi, g + 1)
                for t in range(NT):
                    for k in range(KD):
                        ins = pe.matmul(ps[:, 4, t * E:(t + 1) * E], xf_t[:, k, t * P:(t + 1) * P], wg[:, k],
                                        start=t == 0 and k == 0, stop=k == KD - 1, skip_group_check=True)
                ins.then_inc(logits_ready, 1)
                pe.wait_ge(mix_done, g + 1)
                for t in range(NT):
                    ins = pe.transpose(ps[:, 5, t * P:(t + 1) * P], mix_wide[:, t], ident[:])
                ins.then_inc(mix_turned, 1)
                pe.wait_ge(mix_copied, g + 1)
                pe.wait_ge(turned_lo, g + 1)
                for t in range(NT):
                    ins = pe.matmul(ps[:, 6 + t // 2, (t % 2) * D:(t % 2 + 1) * D], mix_t[:, t], b2_wide[:],
                                    start=t % 2 == 0, stop=True, skip_group_check=True)
                ins.then_inc(b2_ready, 1)
            pe.wait_ge(b2_added, BLOCKS + FREE[b2_added])

            def bias_sums(e):
                pe.wait_ge(ln_now, e + 1)
                pe.wait_ge(w_loaded, (e + 1) * 32)
                for f in range(KF):
                    for k in range(KD):
                        ins = pe.matmul(ps[:, BIAS_BANK, f:f + 1], w1_in[:, k, f * P:(f + 1) * P], lnb_now[:, k:k + 1],
                                        start=f == 0 and k == 0, stop=k == KD - 1, skip_group_check=True)
                ins.then_inc(bias_ready, 1)

            def fc1(step, f, parity, tokens):
                pe.wait_ge(gelu_done, step + 1)
                out, w = ps[:, H_BANK + f % 2], slice(f * P, (f + 1) * P)
                for k in range(KD):
                    x_hi, x_lo = xt_hi[:, k, tokens], xt_lo[:, k, tokens]
                    pe.matmul(out, w1_hi[:, parity, k, w], x_hi, start=k == 0, stop=False)
                    pe.matmul(out, w1_hi[:, parity, k, w], x_lo, start=False, stop=False)
                    ins = pe.matmul(out, w1_lo[:, parity, k, w], x_hi, start=False, stop=k == KD - 1)
                ins.then_inc(h_ready, 1)

            def fc2(step, blocks, f, parity):
                pe.wait_ge(hid_done, step + 1 + FREE[hid_done])
                for n in range(NT):
                    if f == 0:
                        pe.wait_ge(y_free, blocks * NT + n + 1)
                    out, t = ps[:, Y_BANK + n, 0:D], slice(n * P, (n + 1) * P)
                    a_hi, a_lo = hid_hi[:, f % A_RING, t], hid_lo[:, f % A_RING, t]
                    pe.matmul(out, a_hi, w2_hi[:, parity, f], start=f == 0, stop=False)
                    pe.matmul(out, a_hi, w2_lo[:, parity, f], start=False, stop=False)
                    ins = pe.matmul(out, a_lo, w2_hi[:, parity, f], start=False, stop=f == KF - 1)
                    if f == KF - 1 and n < NT - 1:
                        ins.then_inc(y_ready, 1)
                ins.then_inc(hid_used, 1)

            bias_sums(0)
            pe.wait_ge(w_lo_done, PIECES)
            for f in range(G_LEAD):
                fc1(f, f, 0, slice(0, N))

            def expert(e, parity, last):
                def one_block(i, last_block):
                    blocks, step = e * BLOCKS + i, e * STEPS + i * KF
                    if last_block and not last:
                        bias_sums(e + 1)
                    for f in range(KF):
                        if f + G_LEAD < KF:
                            fc1(step + f + G_LEAD, f + G_LEAD, parity, bass.ds(i * N, N))
                        elif not last_block:
                            fc1(step + f + G_LEAD, f + G_LEAD - KF, parity, bass.ds(i * N + N, N))
                        elif not last:
                            if f + G_LEAD == KF:
                                pe.wait_ge(w_lo_done, (e + 2) * PIECES)
                            fc1(step + f + G_LEAD, f + G_LEAD - KF, 1 - parity, slice(0, N))
                        fc2(step + f, blocks, f, parity)
                block_loop(pe, one_block)
            expert_loop(pe, expert)


def program(nc, A, out):
    with ExitStack() as ctx:
        T = {
            "x1": ctx.enter_context(nc.sbuf_tensor("x1", [P, TT, D], F32)),
            "ident": ctx.enter_context(nc.sbuf_tensor("ident", [P, P], F32)),
            "vec_t": ctx.enter_context(nc.sbuf_tensor("vec_t", [P, P], F32)),
            "ps": ctx.enter_context(nc.psum_tensor("ps", [P, 8, 512], F32)),
        }
        attention_block(nc, A, T)
        experts_block(nc, A, T, out)


INPUTS = ["x", "ctx_1024", "L0_xattn_ln_l_w", "L0_xattn_ln_l_b", "L0_xattn_ln_c_w", "L0_xattn_ln_c_b",
          "L0_xattn_Wq", "L0_xattn_Wkv", "L0_xattn_Wo", "L0_xattn_bo", "L0_ffn_Wg", "L0_ffn_alpha",
          "L0_ffn_ln_w", "L0_ffn_ln_b", "L0_ffn_fc1_w", "L0_ffn_fc1_b", "L0_ffn_fc2_w", "L0_ffn_fc2_b"]


def kernel(**inputs):
    import numpy as np
    import concourse.bacc as bacc
    from concourse.bass_utils import run_bass_kernel_spmd

    nc = bacc.Bacc("TRN2", target_bir_lowering=False, num_devices=1)
    arrays, aps = {}, {}
    for name in INPUTS:
        a = np.ascontiguousarray(inputs[name])
        arrays[f"in_{name}"] = a
        aps[name] = nc.dram_tensor(f"in_{name}", a.shape, mybir.dt.from_np(a.dtype), kind="ExternalInput").ap()
    out = nc.dram_tensor("out", (B, N, D), F32, kind="ExternalOutput").ap()
    program(nc, aps, out)
    r = run_bass_kernel_spmd(nc, [arrays], core_ids=[0])
    return r.results[0]["out"]
```

```python
from contextlib import ExitStack
import math

import concourse.bass as bass
from concourse import mybir

F32 = mybir.dt.float32
F16 = mybir.dt.float16
U32 = mybir.dt.uint32
I32 = mybir.dt.int32
AX = mybir.AxisListType
ALU = mybir.AluOpType
ACT = mybir.ActivationFunctionType

P = 128
B = 4
N = 512
S = 1024
D = 256
KD = D // P
H = 16
DH = 64
INNER = H * DH
KI = INNER // P
NT = N // P
ST = S // P
EPS = 1e-5
CLIP = 11.0
W_SCALE = 16.0
LO_SCALE = 2048.0
VW = 130
UNITS = 8
LEAD = 3
E_RING = 4
P_RING = 4
TT = B * NT

E = 8
F = 1024
KF = F // P
F_SCALE = 64.0
BLOCKS = TT // NT
PIECES = 4
TILES = 2 * TT + E - 1


def w1_at(e, k, f, part=0):
    return ((e * 2 + part) * KD + k) * F + f * P


def w2_at(e, f):
    return (e * KF + f) * 2 * D


ROW_B1, ROW_LNW, ROW_LNB, ROW_LW, ROW_LB, ROW_CW, ROW_CB = 0, 64, 80, 96, 98, 100, 102


def attention_block(nc, A, T):
    with ExitStack() as ctx:
        def sb(name, shape, dt):
            return ctx.enter_context(nc.sbuf_tensor(name, shape, dt))

        def sem(name):
            return ctx.enter_context(nc.semaphore(name))

        x1, ident, vec_t = T["x1"], T["ident"], T["vec_t"]
        wq_hi, wq_lo = sb("wq_hi", [P, KD, INNER], F16), sb("wq_lo", [P, KD, INNER], F16)
        wkv_hi, wkv_lo = sb("wkv_hi", [P, KD, 2 * INNER], F16), sb("wkv_lo", [P, KD, 2 * INNER], F16)
        wo_hi, wo_lo = sb("wo_hi", [P, KI, D], F16), sb("wo_lo", [P, KI, D], F16)
        stage = T["space"][:, 0:8192]
        vec_rows = sb("vec_rows", [P, P], F32)
        bo_all, zeros = sb("bo_all", [P, D], F32), sb("zeros", [P, D], F32)
        ctx_in = sb("ctx_in", [P, ST, D], F32)
        x_in = sb("x_in", [P, NT, D], F32)
        lat = sb("lat", [P, NT, D], F32)
        stats = sb("stats", [P, ST, 6], F32)
        mean_var = sb("mean_var", [P, 16, 2], F32)
        var_eps = sb("var_eps", [P, 16], F32)
        rstd = sb("rstd", [P, 16], F32)
        minus_half = sb("minus_half", [P, 16], F32)
        eps = sb("eps", [P, 16], F32)
        ln_lo_scale = sb("ln_lo_scale", [P, 1], F32)
        warm = sb("warm", [P, 1], F32)
        affine = sb("affine", [P, 2, N], F32)
        ctx_hi, ctx_lo = sb("ctx_hi", [P, KD, S], F16), sb("ctx_lo", [P, KD, S], F16)
        lat_hi, lat_lo = sb("lat_hi", [P, KD, N], F16), sb("lat_lo", [P, KD, N], F16)
        keys = sb("keys", [P, 2, 2, S], F16)
        qrys = sb("qrys", [P, 2, 2, 2, N], F16)
        vals = sb("vals", [P, 2, ST, 2, VW], F16)
        vals_s = sb("vals_s", [P, 2, ST, 2, 66], F16)
        expo = T["space"][:, 8192:12288].rearrange("p (r n) -> p r n", r=E_RING)
        p_hi, p_lo = (T["space"][:, 12288 + i * 2048:14336 + i * 2048].bitcast(F16)
                      .rearrange("p (r n) -> p r n", r=P_RING) for i in range(2))
        o_lo = sb("o_lo", [P, NT, DH], F32)
        o_sum = sb("o_sum", [P, 2, NT, DH], F32)
        o_rec = sb("o_rec", [P, 2, NT], F32)
        attn = stage[:, 0:NT * INNER].rearrange("p (n i) -> p n i", n=NT)
        attn_t = stage[:, NT * INNER:].bitcast(F16).rearrange("p (c j n) -> p c j n", c=2, j=KI)
        wkv_in = stage[:, 0:KD * 2 * INNER].rearrange("p (k n) -> p k n", k=KD)
        wq_in = stage[:, 4096:6144].rearrange("p (k n) -> p k n", k=KD)
        wo_in = stage[:, 6144:8192].rearrange("p (k n) -> p k n", k=KI)

        ps = T["ps"]
        S_BANK, O_BANK, J_BANK = 0, 4, 6

        def o_ps(n):
            return ps[:, O_BANK + n // 2, (n % 2) * 256:(n % 2) * 256 + 129]

        o_all = ps[:, O_BANK:O_BANK + 2, :].rearrange("p b (h c) -> p (b h) c", h=2)

        w_in, ctx_loaded, x_loaded = sem("w_in"), sem("ctx_loaded"), sem("x_loaded")
        vec_in, consts, vec_turned, vec_done = sem("vec_in"), sem("consts"), sem("vec_turned"), sem("vec_done")
        rows_cleared = sem("rows_cleared")
        wait_taken, bo_in = sem("wait_taken"), sem("bo_in")
        ident_done, pool_chain, dve_chain = sem("ident_done"), sem("pool_chain"), sem("dve_chain")
        w_hi_done, w_lo_done = sem("w_hi_done"), sem("w_lo_done")
        moments, rstd_done, residual_done = sem("moments"), sem("rstd_done"), sem("residual_done")
        normed, turned, affine_done, split_done = sem("normed"), sem("turned"), sem("affine_done"), sem("split_done")
        proj_ready, proj_hi, proj_free, q_twice = sem("proj_ready"), sem("proj_hi"), sem("proj_free"), sem("q_twice")
        scores_ready, exp_done, clip_done, hi_done, lo_done = (
            sem("scores_ready"), sem("exp_done"), sem("clip_done"), sem("hi_done"), sem("lo_done"))
        pv_done, o_lo_done, o_free, o_step, attn_done = (
            sem("pv_done"), sem("o_lo_done"), sem("o_free"), sem("o_step"), sem("attn_done"))
        at_ready, at_hi, at_lo, y_ready, x1_done = (
            sem("at_ready"), sem("at_hi"), sem("at_lo"), sem("y_ready"), sem("x1_done"))
        FREE = {exp_done: 2, lo_done: E_RING, pv_done: P_RING, o_free: 1, attn_done: 2, proj_free: 1,
                split_done: 2, x1_done: NT}

        block = ctx.enter_context(nc.Block())

        def pair_loop(eng, b, pair):
            with eng.Fori(0, KI // 2 - 1) as mm:
                pair(b, 2 * mm, 0, False)
                pair(b, 2 * mm + 1, 1, False)
            pair(b, KI - 2, 0, False)
            pair(b, KI - 1, 1, True)

        @block.sync
        def _(sp):
            ctx_v = A["ctx_1024"].rearrange("b (t p) d -> b p t d", p=P)
            x_v = A["x"].rearrange("b (t p) d -> b p t d", p=P)
            sp.dma_start(ctx_in[:], ctx_v[0]).then_inc(ctx_loaded, 16)
            sp.dma_start(x_in[:], x_v[0]).then_inc(x_loaded, 16)
            sp.dma_start(wkv_in, A["L0_xattn_Wkv"].rearrange("(k p) n -> p k n", p=P)).then_inc(w_in, 16)
            sp.dma_start(wq_in, A["L0_xattn_Wq"].rearrange("(k p) n -> p k n", p=P)).then_inc(w_in, 16)
            sp.dma_start(wo_in, A["L0_xattn_Wo"].rearrange("(k p) n -> p k n", p=P)).then_inc(w_in, 16)

            def q_to_upper(pairs_before, parity):
                sp.wait_ge(proj_free, pairs_before * 5 + 1 + FREE[proj_free])
                sp.dma_start(qrys[DH:P, parity], qrys[0:DH, parity]).then_inc(q_twice, 16)

            def batch(b, load_next):
                q_to_upper(b * KI, 0)
                if load_next:
                    sp.wait_ge(turned, (b + 1) * 6)
                    sp.dma_start(ctx_in[:], ctx_v[bass.ds(b + 1, 1)].rearrange("o p t d -> (o p) t d")).then_inc(ctx_loaded, 16)
                    sp.wait_ge(residual_done, b + 1)
                    sp.dma_start(x_in[:], x_v[bass.ds(b + 1, 1)].rearrange("o p t d -> (o p) t d")).then_inc(x_loaded, 16)

                def pair(b, m, parity, last):
                    if not last:
                        q_to_upper(b * KI + m + 1, 1 - parity)
                pair_loop(sp, b, pair)

            with sp.Fori(0, B - 1) as b:
                batch(b, True)
            batch(B - 1, False)

        @block.gpsimd
        def _(pool):
            chain = [0]

            def link(ins):
                chain[0] += 1
                ins.then_inc(pool_chain, 1)
                pool.wait_ge(pool_chain, chain[0])

            pool.sem_inc(attn_done, FREE[attn_done])
            link(pool.memset(ident[:], 0.0))
            pool.affine_select(out=ident[:], in_=ident[:], compare_op=ALU.not_equal, fill=1.0, base=0,
                               pattern=[[-1, P]], channel_multiplier=1).then_inc(ident_done, 1)
            link(pool.memset(minus_half[:], -0.5))
            link(pool.memset(eps[:], EPS))
            pool.dma_start(bo_all[:], A["L0_xattn_bo"].partition_broadcast(P)).then_inc(bo_in, 16)
            PER_BATCH = 3

            def root(b, nth, a, z):
                pool.wait_ge(moments, b * 3 + nth + 1)
                pool.tensor_tensor(var_eps[:, a:z], mean_var[:, a:z, 1], eps[:, a:z], ALU.add).then_inc(pool_chain, 1)
                pool.wait_ge(pool_chain, b * PER_BATCH + nth + 1 + chain[0])
                pool.tensor_tensor(rstd[:, a:z], var_eps[:, a:z], minus_half[:, a:z], ALU.pow).then_inc(rstd_done, 1)

            with pool.Fori(0, B) as b:
                root(b, 0, 0, 8)
                root(b, 1, 8, 12)
                root(b, 2, 12, 16)
                pool.wait_ge(x_loaded, b * 16 + 16)
                pool.wait_ge(bo_in, 16)
                pool.tensor_tensor(x1[:, bass.ds(b * NT, NT), :], x_in[:],
                                   bo_all[:].unsqueeze(1).broadcast_to([P, NT, D]), ALU.add).then_inc(residual_done, 1)

                def pair(b, m, parity, last):
                    for h in range(2):
                        pool.wait_ge(o_free, b * H + m * 2 + h + 1 + FREE[o_free])
                        pool.tensor_tensor(attn[:, :, bass.ds(m * P + h * DH, DH)], o_sum[:, h],
                                           o_rec[:, h].unsqueeze(2).broadcast_to([P, NT, DH]),
                                           ALU.mult).then_inc(attn_done, 1)
                pair_loop(pool, b, pair)

        @block.scalar
        def _(act):
            act.sem_inc(exp_done, FREE[exp_done])
            for view, row in ((A["L0_ffn_fc1_b"].rearrange("e (f p) -> (e f) p", p=P), ROW_B1),
                              (A["L0_ffn_ln_w"].rearrange("e (k p) -> (e k) p", p=P), ROW_LNW),
                              (A["L0_ffn_ln_b"].rearrange("e (k p) -> (e k) p", p=P), ROW_LNB),
                              (A["L0_xattn_ln_l_w"].rearrange("(k p) -> k p", p=P), ROW_LW),
                              (A["L0_xattn_ln_l_b"].rearrange("(k p) -> k p", p=P), ROW_LB),
                              (A["L0_xattn_ln_c_w"].rearrange("(k p) -> k p", p=P), ROW_CW),
                              (A["L0_xattn_ln_c_b"].rearrange("(k p) -> k p", p=P), ROW_CB)):
                if row == ROW_B1:
                    act.wait_ge(consts, 1)
                act.dma_start(vec_rows[row:row + view.shape[0], :], view).then_inc(vec_in, 16)
            act.wait_ge(consts, 3)
            act.dma_start(T["rows"].rearrange("(t p) d -> p t d", p=P),
                          zeros[:].unsqueeze(1).broadcast_to([P, TILES, D])).then_inc(rows_cleared, 16)
            act.activation(warm[:], ln_lo_scale[:], ACT.Exp)
            act.wait_ge(w_in, 48)
            for k in range(KD):
                act.activation(wkv_hi[:, k], wkv_in[:, k], ACT.Copy, scale=W_SCALE).then_inc(w_hi_done, 1)
            act.activation(wq_hi[:], wq_in, ACT.Copy, scale=W_SCALE).then_inc(w_hi_done, 1)
            act.activation(wo_hi[:], wo_in, ACT.Copy, scale=W_SCALE).then_inc(w_hi_done, 1)

            def proj_hi_part(pairs_before, c, parity):
                act.wait_ge(proj_ready, pairs_before * 5 + c + 1)
                if c == 0:
                    act.activation(qrys[0:DH, parity, 0, 0], ps[0:DH, J_BANK], ACT.Copy, scale=1 / W_SCALE)
                    act.activation(qrys[0:DH, parity, 1, 0], ps[DH:P, J_BANK], ACT.Copy,
                                   scale=1 / W_SCALE).then_inc(proj_hi, 1)
                elif c < 3:
                    bank, t = J_BANK + c % 2, slice((c - 1) * 512, c * 512)
                    act.activation(keys[0:DH, parity, 0, t], ps[0:DH, bank], ACT.Copy, scale=1 / W_SCALE)
                    act.activation(keys[DH:P, parity, 1, t], ps[DH:P, bank], ACT.Copy,
                                   scale=1 / W_SCALE).then_inc(proj_hi, 1)
                else:
                    bank, t = J_BANK + c % 2, slice((c - 3) * 4, (c - 2) * 4)
                    act.activation(vals[:, parity, t, :, DH:2 * DH].rearrange("p t h d -> p (t h) d"),
                                   ps[:, bank, :].rearrange("p (t d) -> p t d", d=DH),
                                   ACT.Copy, scale=1 / W_SCALE).then_inc(proj_hi, 1)

            def exp(unit, j):
                act.wait_ge(scores_ready, unit + 1)
                act.wait_ge(lo_done, unit + 1)
                act.activation(expo[:, j % E_RING],
                               ps[:, S_BANK + 2 * (j % 2):S_BANK + 2 * (j % 2) + 2, :].rearrange("p a b -> p (a b)"),
                               ACT.Exp, scale=DH ** -0.5, bias=ln_lo_scale[:, 0:1]).then_inc(exp_done, 1)

            def hi(unit, j):
                act.wait_ge(clip_done, unit + 1)
                act.wait_ge(pv_done, unit + 1)
                act.activation(p_hi[:, j % P_RING], expo[:, j % E_RING], ACT.Copy,
                               scale=1 / LO_SCALE).then_inc(hi_done, 1)

            def out_lo(head):
                act.wait_ge(pv_done, head * 4 + 4 + FREE[pv_done])
                act.wait_ge(o_free, head + FREE[o_free])
                act.activation(o_lo[:], o_all[:, :, 0:DH], ACT.Copy).then_inc(o_lo_done, 1)

            with act.Fori(0, B) as b:
                for i in range(6):
                    row_w, row_b, k = (ROW_CW, ROW_CB, i // 2) if i < 4 else (ROW_LW, ROW_LB, i - 4)
                    act.wait_ge(turned, b * 6 + i + 1)
                    if i == 0:
                        act.wait_ge(vec_done, 1)
                    act.wait_ge(split_done, b * 6 + i + 1)
                    act.activation(affine[:, i % 2], ps[:, i], ACT.Identity, bias=vec_t[:, row_b + k:row_b + k + 1],
                                   scale=vec_t[:, row_w + k:row_w + k + 1]).then_inc(affine_done, 1)
                for c in range(5):
                    proj_hi_part(b * KI, c, 0)
                first = b * (KI * UNITS)
                exp(first, 0)
                exp(first + 1, 1)
                hi(first, 0)
                exp(first + 2, 2)
                hi(first + 1, 1)

                def pair(b, m, parity, last):
                    unit, head = (b * KI + m) * UNITS, (b * KI + m) * 2
                    for j in range(UNITS):
                        if j == UNITS // 2:
                            out_lo(head)
                        if not last or j + LEAD < UNITS:
                            exp(unit + j + LEAD, j + LEAD)
                        if not last or j + LEAD - 1 < UNITS:
                            hi(unit + j + LEAD - 1, j + LEAD - 1)
                        if not last and j < 5:
                            proj_hi_part(b * KI + m + 1, j, 1 - parity)
                    out_lo(head + 1)
                pair_loop(act, b, pair)
                for j in range(KI):
                    act.wait_ge(at_ready, b * KI + j + 1)
                    act.activation(attn_t[:, 0, j], ps[:, j], ACT.Copy).then_inc(at_hi, 1)
            act.wait_ge(rows_cleared, 16)

        @block.vector
        def _(dve):
            for s in (lo_done, o_free, proj_free, split_done, x1_done):
                dve.sem_inc(s, FREE[s])
            dve.memset(vec_rows[:], 0.0).then_inc(consts, 1)
            dve.memset(ln_lo_scale[:], math.log(LO_SCALE)).then_inc(consts, 1)
            dve.memset(zeros[:], 0.0).then_inc(consts, 1)
            dve.memset(vals[:, :, :, :, 2 * DH:VW].rearrange("p a t h d -> p (a t h) d"), 1.0)
            dve.memset(vals_s[:, :, :, :, DH:DH + 2].rearrange("p a t h d -> p (a t h) d"), 1 / LO_SCALE)

            def lo_of(out, full, hi, scale):
                return dve.scalar_tensor_tensor(out=out, in0=full, scalar=scale, in1=hi, op0=ALU.mult, op1=ALU.subtract)

            dve.wait_ge(vec_turned, 1)
            dve.tensor_copy(vec_t[:], ps[:, 7, 0:P]).then_inc(vec_done, 1)
            for k in range(KD):
                dve.wait_ge(w_hi_done, k + 1)
                lo_of(wkv_lo[:, k], wkv_in[:, k], wkv_hi[:, k], W_SCALE).then_inc(w_lo_done, 1)
            dve.wait_ge(w_hi_done, KD + 1)
            lo_of(wq_lo[:], wq_in, wq_hi[:], W_SCALE).then_inc(w_lo_done, 1)
            dve.wait_ge(w_hi_done, KD + 2)
            lo_of(wo_lo[:], wo_in, wo_hi[:], W_SCALE).then_inc(w_lo_done, 1)

            def proj_lo_part(pairs_before, c, parity):
                dve.wait_ge(proj_hi, pairs_before * 5 + c + 1)
                if c == 0:
                    lo_of(qrys[0:DH, parity, 0, 1], ps[0:DH, J_BANK], qrys[0:DH, parity, 0, 0], 1 / W_SCALE)
                    lo_of(qrys[0:DH, parity, 1, 1], ps[DH:P, J_BANK], qrys[0:DH, parity, 1, 0],
                          1 / W_SCALE).then_inc(proj_free, 1)
                elif c < 3:
                    bank, t = J_BANK + c % 2, slice((c - 1) * 512, c * 512)
                    lo_of(keys[DH:P, parity, 0, t], ps[0:DH, bank], keys[0:DH, parity, 0, t], 1 / W_SCALE)
                    lo_of(keys[0:DH, parity, 1, t], ps[DH:P, bank], keys[DH:P, parity, 1, t],
                          1 / W_SCALE).then_inc(proj_free, 1)
                else:
                    bank, t = J_BANK + c % 2, slice((c - 3) * 4, (c - 2) * 4)
                    v = vals[:, parity, t].rearrange("p t h d -> p (t h) d")
                    dve.tensor_scalar(vals_s[:, parity, t, :, 0:DH].rearrange("p t h d -> p (t h) d"),
                                      v[:, :, DH:2 * DH], 1 / LO_SCALE, None, ALU.mult)
                    lo_of(v[:, :, 0:DH], ps[:, bank, :].rearrange("p (t d) -> p t d", d=DH),
                          v[:, :, DH:2 * DH], 1 / W_SCALE).then_inc(proj_free, 1)

            def clip(unit, j):
                dve.wait_ge(exp_done, unit + 1 + FREE[exp_done])
                e = expo[:, j % E_RING]
                dve.tensor_scalar(e, e, LO_SCALE * math.exp(CLIP), LO_SCALE * math.exp(-CLIP),
                                  ALU.min, ALU.max).then_inc(clip_done, 1)

            def lo(unit, j):
                dve.wait_ge(hi_done, unit + 1)
                dve.scalar_tensor_tensor(out=p_lo[:, j % P_RING], in0=p_hi[:, j % P_RING], scalar=-LO_SCALE,
                                         in1=expo[:, j % E_RING], op0=ALU.mult, op1=ALU.add).then_inc(lo_done, 1)

            def out_sum(head, h):
                dve.wait_ge(o_lo_done, head + 1)
                dve.wait_ge(attn_done, head + 1)
                dve.reciprocal(o_rec[:, h], o_all[:, :, 2 * DH])
                dve.tensor_tensor(o_sum[:, h], o_all[:, :, DH:2 * DH], o_lo[:], ALU.add).then_inc(o_free, 1)

            CHAIN = 4

            with dve.Fori(0, B) as b:
                steps = [0]

                def link(ins):
                    steps[0] += 1
                    ins.then_inc(dve_chain, 1)
                    dve.wait_ge(dve_chain, b * CHAIN + steps[0])

                def tile_moments(tokens, tiles, at):
                    for t in range(tiles):
                        ins = dve.bn_stats(stats[:, t, :], tokens[:, t, :])
                    link(ins)
                    dve.sem_inc(wait_taken, 1)
                    for t in range(tiles):
                        ins = dve.bn_aggr(mean_var[:, at + t, :], stats[:, t, :])
                    return ins

                def normalise(out, tokens, tiles, at):
                    for t in range(tiles):
                        ins = dve.tensor_scalar(out[:, t, :], tokens[:, t, :], mean_var[:, at + t, 0:1],
                                                rstd[:, at + t:at + t + 1], ALU.subtract, ALU.mult)
                    return ins

                dve.wait_ge(ctx_loaded, b * 16 + 16)
                tile_moments(ctx_in, ST, 0).then_inc(moments, 1)
                dve.wait_ge(x_loaded, b * 16 + 16)
                dve.wait_ge(moments, b * 3 + 1)
                tile_moments(x_in, NT, 8).then_inc(moments, 1)
                dve.wait_ge(rstd_done, b * 3 + 1)
                normalise(ctx_in, ctx_in, ST, 0).then_inc(normed, 1)
                dve.wait_ge(rstd_done, b * 3 + 2)
                link(normalise(lat, x_in, NT, 8))
                tile_moments(lat, NT, 12).then_inc(moments, 1)
                dve.wait_ge(rstd_done, b * 3 + 3)
                normalise(lat, lat, NT, 12).then_inc(normed, 1)
                for i in range(6):
                    hi_, lo_, k = (ctx_hi, ctx_lo, i // 2) if i < 4 else (lat_hi, lat_lo, i - 4)
                    t = slice((i % 2) * N, (i % 2) * N + N) if i < 4 else slice(0, N)
                    dve.wait_ge(affine_done, b * 6 + i + 1)
                    dve.tensor_copy(hi_[:, k, t], affine[:, i % 2]).then_inc(o_step, 1)
                    dve.wait_ge(o_step, b * 6 + i + 1)
                    dve.tensor_tensor(lo_[:, k, t], affine[:, i % 2], hi_[:, k, t], ALU.subtract).then_inc(split_done, 1)
                for c in range(5):
                    proj_lo_part(b * KI, c, 0)
                first = b * (KI * UNITS)
                clip(first, 0)
                clip(first + 1, 1)
                lo(first, 0)
                clip(first + 2, 2)
                lo(first + 1, 1)

                def pair(b, m, parity, last):
                    unit, head = (b * KI + m) * UNITS, (b * KI + m) * 2
                    for j in range(UNITS):
                        if j == UNITS // 2:
                            out_sum(head, 0)
                        if not last or j + LEAD < UNITS:
                            clip(unit + j + LEAD, j + LEAD)
                        if not last or j + LEAD - 1 < UNITS:
                            lo(unit + j + LEAD - 1, j + LEAD - 1)
                        if not last and j < 5:
                            proj_lo_part(b * KI + m + 1, j, 1 - parity)
                    out_sum(head + 1, 1)
                pair_loop(dve, b, pair)
                for j in range(KI):
                    dve.wait_ge(at_hi, b * KI + j + 1)
                    dve.tensor_tensor(attn_t[:, 1, j], ps[:, j], attn_t[:, 0, j], ALU.subtract).then_inc(at_lo, 1)
                for n in range(NT):
                    dve.wait_ge(y_ready, b * NT + n + 1)
                    tile = x1[:, bass.ds(b * NT + n, 1), :].rearrange("p o d -> p (o d)")
                    if n == 0:
                        dve.wait_ge(residual_done, b + 1)
                    dve.scalar_tensor_tensor(out=tile, in0=ps[:, n, 0:D], scalar=1 / W_SCALE, in1=tile,
                                             op0=ALU.mult, op1=ALU.add).then_inc(x1_done, 1)

        @block.tensor
        def _(pe):
            pe.sem_inc(pv_done, FREE[pv_done])
            pe.wait_ge(ident_done, 1)
            pe.wait_ge(vec_in, 16 * 7)
            pe.transpose(ps[:, 7, 0:P], vec_rows[:], ident[:]).then_inc(vec_turned, 1)
            pe.wait_ge(w_lo_done, KD + 2)

            def pairs3(out, w_hi, w_lo, x_hi, x_lo, first, last):
                pe.matmul(out, w_hi, x_hi, start=first, stop=False, skip_group_check=True)
                pe.matmul(out, w_hi, x_lo, start=False, stop=False, skip_group_check=True)
                return pe.matmul(out, w_lo, x_hi, start=False, stop=last, skip_group_check=True)

            def project(pairs_before, m, c, parity):
                pe.wait_ge(proj_free, pairs_before * 5 + c + (FREE[proj_free] if c == 0 else 0))
                out = ps[:, J_BANK + c % 2, :]
                if c < 3:
                    w_hi, w_lo = (wq_hi, wq_lo) if c == 0 else (wkv_hi, wkv_lo)
                    x_hi, x_lo = (lat_hi, lat_lo) if c == 0 else (ctx_hi, ctx_lo)
                    t = slice(0, N) if c == 0 else slice((c - 1) * 512, c * 512)
                    for k in range(KD):
                        w = bass.ds(m * P, P)
                        ins = pairs3(out, w_hi[:, k, w], w_lo[:, k, w], x_hi[:, k, t], x_lo[:, k, t],
                                     k == 0, k == KD - 1)
                else:
                    for t4 in range(4):
                        t = slice(((c - 3) * 4 + t4) * P, ((c - 3) * 4 + t4 + 1) * P)
                        for k in range(KD):
                            w = bass.ds(m * P + INNER, P)
                            ins = pairs3(out[:, t4 * P:(t4 + 1) * P], ctx_hi[:, k, t], ctx_lo[:, k, t],
                                         wkv_hi[:, k, w], wkv_lo[:, k, w], k == 0 and t4 == 0, k == KD - 1)
                ins.then_inc(proj_ready, 1)

            def scores(unit, j, parity):
                h, u = j // 4, j % 4
                pe.wait_ge(exp_done, unit + 1)
                for t in range(2):
                    k = keys[:, parity, h, (2 * u + t) * P:(2 * u + t + 1) * P]
                    out = ps[:, S_BANK + 2 * (j % 2) + t, :]
                    pe.matmul(out, k, qrys[:, parity, h, 0], start=True, stop=False)
                    ins = pe.matmul(out, k, qrys[:, parity, h, 1], start=False, stop=True)
                ins.then_inc(scores_ready, 1)

            def values(unit, head, j, parity):
                h, u = j // 4, j % 4
                pe.wait_ge(lo_done, unit + 1 + FREE[lo_done])
                if u == 0:
                    pe.wait_ge(o_free, head + FREE[o_free])
                for t in range(2):
                    st = 2 * u + t
                    for n in range(NT):
                        w = slice(t * N + n * P, t * N + (n + 1) * P)
                        pe.matmul(o_ps(n), p_hi[:, j % P_RING, w], vals[:, parity, st, h, 0:129],
                                  start=st == 0 and n % 2 == 0, stop=False, skip_group_check=True)
                        ins = pe.matmul(o_ps(n)[:, DH:129], p_lo[:, j % P_RING, w], vals_s[:, parity, st, h, 0:65],
                                        start=False, stop=st == ST - 1, skip_group_check=True)
                ins.then_inc(pv_done, 1)

            def need(pairs_before, chunks):
                pe.wait_ge(proj_free, pairs_before * 5 + chunks + FREE[proj_free])
                if chunks == 2:
                    pe.wait_ge(q_twice, (pairs_before + 1) * 16)

            with pe.Fori(0, B) as b:
                pe.wait_ge(x1_done, b * NT + NT)
                pe.wait_ge(normed, b * 2 + 1)
                for i in range(6):
                    if i == 4:
                        pe.wait_ge(normed, b * 2 + 2)
                    src, k, t0 = (ctx_in, i // 2, (i % 2) * 4) if i < 4 else (lat, i - 4, 0)
                    for t in range(4):
                        ins = pe.transpose(ps[:, i, t * P:(t + 1) * P], src[:, t0 + t, k * P:(k + 1) * P], ident[:])
                    ins.then_inc(turned, 1)
                pe.wait_ge(split_done, b * 6 + 6 + FREE[split_done])
                for c in range(5):
                    project(b * KI, 0, c, 0)
                need(b * KI, 2)
                need(b * KI, 3)
                first = b * (KI * UNITS)
                for j in range(LEAD):
                    scores(first + j, j, 0)

                def pair(b, m, parity, last):
                    before = b * KI + m
                    unit, head = before * UNITS, before * 2
                    for j in range(UNITS):
                        if j + LEAD < UNITS:
                            scores(unit + j + LEAD, j + LEAD, parity)
                        elif not last:
                            if j + LEAD == UNITS:
                                need(before + 1, 2)
                                need(before + 1, 3)
                            scores(unit + j + LEAD, j + LEAD - UNITS, 1 - parity)
                        if not last and j < 5:
                            project(before + 1, m + 1, j, 1 - parity)
                        if j == 0:
                            need(before, 5)
                        values(unit + j, head + j // 4, j, parity)
                pair_loop(pe, b, pair)

                pe.wait_ge(attn_done, b * H + H + FREE[attn_done])
                for j in range(KI):
                    for n in range(NT):
                        ins = pe.transpose(ps[:, j, n * P:(n + 1) * P], attn[:, n, j * P:(j + 1) * P], ident[:])
                    ins.then_inc(at_ready, 1)
                pe.wait_ge(at_lo, b * KI + KI)
                for n in range(NT):
                    t = slice(n * P, (n + 1) * P)
                    for j in range(KI):
                        ins = pairs3(ps[:, n, 0:D], attn_t[:, 0, j, t], attn_t[:, 1, j, t],
                                     wo_hi[:, j], wo_lo[:, j], j == 0, j == KI - 1)
                    ins.then_inc(y_ready, 1)


def experts_block(nc, A, T, out):
    rows = T["rows"]
    ys = nc.dram_tensor("outputs_by_expert", (TILES * P, D), F32, kind="Internal").ap()
    with ExitStack() as ctx:
        def sb(name, shape, dt):
            return ctx.enter_context(nc.sbuf_tensor(name, shape, dt))

        def sem(name):
            return ctx.enter_context(nc.semaphore(name))

        x1, ident, vec_t, ps = T["x1"], T["ident"], T["vec_t"], T["ps"]
        w_in = sb("w_in", [P, PIECES, 1024], F32)
        w1 = T["space"][:].bitcast(F16)

        def w1_piece(e, k, part):
            return w1[:, w1_at(e, k, 0, part):w1_at(e, k, 0, part) + F]

        w2 = sb("w2", [P, E * KF * 2 * D], F16)

        def w2_piece(e, i):
            at = w2_at(e, (i - KD) * 4)
            both = w2[:, at:at + 4 * 2 * D].rearrange("p (f c d) -> p f c d", c=2, d=D)
            return both[:, :, 0], both[:, :, 1]

        lnw_all = sb("lnw_all", [P, E * KD], F32)
        b1_all = sb("b1_all", [P, E * KF], F32)
        b2_all = sb("b2_all", [P, E * D], F32)
        xf = sb("xf", [P, TT, D], F32)
        work = sb("work", [P, 4096], F32)
        stats, mean_var = sb("g_stats", [P, TT, 6], F32), sb("g_mean_var", [P, 2, TT, 2], F32)
        var_eps, rstd = sb("g_var_eps", [P, 2, TT], F32), sb("g_rstd", [P, 2, TT], F32)
        minus_half, eps = sb("g_minus_half", [P, TT], F32), sb("g_eps", [P, TT], F32)
        wg = sb("wg", [P, KD, E], F32)
        alpha = sb("alpha", [P, E], F32)
        expert_no, tile_no = sb("expert_no", [P, E], F32), sb("tile_no", [P, TILES], F32)
        before, ones = sb("before", [P, P], F32), sb("ones", [P, P], F32)
        up_to = sb("up_to", [P, E, E], F32)
        gap, gap_exp = sb("gap", [P, TT], F32), sb("gap_exp", [P, TT], F32)
        share = sb("share", [P, 2, TT], F32)
        share_alpha = sb("share_alpha", [P, 2, TT], F32)
        mix = sb("mix", [P, 2, TT], F32)
        count_i, tiles_i = sb("count_i", [P, E], I32), sb("tiles_i", [P, E], I32)
        tiles_f = sb("tiles_f", [P, E], F32)
        run_end, run_start = sb("run_end", [P, E], F32), sb("run_start", [P, E], F32)
        place_f, place_u = sb("place_f", [P, 2, TT], F32), sb("place_u", [P, 2, TT], U32)
        owner_f, owner = sb("owner_f", [P, TILES], F32), sb("owner", [P, TILES], I32)
        weights_at = sb("weights_at", [P, TILES], I32)
        x_in, y_out = xf[:, 0:2], xf[:, 2:4]
        xt_hi = xf[:, 4].bitcast(F16).rearrange("p (s k n) -> p s k n", s=2, k=KD)
        xt_lo = xf[:, 5].bitcast(F16).rearrange("p (s k n) -> p s k n", s=2, k=KD)
        b1_now = sb("b1_now", [P, 2, KF], F32)
        xf_t = work[:].rearrange("p (g k n) -> p g k n", g=4, k=KD)
        hid = work[:, 0:1024].rearrange("p (h c) -> p h c", h=2)
        hid_hi = work[:, 1024:2048].bitcast(F16).rearrange("p (s h c) -> p s h c", s=2, h=2)
        hid_lo = work[:, 2048:3072].bitcast(F16).rearrange("p (s h c) -> p s h c", s=2, h=2)

        def in_work(i, shape):
            a, b = shape
            return work[:, i * TT * E:i * TT * E + a * b].rearrange("p (a b) -> p a b", b=b)

        logits, top, top_no = (in_work(i, (TT, E)) for i in range(3))
        top_at = in_work(3, (TT, E)).bitcast(U32)
        chosen = work[:, 4 * TT * E:6 * TT * E].rearrange("p (c t e) -> p c t e", c=2, e=E)
        both, scratch, place = (in_work(i, (TT, E)) for i in range(6, 9))
        passed, scratch_e = in_work(9, (TILES, E)), in_work(12, (E, E))
        y_in = w_in[:].rearrange("p a (b c d) -> p (a b) c d", b=2, c=2)
        Y_RING = 8

        LOGIT_BANK, RANK_BANK, COUNT_BANK, BIAS_BANK = 4, 5, 6, 7
        H_BANKS = ((0, 1), (6, 7))
        Y_BANK, X_BANK = 2, 4

        gate_in, gate_const, pool_chain, dve_chain = sem("gate_in"), sem("gate_const"), sem("g_pool_chain"), sem("g_dve_chain")
        w_loaded = [sem(f"w_loaded{i}") for i in range(PIECES)]
        w_hi_done, w_lo_done, bias_ready, bias_done, bias_used = sem("e_w_hi"), sem("e_w_lo"), sem("bias_ready"), sem("bias_done"), sem("bias_used")
        lnw_done, moments, rstd_done, normed = sem("lnw_done"), sem("g_moments"), sem("g_rstd_done"), sem("g_normed")
        turned, xf_copied, logits_ready = sem("g_turned"), sem("g_copied"), sem("logits_ready")
        gap_done, gap_exp_done, chosen_done, ranks_ready = sem("gap_done"), sem("gap_exp_done"), sem("chosen_done"), sem("ranks_ready")
        renormed, places_done, owners_done, sorted_rows = sem("renormed"), sem("places_done"), sem("owners_done"), sem("sorted_rows")
        row_loaded = [sem(f"row_loaded{i}") for i in range(2)]
        x_turned, x_hi_done, x_lo_done, b1_picked = sem("x_turned"), sem("x_hi_done"), sem("x_lo_done"), sem("b1_picked")
        h_ready, gelu_done, hid_hi_done, hid_done, hid_used = (
            sem("h_ready"), sem("gelu_done"), sem("hid_hi_done"), sem("hid_done"), sem("hid_used"))
        y_hi_done, y_done, y_stored = sem("y_hi_done"), sem("y_done"), [sem(f"y_stored{i}") for i in range(2)]
        y_back = [sem(f"y_back{i}") for i in range(Y_RING)]
        half_added, added, stored = sem("half_added"), sem("added"), sem("stored")
        FREE = {gelu_done: 4, hid_done: 2, hid_used: 4, x_lo_done: 2, y_done: 2, b1_picked: 1}

        block = ctx.enter_context(nc.Block())

        def tile_loop(eng, pair):
            with eng.Fori(0, (TILES - 2) // 2) as i:
                pair(i, 3)
            for i in range((TILES - 2) // 2, (TILES + 1) // 2):
                pair(i, TILES - 1 - 2 * i)

        assert TILES % 2 == 1

        @block.sync
        def _(sp):
            w1_v = A["L0_ffn_fc1_w"].rearrange("e (k p) f -> e k p f", p=P)
            w2_v = A["L0_ffn_fc2_w"].rearrange("e (h f p) d -> e h p f d", p=P, h=2)
            for e in range(E):
                for i in range(PIECES):
                    if e:
                        sp.wait_ge(w_lo_done, (e - 1) * PIECES + i + 1)
                        if i < KD:
                            sp.wait_ge(bias_ready, (e - 1) * KD + i + 1)
                    if i < KD:
                        sp.dma_start(w_in[:, i], w1_v[e, i]).then_inc(w_loaded[i], 16)
                    else:
                        sp.dma_start(w_in[:, i].rearrange("p (f d) -> p f d", d=D), w2_v[e, i - KD]).then_inc(w_loaded[i], 16)
            sp.wait_ge(sorted_rows, 2 * TT * 16)
            rows_v = rows.rearrange("(t p) d -> t p d", p=P)
            ys_v = ys.rearrange("(t p) d -> t p d", p=P)
            for t in range(2):
                sp.dma_start(x_in[:, t], rows_v[t]).then_inc(row_loaded[t], 16)
            for t in range(2, 4):
                sp.wait_ge(x_turned, t - 1)
                sp.dma_start(x_in[:, t % 2], rows_v[t]).then_inc(row_loaded[t % 2], 16)

            def tile(i, parity, t, ahead):
                if ahead:
                    sp.wait_ge(x_turned, t + 3)
                    sp.dma_start(x_in[:, parity], rows_v[bass.ds(t + 4, 1)].rearrange("o p d -> (o p) d"))\
                      .then_inc(row_loaded[parity], 16)
                sp.wait_ge(y_done, t + 1 + FREE[y_done])
                dst = ys_v[t] if isinstance(t, int) else ys_v[bass.ds(t, 1)].rearrange("o p d -> (o p) d")
                sp.dma_start(dst, y_out[:, parity]).then_inc(y_stored[parity], 16)

            with sp.Fori(0, (TILES - 4) // 2) as i:
                for parity in range(2):
                    tile(i, parity, 2 * i + parity, True)
            for t in range((TILES - 4) // 2 * 2, TILES):
                tile(t // 2, t % 2, t, t + 4 < TILES)
            for t in range(TT):
                sp.wait_ge(added, t + 1)
                if t % NT == NT - 1:
                    b = t // NT
                    sp.dma_start(out[b].rearrange("(t p) d -> p t d", p=P), x1[:, b * NT:(b + 1) * NT, :]).then_inc(stored, 16)
            sp.wait_ge(stored, B * 16)

        @block.gpsimd
        def _(pool):
            pool.memset(eps[:], EPS).then_inc(pool_chain, 1)
            pool.memset(minus_half[:], -0.5).then_inc(pool_chain, 1)
            pool.iota(expert_no[:], [[1, E]], base=0, channel_multiplier=0, allow_small_or_imprecise_dtypes=True).then_inc(gate_const, 1)
            pool.iota(tile_no[:], [[1, TILES]], base=0, channel_multiplier=0, allow_small_or_imprecise_dtypes=True).then_inc(gate_const, 1)
            pool.memset(ones[:], 1.0).then_inc(gate_const, 1)
            pool.memset(up_to[:], 1.0).then_inc(pool_chain, 1)
            pool.wait_ge(pool_chain, 3)
            pool.wait_ge(gate_const, 3)
            pool.affine_select(out=before[:], in_=ones[:], compare_op=ALU.is_gt, fill=0.0, base=0,
                               pattern=[[1, P]], channel_multiplier=-1).then_inc(gate_const, 1)
            pool.affine_select(out=up_to[:], in_=up_to[:], compare_op=ALU.is_ge, fill=0.0, base=0,
                               pattern=[[1, E], [-1, E]], channel_multiplier=0).then_inc(gate_const, 1)
            for nth in range(2):
                pool.wait_ge(moments, nth + 1)
                pool.tensor_tensor(var_eps[:, nth], mean_var[:, nth, :, 1], eps[:], ALU.add).then_inc(pool_chain, 1)
                pool.wait_ge(pool_chain, nth + 4)
                pool.tensor_tensor(rstd[:, nth], var_eps[:, nth], minus_half[:], ALU.pow).then_inc(rstd_done, 1)
            pool.wait_ge(renormed, 1)
            pool.wait_ge(places_done, 1)
            for t in range(TT):
                for c in range(2):
                    pool.indirect_dma_start(rows, bass.IndirectOffsetOnAxis(ap=place_u[:, c, t:t + 1], axis=0),
                                            xf[:, t, :], None).then_inc(sorted_rows, 16)
            for parity in range(2):
                pool.wait_ge(y_stored[parity], (TILES + 1 - parity) // 2 * 16 + 16)
            for t in range(TT):
                if t >= Y_RING:
                    pool.wait_ge(added, t - Y_RING + 1)
                for c in range(2):
                    pool.indirect_dma_start(y_in[:, t % Y_RING, c], None, ys,
                                            bass.IndirectOffsetOnAxis(ap=place_u[:, c, t:t + 1], axis=0))\
                        .then_inc(y_back[t % Y_RING], 16)

        @block.scalar
        def _(act):
            act.sem_inc(gelu_done, FREE[gelu_done])
            act.dma_start(wg[:], A["L0_ffn_Wg"].rearrange("(k p) e -> p k e", p=P)).then_inc(gate_in, 16)
            act.dma_start(alpha[:], A["L0_ffn_alpha"].partition_broadcast(P)).then_inc(gate_in, 16)
            act.dma_start(b2_all[:], A["L0_ffn_fc2_b"].rearrange("e d -> (e d)").partition_broadcast(P)).then_inc(gate_in, 16)

            def weights_hi(pieces):
                for piece in pieces:
                    e, i = divmod(piece, PIECES)
                    act.wait_ge(w_loaded[i], (e + 1) * 16)
                    if i < KD:
                        if piece == 0:
                            act.wait_ge(lnw_done, 1)
                        ins = act.activation(w1_piece(e, i, 0), w_in[:, i], ACT.Identity,
                                             scale=lnw_all[:, e * KD + i:e * KD + i + 1])
                    else:
                        ins = act.activation(w2_piece(e, i)[0], w_in[:, i].rearrange("p (f d) -> p f d", d=D),
                                             ACT.Copy, scale=F_SCALE)
                    ins.then_inc(w_hi_done, 1)

            weights_hi(range(0, 3))
            for g in range(BLOCKS):
                act.wait_ge(turned, g + 1)
                for k in range(KD):
                    ins = act.activation(xf_t[:, g, k], ps[:, g % 2 * KD + k], ACT.Copy)
                ins.then_inc(xf_copied, 1)
            weights_hi(range(3, 15))
            act.wait_ge(gap_done, 1)
            act.activation(gap_exp[:], gap[:], ACT.Exp).then_inc(gap_exp_done, 1)
            weights_hi(range(15, E * PIECES))

            def x_hi(t, parity):
                act.wait_ge(x_turned, t + 1)
                act.activation(xt_hi[:, parity].rearrange("p k n -> p (k n)"), ps[:, X_BANK + parity, 0:KD * P],
                               ACT.Copy).then_inc(x_hi_done, 1)

            def gelu(t, parity, half):
                act.wait_ge(h_ready, 2 * t + half + 1)
                act.wait_ge(hid_done, 2 * t + half + 1)
                if half == 0:
                    act.wait_ge(b1_picked, t + 1 + FREE[b1_picked])
                for f in range(4):
                    c = slice(f * P, (f + 1) * P)
                    ins = act.activation(hid[:, half, c], ps[:, H_BANKS[parity][half], c], ACT.Gelu_apprx_tanh,
                                         bias=b1_now[:, parity, half * 4 + f:half * 4 + f + 1], scale=1 / F_SCALE)
                ins.then_inc(gelu_done, 1)

            act.activation(gap_exp[:], gap[:], ACT.Gelu_apprx_tanh)
            x_hi(0, 0)
            x_hi(1, 1)
            for half in range(2):
                gelu(0, 0, half)

            def pair(i, more):
                for parity in range(min(more, 2)):
                    t = 2 * i + parity
                    gelu(t + 1, 1 - parity, 0)
                    if more >= 2 + parity:
                        x_hi(t + 2, parity)
                    gelu(t + 1, 1 - parity, 1)
            tile_loop(act, pair)

        @block.vector
        def _(dve):
            for s in (hid_done, x_lo_done, y_done, b1_picked):
                dve.sem_inc(s, FREE[s])
            chain = [0]

            def link(ins):
                chain[0] += 1
                ins.then_inc(dve_chain, 1)
                dve.wait_ge(dve_chain, chain[0])

            def weights_lo(pieces):
                for piece in pieces:
                    e, i = divmod(piece, PIECES)
                    dve.wait_ge(w_hi_done, piece + 1)
                    if i < KD:
                        full, w_hi, w_lo, scale = w_in[:, i], w1_piece(e, i, 0), w1_piece(e, i, 1), lnw_all[:, e * KD + i:e * KD + i + 1]
                    else:
                        full, scale = w_in[:, i].rearrange("p (f d) -> p f d", d=D), F_SCALE
                        w_hi, w_lo = w2_piece(e, i)
                    dve.scalar_tensor_tensor(out=w_lo, in0=full, scalar=scale, in1=w_hi,
                                             op0=ALU.mult, op1=ALU.subtract).then_inc(w_lo_done, 1)

            def tile_moments(tokens, nth):
                for t in range(TT):
                    ins = dve.bn_stats(stats[:, t, :], tokens[:, t, :])
                link(ins)
                for t in range(TT):
                    ins = dve.bn_aggr(mean_var[:, nth, t, :], stats[:, t, :])
                ins.then_inc(moments, 1)

            def normalise(tokens, nth, done):
                for t in range(TT):
                    ins = dve.tensor_scalar(xf[:, t, :], tokens[:, t, :], mean_var[:, nth, t, 0:1],
                                            rstd[:, nth, t:t + 1], ALU.subtract, ALU.mult)
                    if t % NT == NT - 1:
                        ins.then_inc(done, 1)

            dve.tensor_scalar(lnw_all[:], vec_t[:, ROW_LNW:ROW_LNW + E * KD], F_SCALE, None, ALU.mult).then_inc(lnw_done, 1)
            tile_moments(x1, 0)
            dve.wait_ge(lnw_done, 1)
            weights_lo(range(0, 3))
            dve.wait_ge(rstd_done, 1)
            normalise(x1, 0, normed)
            dve.wait_ge(normed, BLOCKS)
            dve.wait_ge(moments, 1)
            tile_moments(xf, 1)
            weights_lo(range(3, 9))
            dve.wait_ge(rstd_done, 2)
            dve.wait_ge(turned, BLOCKS)
            normalise(xf, 1, renormed)
            weights_lo(range(9, 15))
            dve.wait_ge(logits_ready, 1)
            link(dve.tensor_copy(logits.rearrange("p t e -> p (t e)"), ps[:, LOGIT_BANK, 0:TT * E]))
            for t in range(TT):
                ins = dve.max(top[:, t, :], logits[:, t, :])
            link(ins)
            for t in range(TT):
                ins = dve.max_index(top_at[:, t, :], top[:, t, :], logits[:, t, :])
            link(ins)
            dve.tensor_tensor(gap[:], top[:, :, 1], top[:, :, 0], ALU.subtract).then_inc(gap_done, 1)
            link(dve.tensor_copy(top_no, top_at))
            dve.wait_ge(gate_const, 5)
            wide = [P, TT, E]
            for c in range(2):
                ins = dve.tensor_tensor(chosen[:, c], expert_no[:].unsqueeze(1).broadcast_to(wide),
                                        top_no[:, :, c:c + 1].broadcast_to(wide), ALU.is_equal)
            link(ins)
            dve.tensor_tensor(both, chosen[:, 0], chosen[:, 1], ALU.add).then_inc(chosen_done, 1)
            dve.wait_ge(gap_exp_done, 1)
            link(dve.tensor_scalar(gap[:], gap_exp[:], 1.0, None, ALU.add))
            link(dve.reciprocal(share[:, 0], gap[:]))
            link(dve.tensor_tensor(share[:, 1], gap_exp[:], share[:, 0], ALU.mult))
            dve.wait_ge(gate_in, 48)
            for c in range(2):
                link(dve.tensor_tensor(scratch, chosen[:, c], alpha[:].unsqueeze(1).broadcast_to(wide), ALU.mult))
                link(dve.tensor_reduce(share_alpha[:, c], scratch, AX.X, ALU.add))
            link(dve.tensor_tensor(mix[:], share[:], share_alpha[:], ALU.mult))
            dve.wait_ge(ranks_ready, 1)
            link(dve.tensor_scalar(count_i[:], ps[:, COUNT_BANK, 0:E], float(P - 1), None, ALU.add))
            link(dve.tensor_scalar(tiles_i[:], count_i[:], P.bit_length() - 1, None, ALU.logical_shift_right))
            link(dve.tensor_copy(tiles_f[:], tiles_i[:]))
            link(dve.tensor_tensor(scratch_e, tiles_f[:].unsqueeze(1).broadcast_to([P, E, E]), up_to[:], ALU.mult))
            link(dve.tensor_reduce(run_end[:], scratch_e, AX.X, ALU.add))
            link(dve.tensor_tensor(run_start[:], run_end[:], tiles_f[:], ALU.subtract))
            link(dve.tensor_scalar(run_start[:], run_start[:], float(P), None, ALU.mult))
            link(dve.tensor_tensor(place, ps[:, RANK_BANK, 0:TT * E].rearrange("p (t e) -> p t e", e=E),
                                   run_start[:].unsqueeze(1).broadcast_to(wide), ALU.add))
            for c in range(2):
                link(dve.tensor_tensor(scratch, chosen[:, c], place, ALU.mult))
                link(dve.tensor_reduce(place_f[:, c], scratch, AX.X, ALU.add))
            dve.tensor_copy(place_u[:], place_f[:]).then_inc(places_done, 1)
            tiles_wide = [P, TILES, E]
            link(dve.tensor_tensor(passed, tile_no[:].unsqueeze(2).broadcast_to(tiles_wide),
                                   run_end[:].unsqueeze(1).broadcast_to(tiles_wide), ALU.is_ge))
            link(dve.tensor_reduce(owner_f[:], passed, AX.X, ALU.add))
            link(dve.tensor_scalar(owner_f[:], owner_f[:], float(E - 1), None, ALU.min))
            dve.tensor_copy(owner[:], owner_f[:]).then_inc(owners_done, 1)
            dve.tensor_scalar(weights_at[:], owner_f[:], float(2 * KD * F), None, ALU.mult).then_inc(owners_done, 1)
            weights_lo(range(15, E * PIECES))
            dve.wait_ge(bias_ready, E * KD)
            dve.tensor_tensor(b1_all[:], ps[:, BIAS_BANK, 0:E * KF], vec_t[:, ROW_B1:ROW_B1 + E * KF], ALU.add).then_inc(bias_done, 1)
            dve.wait_ge(bias_done, 1)
            dve.wait_ge(owners_done, 2)

            def owner_of(t):
                return dve.value_load(owner[0:1, bass.ds(t, 1)], min_val=0, max_val=E - 1)

            def pick_b1(t, parity):
                dve.tensor_copy(b1_now[:, parity], b1_all[:, bass.ds(owner_of(t) * KF, KF)]).then_inc(b1_picked, 1)

            def x_lo(t, parity):
                dve.wait_ge(x_hi_done, t + 1)
                dve.tensor_tensor(xt_lo[:, parity].rearrange("p k n -> p (k n)"), ps[:, X_BANK + parity, 0:KD * P],
                                  xt_hi[:, parity].rearrange("p k n -> p (k n)"), ALU.subtract).then_inc(x_lo_done, 1)

            def split(t, parity, half):
                dve.wait_ge(gelu_done, 2 * t + half + 1 + FREE[gelu_done])
                dve.wait_ge(hid_used, 2 * t + half + 1)
                dve.tensor_copy(hid_hi[:, parity, half], hid[:, half]).then_inc(hid_hi_done, 1)
                dve.wait_ge(hid_hi_done, 2 * t + half + 1)
                dve.tensor_tensor(hid_lo[:, parity, half], hid[:, half], hid_hi[:, parity, half],
                                  ALU.subtract).then_inc(hid_done, 1)

            def y(i, t, parity):
                e = owner_of(t)
                dve.wait_ge(hid_used, 2 * t + 2 + FREE[hid_used])
                dve.wait_ge(y_stored[parity], i * 16 + 16)
                dve.scalar_tensor_tensor(out=y_out[:, parity], in0=ps[:, Y_BANK + parity, 0:D], scalar=1 / F_SCALE,
                                         in1=b2_all[:, bass.ds(e * D, D)], op0=ALU.mult, op1=ALU.add).then_inc(y_hi_done, 1)
                dve.wait_ge(y_hi_done, t + 1)
                dve.scalar_tensor_tensor(out=y_out[:, parity], in0=ps[:, Y_BANK + parity, D:2 * D], scalar=1 / F_SCALE,
                                         in1=y_out[:, parity], op0=ALU.mult, op1=ALU.add).then_inc(y_done, 1)

            for t in range(2):
                pick_b1(t, t)
                x_lo(t, t)
                dve.sem_inc(y_stored[t], 16)

            for half in range(2):
                split(0, 0, half)

            def pair(i, more):
                for parity in range(min(more + 1, 2)):
                    t = 2 * i + parity
                    if more >= 1 + parity:
                        split(t + 1, 1 - parity, 0)
                    if more >= 2 + parity:
                        x_lo(t + 2, parity)
                        pick_b1(t + 2, parity)
                    if more >= 1 + parity:
                        split(t + 1, 1 - parity, 1)
                    y(i, t, parity)
            tile_loop(dve, pair)

            def second(t):
                dve.wait_ge(half_added, t + 1)
                dve.scalar_tensor_tensor(out=x1[:, t, :], in0=y_in[:, t % Y_RING, 1], scalar=mix[:, 1, t:t + 1],
                                         in1=x1[:, t, :], op0=ALU.mult, op1=ALU.add).then_inc(added, 1)
            for t in range(TT):
                dve.wait_ge(y_back[t % Y_RING], (t // Y_RING + 1) * 32)
                dve.scalar_tensor_tensor(out=x1[:, t, :], in0=y_in[:, t % Y_RING, 0], scalar=mix[:, 0, t:t + 1],
                                         in1=x1[:, t, :], op0=ALU.mult, op1=ALU.add).then_inc(half_added, 1)
                if t:
                    second(t - 1)
            second(TT - 1)

        @block.tensor
        def _(pe):
            pe.sem_inc(hid_used, FREE[hid_used])

            def bias_sums(e):
                for k in range(KD):
                    pe.wait_ge(w_loaded[k], (e + 1) * 16)
                    for f in range(KF):
                        c = e * KF + f
                        ins = pe.matmul(ps[:, BIAS_BANK, c:c + 1], w_in[:, k, f * P:(f + 1) * P],
                                        vec_t[:, ROW_LNB + e * KD + k:ROW_LNB + e * KD + k + 1],
                                        start=e == 0 and k == 0 and f == 0, stop=k == KD - 1, skip_group_check=True)
                    ins.then_inc(bias_ready, 1)

            bias_sums(0)
            for g in range(BLOCKS):
                pe.wait_ge(normed, g + 1)
                if g >= 2:
                    pe.wait_ge(xf_copied, g - 1)
                for k in range(KD):
                    for t in range(NT):
                        ins = pe.transpose(ps[:, g % 2 * KD + k, t * P:(t + 1) * P],
                                           xf[:, g * NT + t, k * P:(k + 1) * P], ident[:])
                ins.then_inc(turned, 1)
            bias_sums(1)
            pe.wait_ge(gate_in, 48)
            for g in range(BLOCKS):
                pe.wait_ge(xf_copied, g + 1)
                for t in range(NT):
                    for k in range(KD):
                        c = (g * NT + t) * E
                        ins = pe.matmul(ps[:, LOGIT_BANK, c:c + E], xf_t[:, g, k, t * P:(t + 1) * P], wg[:, k],
                                        start=g == 0 and t == 0 and k == 0, stop=k == KD - 1, skip_group_check=True)
            ins.then_inc(logits_ready, 1)
            bias_sums(2)
            bias_sums(3)
            pe.wait_ge(chosen_done, 1)
            pe.wait_ge(gate_const, 5)
            pe.matmul(ps[:, RANK_BANK, 0:TT * E], before[:], both.rearrange("p t e -> p (t e)"),
                      start=True, stop=False, skip_group_check=True)
            for t in range(TT):
                later = TT - 1 - t
                if later:
                    pe.matmul(ps[:, RANK_BANK, (t + 1) * E:TT * E].rearrange("p (t e) -> p t e", e=E), ones[:],
                              both[:, t:t + 1, :].broadcast_to([P, later, E]),
                              start=False, stop=False, skip_group_check=True)
                ins = pe.matmul(ps[:, COUNT_BANK, 0:E], ones[:], both[:, t, :], start=t == 0, stop=t == TT - 1,
                                skip_group_check=True)
            ins.then_inc(ranks_ready, 1)
            for e in range(4, E):
                bias_sums(e)
            pe.wait_ge(owners_done, 2)

            def weights_of(t):
                return pe.value_load(weights_at[0:1, bass.ds(t, 1)], min_val=0, max_val=(E - 1) * 2 * KD * F)

            def turn(i, t, parity):
                pe.wait_ge(row_loaded[parity], (i + 1) * 16)
                pe.wait_ge(x_lo_done, t + 1)
                for k in range(KD):
                    ins = pe.transpose(ps[:, X_BANK + parity, k * P:(k + 1) * P], x_in[:, parity, k * P:(k + 1) * P], ident[:])
                ins.then_inc(x_turned, 1)

            def fc1_ready(t, parity, half):
                pe.wait_ge(gelu_done, 2 * t + half + 1)
                if half == 0:
                    pe.wait_ge(x_lo_done, t + 1 + FREE[x_lo_done])

            def fc1_part(e, parity, half, f):
                out = ps[:, H_BANKS[parity][half], f * P:(f + 1) * P]
                for k in range(KD):
                    w_hi, w_lo = (w1[:, bass.ds(e + w1_at(0, k, half * 4 + f, part), P)] for part in range(2))
                    pe.matmul(out, w_hi, xt_hi[:, parity, k], start=f == 0 and k == 0, stop=False, skip_group_check=True)
                    pe.matmul(out, w_hi, xt_lo[:, parity, k], start=False, stop=False, skip_group_check=True)
                    ins = pe.matmul(out, w_lo, xt_hi[:, parity, k], start=False, stop=k == KD - 1, skip_group_check=True)
                return ins

            def fc1(t, e, parity, half):
                fc1_ready(t, parity, half)
                for f in range(4):
                    ins = fc1_part(e, parity, half, f)
                ins.then_inc(h_ready, 1)

            def fc2_ready(t, half):
                pe.wait_ge(hid_done, 2 * t + half + 1 + FREE[hid_done])
                if half == 0:
                    pe.wait_ge(y_done, t + 1)

            def fc2_part(e, parity, half, f):
                c, w = slice(f * P, (f + 1) * P), w2[:, bass.ds(e + w2_at(0, half * 4 + f), 2 * D)]
                pe.matmul(ps[:, Y_BANK + parity], hid_hi[:, parity, half, c], w,
                          start=half == 0 and f == 0, stop=False, skip_group_check=True)
                return pe.matmul(ps[:, Y_BANK + parity, 0:D], hid_lo[:, parity, half, c], w[:, 0:D],
                                 start=False, stop=half == 1 and f == 3, skip_group_check=True)

            def fc2(t, e, parity, half):
                fc2_ready(t, half)
                for f in range(4):
                    ins = fc2_part(e, parity, half, f)
                ins.then_inc(hid_used, 1)

            turn(0, 0, 0)
            turn(0, 1, 1)
            pe.wait_ge(w_lo_done, E * PIECES)
            pe.wait_ge(bias_done, 1)

            first = weights_of(0)
            for half in range(2):
                fc1(0, first, 0, half)
            ahead = [pe.alloc_register("even_weights"), pe.alloc_register("odd_weights")]
            pe.reg_mov(ahead[0], first)
            pe.reg_mov(ahead[1], weights_of(1))

            def pair(i, more):
                owners = [pe.snap(r, min_val=0, max_val=(E - 1) * 2 * KD * F) for r in ahead]
                for parity in range(min(more, 2)):
                    t = 2 * i + parity
                    for half in range(2):
                        fc1_ready(t + 1, 1 - parity, half)
                        fc2_ready(t, half)
                        for f in range(4):
                            h = fc1_part(owners[parity + 1], 1 - parity, half, f)
                            used = fc2_part(owners[parity], parity, half, f)
                        h.then_inc(h_ready, 1)
                        used.then_inc(hid_used, 1)
                        if half == 0 and more >= 2 + parity:
                            turn(i + 1, t + 2, parity)
                            owners.append(weights_of(t + 2))
                for r, owner_ahead in zip(ahead, owners[2:]):
                    pe.reg_mov(r, owner_ahead)
                if more == 0:
                    for half in range(2):
                        fc2(2 * i, owners[0], 0, half)
            tile_loop(pe, pair)


def program(nc, A, out):
    with ExitStack() as ctx:
        T = {
            "space": ctx.enter_context(nc.sbuf_tensor("space", [P, 16384], F32)),
            "x1": ctx.enter_context(nc.sbuf_tensor("x1", [P, TT, D], F32)),
            "ident": ctx.enter_context(nc.sbuf_tensor("ident", [P, P], F32)),
            "vec_t": ctx.enter_context(nc.sbuf_tensor("vec_t", [P, P], F32)),
            "ps": ctx.enter_context(nc.psum_tensor("ps", [P, 8, 512], F32)),
        }
        T["rows"] = nc.dram_tensor("rows_by_expert", (TILES * P, D), F32, kind="Internal").ap()
        attention_block(nc, A, T)
        experts_block(nc, A, T, out)


INPUTS = ["x", "ctx_1024", "L0_xattn_ln_l_w", "L0_xattn_ln_l_b", "L0_xattn_ln_c_w", "L0_xattn_ln_c_b",
          "L0_xattn_Wq", "L0_xattn_Wkv", "L0_xattn_Wo", "L0_xattn_bo", "L0_ffn_Wg", "L0_ffn_alpha",
          "L0_ffn_ln_w", "L0_ffn_ln_b", "L0_ffn_fc1_w", "L0_ffn_fc1_b", "L0_ffn_fc2_w", "L0_ffn_fc2_b"]


def kernel(**inputs):
    import numpy as np
    import concourse.bacc as bacc
    from concourse.bass_utils import run_bass_kernel_spmd

    nc = bacc.Bacc("TRN2", target_bir_lowering=False, num_devices=1)
    arrays, aps = {}, {}
    for name in INPUTS:
        a = np.ascontiguousarray(inputs[name])
        arrays[f"in_{name}"] = a
        aps[name] = nc.dram_tensor(f"in_{name}", a.shape, mybir.dt.from_np(a.dtype), kind="ExternalInput").ap()
    out = nc.dram_tensor("out", (B, N, D), F32, kind="ExternalOutput").ap()
    program(nc, aps, out)
    r = run_bass_kernel_spmd(nc, [arrays], core_ids=[0])
    return r.results[0]["out"]
```

```python
from contextlib import ExitStack
import math

import concourse.bass as bass
from concourse import mybir

F32 = mybir.dt.float32
F16 = mybir.dt.float16
U32 = mybir.dt.uint32
I32 = mybir.dt.int32
AX = mybir.AxisListType
ALU = mybir.AluOpType
ACT = mybir.ActivationFunctionType

P = 128
B = 4
N = 512
S = 1024
D = 256
KD = D // P
H = 16
DH = 64
INNER = H * DH
KI = INNER // P
NT = N // P
ST = S // P
EPS = 1e-5
CLIP = 11.0
W_SCALE = 16.0
LO_SCALE = 2048.0
VW = 130
UNITS = 8
LEAD = 3
E_RING = 4
P_RING = 4
TT = B * NT

E = 8
F = 1024
KF = F // P
F_SCALE = 64.0
PIECES = 4
TILES = 2 * TT + E - 1
ID_AT, MIX_AT = D, D + 1
ROW_W = D + 1 + E
CLEARED = -(-TILES // B)


def w1_at(e, k, f, part=0):
    return ((e * 2 + part) * KD + k) * F + f * P


def w2_at(e, f):
    return (e * KF + f) * 2 * D


ROW_B1, ROW_LNW, ROW_LNB, ROW_LW, ROW_LB, ROW_CW, ROW_CB = 0, 64, 80, 96, 98, 100, 102


def w_buffers(T):
    space = [T["space"][:, at:at + 4096].rearrange("p (a n) -> p a n", a=PIECES) for at in (8192, 12288)]
    return [T["w_even"], T["w_odd"]] + space + [T["w_even"], T["w_odd"]] * 2


AHEAD = 4


def load_piece(eng, A, dst, e, i):
    if i < KD:
        return eng.dma_start(dst, A["L0_ffn_fc1_w"].rearrange("e (k p) f -> e k p f", p=P)[e, i])
    w2_v = A["L0_ffn_fc2_w"].rearrange("e (h f p) d -> e h p f d", p=P, h=2)
    return eng.dma_start(dst.rearrange("p (f d) -> p f d", d=D), w2_v[e, i - KD])


def attention_block(nc, A, T):
    with ExitStack() as ctx:
        def sb(name, shape, dt):
            return ctx.enter_context(nc.sbuf_tensor(name, shape, dt))

        def sem(name):
            return ctx.enter_context(nc.semaphore(name))

        x1, ident, vec_t, xf, logits = T["x1"], T["ident"], T["vec_t"], T["xf"], T["logits"]
        wq_hi, wq_lo = sb("wq_hi", [P, KD, INNER], F16), sb("wq_lo", [P, KD, INNER], F16)
        wkv_hi, wkv_lo = (T["w_odd"][:, KD * c:KD * (c + 1)].bitcast(F16) for c in range(2))
        wo_hi, wo_lo = sb("wo_hi", [P, KI, D], F16), sb("wo_lo", [P, KI, D], F16)
        stage = T["space"][:, 0:8192]
        vec_rows = sb("vec_rows", [P, P], F32)
        bo_all, blank = sb("bo_all", [P, D], F32), sb("blank", [P, ROW_W], F32)
        tokens = T["w_even"][:].rearrange("p a (t d) -> p (a t) d", d=D)
        ctx_in, x_in, lat = tokens[:, 0:ST], tokens[:, ST:ST + NT], tokens[:, ST + NT:ST + 2 * NT]
        stats = sb("stats", [P, ST + NT, 6], F32)
        mean_var = sb("mean_var", [P, 16, 2], F32)
        var_eps = sb("var_eps", [P, 16], F32)
        rstd = sb("rstd", [P, 16], F32)
        neg_mean, nought = sb("neg_mean", [P, 16], F32), sb("nought", [P, 16], F32)
        shift = sb("shift", [P, 16], F32)
        minus_half = sb("minus_half", [P, 16], F32)
        eps = sb("eps", [P, 16], F32)
        ln_lo_scale = sb("ln_lo_scale", [P, 1], F32)
        warm = sb("warm", [P, 1], F32)
        affine = sb("affine", [P, 3, N], F32)
        ctx_hi, ctx_lo = sb("ctx_hi", [P, KD, S], F16), sb("ctx_lo", [P, KD, S], F16)
        lat_hi, lat_lo = sb("lat_hi", [P, KD, N], F16), sb("lat_lo", [P, KD, N], F16)
        keys = sb("keys", [P, 2, 2, S], F16)
        qrys = sb("qrys", [P, 2, 2, 2, N], F16)
        vals = sb("vals", [P, 2, ST, 2, VW], F16)
        vals_s = sb("vals_s", [P, 2, ST, 2, 66], F16)
        expo = T["space"][:, 8192:12288].rearrange("p (r n) -> p r n", r=E_RING)
        p_hi, p_lo = (T["space"][:, 12288 + i * 2048:14336 + i * 2048].bitcast(F16)
                      .rearrange("p (r n) -> p r n", r=P_RING) for i in range(2))
        g_stats, g_mean_var = sb("g_stats", [P, NT, 6], F32), sb("g_mean_var", [P, 2, NT, 2], F32)
        g_var_eps, g_rstd = sb("g_var_eps", [P, 2, NT], F32), sb("g_rstd", [P, 2, NT], F32)
        xn, xf_t = sb("xn", [P, NT, D], F32), sb("xf_t", [P, KD, N], F32)
        wg = sb("wg", [P, KD, E], F32)
        o_lo = sb("o_lo", [P, NT, DH], F32)
        o_sum = sb("o_sum", [P, 2, NT, DH], F32)
        o_rec = sb("o_rec", [P, 2, NT], F32)
        attn = stage[:, 0:NT * INNER].rearrange("p (n i) -> p n i", n=NT)
        attn_t = stage[:, NT * INNER:].bitcast(F16).rearrange("p (c j n) -> p c j n", c=2, j=KI)
        wkv_in = stage[:, 0:KD * 2 * INNER].rearrange("p (k n) -> p k n", k=KD)
        wq_in = stage[:, 4096:6144].rearrange("p (k n) -> p k n", k=KD)
        wo_in = stage[:, 6144:8192].rearrange("p (k n) -> p k n", k=KI)

        ps = T["ps"]
        S_BANK, O_BANK, J_BANK = 0, 4, 6
        G_BANK, LOGIT_BANK = 2, 5

        def o_ps(n):
            return ps[:, O_BANK + n // 2, (n % 2) * 256:(n % 2) * 256 + 129]

        o_all = ps[:, O_BANK:O_BANK + 2, :].rearrange("p b (h c) -> p (b h) c", h=2)

        wkv_loaded, wq_loaded, wo_loaded = sem("wkv_loaded"), sem("wq_loaded"), sem("wo_loaded")
        ctx_loaded, x_loaded = sem("ctx_loaded"), sem("x_loaded")
        vec_in, consts, vec_turned, vec_done = sem("vec_in"), sem("consts"), sem("vec_turned"), sem("vec_done")
        rows_cleared, acc_cleared, blank_done, acc_set = sem("rows_cleared"), sem("acc_cleared"), sem("blank_done"), sem("acc_set")
        wait_taken, bo_in = sem("wait_taken"), sem("bo_in")
        ident_done, pool_chain, dve_chain = sem("ident_done"), sem("pool_chain"), sem("dve_chain")
        w_hi_done, w_lo_done = sem("w_hi_done"), sem("w_lo_done")
        moments, rstd_done, residual_done = sem("moments"), sem("rstd_done"), sem("residual_done")
        lat_first, lat_normed = sem("lat_first"), sem("lat_normed")
        ctx_normed, turned, affine_done, split_done = sem("ctx_normed"), sem("turned"), sem("affine_done"), sem("split_done")
        proj_ready, proj_hi, proj_free, q_twice = sem("proj_ready"), sem("proj_hi"), sem("proj_free"), sem("q_twice")
        scores_ready, exp_done, clip_done, hi_done, lo_done = (
            sem("scores_ready"), sem("exp_done"), sem("clip_done"), sem("hi_done"), sem("lo_done"))
        pv_done, o_lo_done, o_free, hi_copied, attn_done = (
            sem("pv_done"), sem("o_lo_done"), sem("o_free"), sem("hi_copied"), sem("attn_done"))
        first_loaded = sem("first_loaded")
        wg_in, g_chain, g_pool_chain = sem("wg_in"), sem("g_chain"), sem("g_pool_chain")
        g_moments, g_rstd_done, g_normed = sem("g_moments"), sem("g_rstd_done"), sem("g_normed")
        g_turned, g_copied, logits_ready, logits_done = (
            sem("g_turned"), sem("g_copied"), sem("logits_ready"), sem("logits_done"))
        at_ready, at_hi, at_lo, y_ready, x1_done = (
            sem("at_ready"), sem("at_hi"), sem("at_lo"), sem("y_ready"), sem("x1_done"))
        FREE = {exp_done: 2, lo_done: E_RING, pv_done: P_RING, o_free: 1, attn_done: 2, proj_free: 1,
                split_done: 3, x1_done: NT}

        block = ctx.enter_context(nc.Block())

        def batch_loop(eng, batch):
            with eng.Fori(0, B - 1) as b:
                batch(b, True)
            batch(B - 1, False)

        def turned_bank(i):
            return 4 + i if i < 4 else i - 4

        def pair_loop(eng, b, pair):
            with eng.Fori(0, KI // 2 - 1) as mm:
                pair(b, 2 * mm, 0, False)
                pair(b, 2 * mm + 1, 1, False)
            pair(b, KI - 2, 0, False)
            pair(b, KI - 1, 1, True)

        @block.sync
        def _(sp):
            ctx_v = A["ctx_1024"].rearrange("b (t p) d -> b p t d", p=P)
            x_v = A["x"].rearrange("b (t p) d -> b p t d", p=P)
            rows_v = T["rows"].rearrange("(b t p) d -> b p t d", b=B, p=P)
            acc_v = T["acc"][0:TT * P, :].rearrange("(b t p) d -> b p t d", b=B, p=P)
            sp.dma_start(x_in, x_v[0]).then_inc(x_loaded, 16)
            sp.dma_start(ctx_in, ctx_v[0]).then_inc(ctx_loaded, 16)
            sp.dma_start(wkv_in, A["L0_xattn_Wkv"].rearrange("(k p) n -> p k n", p=P)).then_inc(wkv_loaded, 16)
            sp.dma_start(wq_in, A["L0_xattn_Wq"].rearrange("(k p) n -> p k n", p=P)).then_inc(wq_loaded, 16)
            sp.dma_start(wo_in, A["L0_xattn_Wo"].rearrange("(k p) n -> p k n", p=P)).then_inc(wo_loaded, 16)

            def q_to_upper(pairs_before, parity):
                sp.wait_ge(proj_free, pairs_before * 5 + 1 + FREE[proj_free])
                sp.dma_start(qrys[DH:P, parity], qrys[0:DH, parity]).then_inc(q_twice, 16)

            def batch(b, more):
                if not more:
                    sp.wait_ge(turned, B * 6)
                    sp.wait_ge(residual_done, B)
                    for i in range(PIECES):
                        load_piece(sp, A, T["w_even"][:, i], 0, i).then_inc(first_loaded, 16)
                if more:
                    sp.wait_ge(turned, (b + 1) * 6)
                    sp.dma_start(ctx_in, ctx_v[bass.ds(b + 1, 1)].rearrange("o p t d -> (o p) t d")).then_inc(ctx_loaded, 16)
                    sp.wait_ge(residual_done, b + 1)
                    sp.dma_start(x_in, x_v[bass.ds(b + 1, 1)].rearrange("o p t d -> (o p) t d")).then_inc(x_loaded, 16)

                def pair(b, m, parity, last):
                    if not last:
                        q_to_upper(b * KI + m + 1, 1 - parity)
                pair_loop(sp, b, pair)
                sp.wait_ge(blank_done, 1)
                dst = rows_v[b] if isinstance(b, int) else rows_v[bass.ds(b, 1)].rearrange("o p t d -> (o p) t d")
                sp.dma_start(dst, blank[:].unsqueeze(1).broadcast_to([P, CLEARED, ROW_W])).then_inc(rows_cleared, 16)
                for e in range(1, 1 if more else AHEAD):
                    if e == 1:
                        sp.wait_ge(proj_ready, B * KI * 5)
                    if e == 2:
                        sp.wait_ge(pv_done, B * KI * UNITS + FREE[pv_done])
                    for i in range(PIECES):
                        load_piece(sp, A, w_buffers(T)[e][:, i], e, i).then_inc(first_loaded, 16)
                sp.wait_ge(x1_done, b * NT + NT + FREE[x1_done])
                dst = acc_v[b] if isinstance(b, int) else acc_v[bass.ds(b, 1)].rearrange("o p t d -> (o p) t d")
                sp.dma_start(dst, x1[:, bass.ds(b * NT, NT), :]).then_inc(acc_set, 16)
                if more:
                    q_to_upper((b + 1) * KI, 0)

            q_to_upper(0, 0)
            batch_loop(sp, batch)
            sp.wait_ge(first_loaded, AHEAD * PIECES * 16)
            sp.wait_ge(acc_set, B * 16)
            sp.wait_ge(rows_cleared, B * 16)

        @block.gpsimd
        def _(pool):
            chain = [0]

            def link(ins):
                chain[0] += 1
                ins.then_inc(pool_chain, 1)
                pool.wait_ge(pool_chain, chain[0])

            pool.sem_inc(attn_done, FREE[attn_done])
            link(pool.memset(ident[:], 0.0))
            pool.affine_select(out=ident[:], in_=ident[:], compare_op=ALU.not_equal, fill=1.0, base=0,
                               pattern=[[-1, P]], channel_multiplier=1).then_inc(ident_done, 1)
            link(pool.memset(minus_half[:], -0.5))
            link(pool.memset(eps[:], EPS))
            link(pool.memset(nought[:], 0.0))
            pool.wait_ge(consts, 3)
            pool.iota(blank[:].bitcast(I32)[:, ID_AT:ID_AT + 1], [[1, 1]], base=TT * P, channel_multiplier=1).then_inc(blank_done, 1)
            pool.dma_start(bo_all[:], A["L0_xattn_bo"].partition_broadcast(P)).then_inc(bo_in, 16)
            pool.dma_start(wg[:], A["L0_ffn_Wg"].rearrange("(k p) e -> p k e", p=P)).then_inc(wg_in, 16)
            PER_ROOT = 3

            def root(b, nth, a, z):
                before = (b * 3 + nth) * PER_ROOT + chain[0]
                pool.wait_ge(moments, b * 3 + nth + 1)
                pool.tensor_tensor(var_eps[:, a:z], mean_var[:, a:z, 1], eps[:, a:z], ALU.add).then_inc(pool_chain, 1)
                pool.tensor_tensor(neg_mean[:, a:z], nought[:, a:z], mean_var[:, a:z, 0], ALU.subtract).then_inc(pool_chain, 1)
                pool.wait_ge(pool_chain, before + 2)
                pool.tensor_tensor(rstd[:, a:z], var_eps[:, a:z], minus_half[:, a:z], ALU.pow).then_inc(pool_chain, 1)
                pool.wait_ge(pool_chain, before + 3)
                pool.tensor_tensor(shift[:, a:z], neg_mean[:, a:z], rstd[:, a:z], ALU.mult).then_inc(rstd_done, 1)

            def roots(b):
                root(b, 0, 8, 12)
                root(b, 1, 0, 8)
                root(b, 2, 12, 16)

            def batch(b, more):
                pool.wait_ge(x_loaded, b * 16 + 16)
                pool.wait_ge(bo_in, 16)
                pool.tensor_tensor(x1[:, bass.ds(b * NT, NT), :], x_in,
                                   bo_all[:].unsqueeze(1).broadcast_to([P, NT, D]), ALU.add).then_inc(residual_done, 1)

                def pair(b, m, parity, last):
                    for h in range(2):
                        pool.wait_ge(o_free, b * H + m * 2 + h + 1 + FREE[o_free])
                        pool.tensor_tensor(attn[:, :, bass.ds(m * P + h * DH, DH)], o_sum[:, h],
                                           o_rec[:, h].unsqueeze(2).broadcast_to([P, NT, DH]),
                                           ALU.mult).then_inc(attn_done, 1)
                pair_loop(pool, b, pair)
                if more:
                    roots(b + 1)
                for nth in range(2):
                    pool.wait_ge(g_moments, b * 2 + nth + 1)
                    pool.tensor_tensor(g_var_eps[:, nth], g_mean_var[:, nth, :, 1], eps[:, 0:NT], ALU.add).then_inc(g_pool_chain, 1)
                    pool.wait_ge(g_pool_chain, b * 2 + nth + 1)
                    pool.tensor_tensor(g_rstd[:, nth], g_var_eps[:, nth], minus_half[:, 0:NT], ALU.pow).then_inc(g_rstd_done, 1)

            roots(0)
            batch_loop(pool, batch)

        @block.scalar
        def _(act):
            act.sem_inc(exp_done, FREE[exp_done])
            for view, row in ((A["L0_ffn_fc1_b"].rearrange("e (f p) -> (e f) p", p=P), ROW_B1),
                              (A["L0_ffn_ln_w"].rearrange("e (k p) -> (e k) p", p=P), ROW_LNW),
                              (A["L0_ffn_ln_b"].rearrange("e (k p) -> (e k) p", p=P), ROW_LNB),
                              (A["L0_xattn_ln_l_w"].rearrange("(k p) -> k p", p=P), ROW_LW),
                              (A["L0_xattn_ln_l_b"].rearrange("(k p) -> k p", p=P), ROW_LB),
                              (A["L0_xattn_ln_c_w"].rearrange("(k p) -> k p", p=P), ROW_CW),
                              (A["L0_xattn_ln_c_b"].rearrange("(k p) -> k p", p=P), ROW_CB)):
                if row == ROW_B1:
                    act.wait_ge(consts, 1)
                act.dma_start(vec_rows[row:row + view.shape[0], :], view).then_inc(vec_in, 16)
            act.wait_ge(consts, 3)
            act.activation(warm[:], ln_lo_scale[:], ACT.Exp)
            def proj_hi_part(pairs_before, c, parity):
                act.wait_ge(proj_ready, pairs_before * 5 + c + 1)
                if c == 0:
                    act.activation(qrys[0:DH, parity, 0, 0], ps[0:DH, J_BANK], ACT.Copy, scale=1 / W_SCALE)
                    act.activation(qrys[0:DH, parity, 1, 0], ps[DH:P, J_BANK], ACT.Copy,
                                   scale=1 / W_SCALE).then_inc(proj_hi, 1)
                elif c < 3:
                    bank, t = J_BANK + c % 2, slice((c - 1) * 512, c * 512)
                    act.activation(keys[0:DH, parity, 0, t], ps[0:DH, bank], ACT.Copy, scale=1 / W_SCALE)
                    act.activation(keys[DH:P, parity, 1, t], ps[DH:P, bank], ACT.Copy,
                                   scale=1 / W_SCALE).then_inc(proj_hi, 1)
                else:
                    bank, t = J_BANK + c % 2, slice((c - 3) * 4, (c - 2) * 4)
                    act.activation(vals[:, parity, t, :, DH:2 * DH].rearrange("p t h d -> p (t h) d"),
                                   ps[:, bank, :].rearrange("p (t d) -> p t d", d=DH),
                                   ACT.Copy, scale=1 / W_SCALE).then_inc(proj_hi, 1)

            def exp(unit, j):
                act.wait_ge(scores_ready, unit + 1)
                act.wait_ge(lo_done, unit + 1)
                act.activation(expo[:, j % E_RING],
                               ps[:, S_BANK + 2 * (j % 2):S_BANK + 2 * (j % 2) + 2, :].rearrange("p a b -> p (a b)"),
                               ACT.Exp, scale=DH ** -0.5, bias=ln_lo_scale[:, 0:1]).then_inc(exp_done, 1)

            def hi(unit, j):
                act.wait_ge(clip_done, unit + 1)
                act.wait_ge(pv_done, unit + 1)
                act.activation(p_hi[:, j % P_RING], expo[:, j % E_RING], ACT.Copy,
                               scale=1 / LO_SCALE).then_inc(hi_done, 1)

            def out_lo(head):
                act.wait_ge(pv_done, head * 4 + 4 + FREE[pv_done])
                act.wait_ge(o_free, head + FREE[o_free])
                act.activation(o_lo[:], o_all[:, :, 0:DH], ACT.Copy).then_inc(o_lo_done, 1)

            def attn_hi(b, j):
                act.wait_ge(at_ready, b * KI + j + 1)
                act.activation(attn_t[:, 0, j], ps[:, J_BANK + j % 2], ACT.Copy).then_inc(at_hi, 1)

            def latents(b):
                for nth, src, done in ((0, x_in, lat_first), (2, lat, lat_normed)):
                    act.wait_ge(rstd_done, b * 3 + nth + 1)
                    at = 8 + 2 * nth
                    for t in range(NT):
                        ins = act.activation(lat[:, t, :], src[:, t, :], ACT.Identity, bias=shift[:, at + t:at + t + 1],
                                             scale=rstd[:, at + t:at + t + 1])
                    ins.then_inc(done, 1)

            def gate_copy(b):
                act.wait_ge(g_turned, b + 1)
                for k in range(KD):
                    ins = act.activation(xf_t[:, k], ps[:, G_BANK + k], ACT.Copy)
                ins.then_inc(g_copied, 1)

            def start(b, gate):
                for i in range(6):
                    row_w, row_b, k = (ROW_CW, ROW_CB, i // 2) if i < 4 else (ROW_LW, ROW_LB, i - 4)
                    act.wait_ge(turned, b * 6 + i + 1)
                    if i == 0:
                        act.wait_ge(vec_done, 1)
                    act.wait_ge(split_done, b * 6 + i + 1)
                    hi_part = (ctx_hi[:, k, (i % 2) * N:(i % 2) * N + N] if i < 4 else lat_hi[:, k])
                    for out in (affine[:, i % 3], hi_part)[:2 - i % 2]:
                        ins = act.activation(out, ps[:, turned_bank(i)], ACT.Identity, bias=vec_t[:, row_b + k:row_b + k + 1],
                                             scale=vec_t[:, row_w + k:row_w + k + 1])
                    ins.then_inc(affine_done, 1)
                for c in range(5):
                    proj_hi_part(b * KI, c, 0)
                    if c == 1 and gate:
                        gate_copy(b - 1)
                first = b * (KI * UNITS)
                exp(first, 0)
                exp(first + 1, 1)
                hi(first, 0)
                exp(first + 2, 2)
                hi(first + 1, 1)

            def batch(b, more):
                def pair(b, m, parity, last):
                    unit, head = (b * KI + m) * UNITS, (b * KI + m) * 2
                    for j in range(UNITS):
                        if j == UNITS // 2:
                            out_lo(head)
                        if not last or j + LEAD < UNITS:
                            exp(unit + j + LEAD, j + LEAD)
                        if not last or j + LEAD - 1 < UNITS:
                            hi(unit + j + LEAD - 1, j + LEAD - 1)
                        if not last and j < 5:
                            proj_hi_part(b * KI + m + 1, j, 1 - parity)
                        if last and j < KI - 1:
                            attn_hi(b, j)
                    out_lo(head + 1)
                pair_loop(act, b, pair)
                if more:
                    latents(b + 1)
                attn_hi(b, KI - 1)
                if more:
                    start(b + 1, True)
                else:
                    gate_copy(b)
            latents(0)
            act.wait_ge(wkv_loaded, 16)
            for k in range(KD):
                act.activation(wkv_hi[:, k], wkv_in[:, k], ACT.Copy, scale=W_SCALE).then_inc(w_hi_done, 1)
            act.wait_ge(wq_loaded, 16)
            act.activation(wq_hi[:], wq_in, ACT.Copy, scale=W_SCALE).then_inc(w_hi_done, 1)
            act.wait_ge(wo_loaded, 16)
            act.wait_ge(blank_done, 1)
            act.dma_start(T["acc"][TT * P:(TT + 1) * P, :], blank[:, 0:D]).then_inc(acc_cleared, 16)
            act.activation(wo_hi[:], wo_in, ACT.Copy, scale=W_SCALE).then_inc(w_hi_done, 1)
            start(0, False)
            batch_loop(act, batch)
            act.wait_ge(acc_cleared, 16)

        @block.vector
        def _(dve):
            for s in (lo_done, o_free, proj_free, split_done, x1_done):
                dve.sem_inc(s, FREE[s])
            dve.memset(vec_rows[:], 0.0).then_inc(consts, 1)
            dve.memset(ln_lo_scale[:], math.log(LO_SCALE)).then_inc(consts, 1)
            dve.memset(blank[:], 0.0).then_inc(consts, 1)
            dve.memset(vals[:, :, :, :, 2 * DH:VW].rearrange("p a t h d -> p (a t h) d"), 1.0)
            dve.memset(vals_s[:, :, :, :, DH:DH + 2].rearrange("p a t h d -> p (a t h) d"), 1 / LO_SCALE)

            def lo_of(out, full, hi, scale):
                return dve.scalar_tensor_tensor(out=out, in0=full, scalar=scale, in1=hi, op0=ALU.mult, op1=ALU.subtract)

            def proj_lo_part(pairs_before, c, parity):
                dve.wait_ge(proj_hi, pairs_before * 5 + c + 1)
                if c == 0:
                    lo_of(qrys[0:DH, parity, 0, 1], ps[0:DH, J_BANK], qrys[0:DH, parity, 0, 0], 1 / W_SCALE)
                    lo_of(qrys[0:DH, parity, 1, 1], ps[DH:P, J_BANK], qrys[0:DH, parity, 1, 0],
                          1 / W_SCALE).then_inc(proj_free, 1)
                elif c < 3:
                    bank, t = J_BANK + c % 2, slice((c - 1) * 512, c * 512)
                    lo_of(keys[DH:P, parity, 0, t], ps[0:DH, bank], keys[0:DH, parity, 0, t], 1 / W_SCALE)
                    lo_of(keys[0:DH, parity, 1, t], ps[DH:P, bank], keys[DH:P, parity, 1, t],
                          1 / W_SCALE).then_inc(proj_free, 1)
                else:
                    bank, t = J_BANK + c % 2, slice((c - 3) * 4, (c - 2) * 4)
                    v = vals[:, parity, t].rearrange("p t h d -> p (t h) d")
                    dve.tensor_scalar(vals_s[:, parity, t, :, 0:DH].rearrange("p t h d -> p (t h) d"),
                                      v[:, :, DH:2 * DH], 1 / LO_SCALE, None, ALU.mult)
                    lo_of(v[:, :, 0:DH], ps[:, bank, :].rearrange("p (t d) -> p t d", d=DH),
                          v[:, :, DH:2 * DH], 1 / W_SCALE).then_inc(proj_free, 1)

            def clip(unit, j):
                dve.wait_ge(exp_done, unit + 1 + FREE[exp_done])
                e = expo[:, j % E_RING]
                dve.tensor_scalar(e, e, LO_SCALE * math.exp(CLIP), LO_SCALE * math.exp(-CLIP),
                                  ALU.min, ALU.max).then_inc(clip_done, 1)

            def lo(unit, j):
                dve.wait_ge(hi_done, unit + 1)
                dve.scalar_tensor_tensor(out=p_lo[:, j % P_RING], in0=p_hi[:, j % P_RING], scalar=-LO_SCALE,
                                         in1=expo[:, j % E_RING], op0=ALU.mult, op1=ALU.add).then_inc(lo_done, 1)

            def out_sum(head, h):
                dve.wait_ge(o_lo_done, head + 1)
                dve.wait_ge(attn_done, head + 1)
                dve.reciprocal(o_rec[:, h], o_all[:, :, 2 * DH])
                dve.tensor_tensor(o_sum[:, h], o_all[:, :, DH:2 * DH], o_lo[:], ALU.add).then_inc(o_free, 1)

            CHAIN = 3

            def norms(b):
                steps = [0]

                def link(ins):
                    steps[0] += 1
                    ins.then_inc(dve_chain, 1)
                    dve.wait_ge(dve_chain, b * CHAIN + steps[0])

                def tile_moments(tokens, tiles, at, stats_at):
                    for t in range(tiles):
                        ins = dve.bn_stats(stats[:, stats_at + t, :], tokens[:, t, :])
                    link(ins)
                    dve.sem_inc(wait_taken, 1)
                    for t in range(tiles):
                        ins = dve.bn_aggr(mean_var[:, at + t, :], stats[:, stats_at + t, :])
                    return ins

                dve.wait_ge(x_loaded, b * 16 + 16)
                tile_moments(x_in, NT, 8, ST).then_inc(moments, 1)
                dve.wait_ge(ctx_loaded, b * 16 + 16)
                tile_moments(ctx_in, ST, 0, 0).then_inc(moments, 1)
                dve.wait_ge(moments, b * 3 + 1)
                dve.wait_ge(lat_first, b + 1)
                tile_moments(lat, NT, 12, ST).then_inc(moments, 1)
                dve.wait_ge(rstd_done, b * 3 + 2)
                for t in range(ST):
                    ins = dve.tensor_scalar(ctx_in[:, t, :], ctx_in[:, t, :], mean_var[:, t, 0:1], rstd[:, t:t + 1],
                                            ALU.subtract, ALU.mult)
                ins.then_inc(ctx_normed, 1)

            def attn_lo(b, j):
                dve.wait_ge(at_hi, b * KI + j + 1)
                dve.tensor_tensor(attn_t[:, 1, j], ps[:, J_BANK + j % 2], attn_t[:, 0, j], ALU.subtract).then_inc(at_lo, 1)

            def gate_moments(b, nth):
                g = g_stats[:]
                if nth == 0:
                    dve.wait_ge(x1_done, b * NT + NT + FREE[x1_done])
                    dve.sem_inc(wait_taken, 1)
                else:
                    dve.wait_ge(g_normed, b + 1)
                for t in range(NT):
                    tile = x1[:, bass.ds(b * NT + t, 1), :].rearrange("p o d -> p (o d)") if nth == 0 else xn[:, t, :]
                    ins = dve.bn_stats(g[:, t, :], tile)
                ins.then_inc(g_chain, 1)
                dve.wait_ge(g_chain, b * 2 + nth + 1)
                dve.sem_inc(wait_taken, 1)
                for t in range(NT):
                    ins = dve.bn_aggr(g_mean_var[:, nth, t, :], g[:, t, :])
                ins.then_inc(g_moments, 1)

            def gate_norm(b, nth):
                dve.wait_ge(g_rstd_done, b * 2 + nth + 1)
                for t in range(NT):
                    x1_tile, xf_tile = (a[:, bass.ds(b * NT + t, 1), 0:D].rearrange("p o d -> p (o d)") for a in (x1, xf))
                    src, dst = (x1_tile, xn[:, t, :]) if nth == 0 else (xn[:, t, :], xf_tile)
                    ins = dve.tensor_scalar(dst, src, g_mean_var[:, nth, t, 0:1], g_rstd[:, nth, t:t + 1],
                                            ALU.subtract, ALU.mult)
                if nth == 0:
                    ins.then_inc(g_normed, 1)

            def gate_logits(b):
                dve.wait_ge(logits_ready, b + 1)
                dve.tensor_copy(logits[:, bass.ds(b * NT * E, NT * E)], ps[:, LOGIT_BANK, 0:NT * E]).then_inc(logits_done, 1)

            def start(b, gate):
                for i in range(6):
                    hi_, lo_, k = (ctx_hi, ctx_lo, i // 2) if i < 4 else (lat_hi, lat_lo, i - 4)
                    t = slice((i % 2) * N, (i % 2) * N + N) if i < 4 else slice(0, N)
                    dve.wait_ge(affine_done, b * 6 + i + 1)
                    if i % 2:
                        dve.tensor_copy(hi_[:, k, t], affine[:, i % 3]).then_inc(hi_copied, 1)
                        dve.wait_ge(hi_copied, b * 3 + i // 2 + 1)
                    dve.tensor_tensor(lo_[:, k, t], affine[:, i % 3], hi_[:, k, t], ALU.subtract).then_inc(split_done, 1)
                if gate:
                    gate_moments(b - 1, 0)
                for c in range(5):
                    proj_lo_part(b * KI, c, 0)
                    if gate and c == 0:
                        gate_norm(b - 1, 0)
                    if gate and c == 1:
                        gate_moments(b - 1, 1)
                    if gate and c == 2:
                        gate_norm(b - 1, 1)
                    if gate and c == 3:
                        gate_logits(b - 1)
                first = b * (KI * UNITS)
                clip(first, 0)
                clip(first + 1, 1)
                lo(first, 0)
                clip(first + 2, 2)
                lo(first + 1, 1)

            def batch(b, more):
                def pair(b, m, parity, last):
                    unit, head = (b * KI + m) * UNITS, (b * KI + m) * 2
                    for j in range(UNITS):
                        if j == UNITS // 2:
                            out_sum(head, 0)
                        if not last or j + LEAD < UNITS:
                            clip(unit + j + LEAD, j + LEAD)
                        if not last or j + LEAD - 1 < UNITS:
                            lo(unit + j + LEAD - 1, j + LEAD - 1)
                        if not last and j < 5:
                            proj_lo_part(b * KI + m + 1, j, 1 - parity)
                        if last and j < KI - 1:
                            attn_lo(b, j)
                    out_sum(head + 1, 1)
                pair_loop(dve, b, pair)

                def output(n):
                    dve.wait_ge(y_ready, b * NT + n + 1)
                    tile = x1[:, bass.ds(b * NT + n, 1), :].rearrange("p o d -> p (o d)")
                    if n == 0:
                        dve.wait_ge(residual_done, b + 1)
                    dve.scalar_tensor_tensor(out=tile, in0=ps[:, n, 0:D], scalar=1 / W_SCALE, in1=tile,
                                             op0=ALU.mult, op1=ALU.add).then_inc(x1_done, 1)
                if more:
                    norms(b + 1)
                attn_lo(b, KI - 1)
                for n in range(NT):
                    output(n)
                if more:
                    start(b + 1, True)
                else:
                    for nth in range(2):
                        gate_moments(b, nth)
                        gate_norm(b, nth)
                    gate_logits(b)

            norms(0)
            for k in range(KD):
                dve.wait_ge(w_hi_done, k + 1)
                lo_of(wkv_lo[:, k], wkv_in[:, k], wkv_hi[:, k], W_SCALE).then_inc(w_lo_done, 1)
                if k == 0:
                    dve.wait_ge(vec_turned, 1)
                    dve.tensor_copy(vec_t[:], ps[:, 7, 0:P]).then_inc(vec_done, 1)
            dve.wait_ge(w_hi_done, KD + 1)
            lo_of(wq_lo[:], wq_in, wq_hi[:], W_SCALE).then_inc(w_lo_done, 1)
            dve.wait_ge(w_hi_done, KD + 2)
            lo_of(wo_lo[:], wo_in, wo_hi[:], W_SCALE).then_inc(w_lo_done, 1)
            start(0, False)
            batch_loop(dve, batch)

        @block.tensor
        def _(pe):
            pe.sem_inc(pv_done, FREE[pv_done])
            pe.wait_ge(ident_done, 1)
            pe.wait_ge(vec_in, 16 * 7)
            pe.transpose(ps[:, 7, 0:P], vec_rows[:], ident[:]).then_inc(vec_turned, 1)

            def pairs3(out, w_hi, w_lo, x_hi, x_lo, first, last):
                pe.matmul(out, w_hi, x_hi, start=first, stop=False, skip_group_check=True)
                pe.matmul(out, w_hi, x_lo, start=False, stop=False, skip_group_check=True)
                return pe.matmul(out, w_lo, x_hi, start=False, stop=last, skip_group_check=True)

            def project(pairs_before, m, c, parity):
                pe.wait_ge(proj_free, pairs_before * 5 + c + (FREE[proj_free] if c == 0 else 0))
                out = ps[:, J_BANK + c % 2, :]
                if c < 3:
                    w_hi, w_lo = (wq_hi, wq_lo) if c == 0 else (wkv_hi, wkv_lo)
                    x_hi, x_lo = (lat_hi, lat_lo) if c == 0 else (ctx_hi, ctx_lo)
                    t = slice(0, N) if c == 0 else slice((c - 1) * 512, c * 512)
                    for k in range(KD):
                        w = bass.ds(m * P, P)
                        ins = pairs3(out, w_hi[:, k, w], w_lo[:, k, w], x_hi[:, k, t], x_lo[:, k, t],
                                     k == 0, k == KD - 1)
                else:
                    for t4 in range(4):
                        t = slice(((c - 3) * 4 + t4) * P, ((c - 3) * 4 + t4 + 1) * P)
                        for k in range(KD):
                            w = bass.ds(m * P + INNER, P)
                            ins = pairs3(out[:, t4 * P:(t4 + 1) * P], ctx_hi[:, k, t], ctx_lo[:, k, t],
                                         wkv_hi[:, k, w], wkv_lo[:, k, w], k == 0 and t4 == 0, k == KD - 1)
                ins.then_inc(proj_ready, 1)

            def scores(unit, j, parity):
                h, u = j // 4, j % 4
                pe.wait_ge(exp_done, unit + 1)
                for t in range(2):
                    k = keys[:, parity, h, (2 * u + t) * P:(2 * u + t + 1) * P]
                    out = ps[:, S_BANK + 2 * (j % 2) + t, :]
                    pe.matmul(out, k, qrys[:, parity, h, 0], start=True, stop=False)
                    ins = pe.matmul(out, k, qrys[:, parity, h, 1], start=False, stop=True)
                ins.then_inc(scores_ready, 1)

            def values(unit, head, j, parity):
                h, u = j // 4, j % 4
                pe.wait_ge(lo_done, unit + 1 + FREE[lo_done])
                if u == 0:
                    pe.wait_ge(o_free, head + FREE[o_free])
                for t in range(2):
                    st = 2 * u + t
                    for n in range(NT):
                        w = slice(t * N + n * P, t * N + (n + 1) * P)
                        pe.matmul(o_ps(n), p_hi[:, j % P_RING, w], vals[:, parity, st, h, 0:129],
                                  start=st == 0 and n % 2 == 0, stop=False, skip_group_check=True)
                        ins = pe.matmul(o_ps(n)[:, DH:129], p_lo[:, j % P_RING, w], vals_s[:, parity, st, h, 0:65],
                                        start=False, stop=st == ST - 1, skip_group_check=True)
                ins.then_inc(pv_done, 1)

            def need(pairs_before, chunks):
                pe.wait_ge(proj_free, pairs_before * 5 + chunks + FREE[proj_free])
                if chunks == 2:
                    pe.wait_ge(q_twice, (pairs_before + 1) * 16)

            def turn(b, i):
                if i == 0:
                    pe.wait_ge(ctx_normed, b + 1)
                if i == 4:
                    pe.wait_ge(x1_done, b * NT + NT)
                    pe.wait_ge(lat_normed, b + 1)
                src, k, t0 = (ctx_in, i // 2, (i % 2) * 4) if i < 4 else (lat, i - 4, 0)
                for t in range(4):
                    ins = pe.transpose(ps[:, turned_bank(i), t * P:(t + 1) * P],
                                       src[:, t0 + t, k * P:(k + 1) * P], ident[:])
                ins.then_inc(turned, 1)

            def turn_attn(b, j):
                pe.wait_ge(attn_done, b * H + 2 * (j + 1) + FREE[attn_done])
                if j >= 2:
                    pe.wait_ge(at_lo, b * KI + j - 1)
                for n in range(NT):
                    ins = pe.transpose(ps[:, J_BANK + j % 2, n * P:(n + 1) * P], attn[:, n, j * P:(j + 1) * P], ident[:])
                ins.then_inc(at_ready, 1)

            def project_out(n, j):
                t = slice(n * P, (n + 1) * P)
                return pairs3(ps[:, n, 0:D], attn_t[:, 0, j, t], attn_t[:, 1, j, t], wo_hi[:, j], wo_lo[:, j],
                              j == 0, j == KI - 1)

            def gate_turn(b):
                pe.wait_ge(g_normed, b + 1)
                for k in range(KD):
                    for t in range(NT):
                        ins = pe.transpose(ps[:, G_BANK + k, t * P:(t + 1) * P], xn[:, t, k * P:(k + 1) * P], ident[:])
                ins.then_inc(g_turned, 1)

            def gate_logits(b):
                pe.wait_ge(wg_in, 16)
                pe.wait_ge(g_copied, b + 1)
                for t in range(NT):
                    for k in range(KD):
                        ins = pe.matmul(ps[:, LOGIT_BANK, t * E:(t + 1) * E], xf_t[:, k, t * P:(t + 1) * P], wg[:, k],
                                        start=t == 0 and k == 0, stop=k == KD - 1, skip_group_check=True)
                ins.then_inc(logits_ready, 1)

            def start(b, gate):
                turn(b, 4)
                turn(b, 5)
                pe.wait_ge(split_done, b * 6 + 6 + FREE[split_done])
                pe.wait_ge(w_lo_done, KD + 1)
                for c in range(5):
                    project(b * KI, 0, c, 0)
                    if gate and c == 1:
                        gate_turn(b - 1)
                    if gate and c == 2:
                        gate_logits(b - 1)
                need(b * KI, 2)
                need(b * KI, 3)
                first = b * (KI * UNITS)
                for j in range(LEAD):
                    scores(first + j, j, 0)
                if gate:
                    pe.wait_ge(logits_done, b)

            def batch(b, more):
                def pair(b, m, parity, last):
                    before = b * KI + m
                    unit, head = before * UNITS, before * 2
                    for j in range(UNITS):
                        if j + LEAD < UNITS:
                            scores(unit + j + LEAD, j + LEAD, parity)
                        elif not last:
                            if j + LEAD == UNITS:
                                need(before + 1, 2)
                                need(before + 1, 3)
                            scores(unit + j + LEAD, j + LEAD - UNITS, 1 - parity)
                        if not last and j < 5:
                            project(before + 1, m + 1, j, 1 - parity)
                        if j == 0:
                            need(before, 5)
                        if last and j < KI - 1:
                            turn_attn(b, j)
                        values(unit + j, head + j // 4, j, parity)
                pair_loop(pe, b, pair)

                pe.wait_ge(at_lo, b * KI + KI - 1)
                pe.wait_ge(w_lo_done, KD + 2)
                for n in range(NT):
                    for j in range(KI - 1):
                        project_out(n, j)
                turn_attn(b, KI - 1)
                if more:
                    for i in range(2):
                        turn(b + 1, i)
                pe.wait_ge(at_lo, b * KI + KI)
                for n in range(NT):
                    project_out(n, KI - 1).then_inc(y_ready, 1)
                if more:
                    for i in range(2, 4):
                        turn(b + 1, i)
                if more:
                    start(b + 1, True)
                else:
                    gate_turn(b)
                    gate_logits(b)

            for i in range(4):
                if i == 3:
                    pe.wait_ge(vec_done, 1)
                turn(0, i)
            start(0, False)
            batch_loop(pe, batch)


def experts_block(nc, A, T, out):
    rows, acc = T["rows"], T["acc"]
    with ExitStack() as ctx:
        def sb(name, shape, dt):
            return ctx.enter_context(nc.sbuf_tensor(name, shape, dt))

        def sem(name):
            return ctx.enter_context(nc.semaphore(name))

        ident, vec_t, ps = T["ident"], T["vec_t"], T["ps"]
        w_in = w_buffers(T)
        w1 = T["space"][:].bitcast(F16)

        def w1_piece(e, k, part):
            return w1[:, w1_at(e, k, 0, part):w1_at(e, k, 0, part) + F]

        w2 = sb("w2", [P, E * KF * 2 * D], F16)

        def w2_piece(e, i):
            at = w2_at(e, (i - KD) * 4)
            both = w2[:, at:at + 4 * 2 * D].rearrange("p (f c d) -> p f c d", c=2, d=D)
            return both[:, :, 0], both[:, :, 1]

        lnw_all = sb("lnw_all", [P, E * KD], F32)
        b1_all = sb("b1_all", [P, E * KF], F32)
        b2_all = sb("b2_all", [P, E * D], F32)
        xf = T["xf"]
        logits = T["logits"][:].rearrange("p (t e) -> p t e", e=E)
        gate_sums = w2[:, w2_at(E - 1, 0):].bitcast(F32)
        work = w_in[1][:].rearrange("p a c -> p (a c)")
        alpha = sb("alpha", [P, E], F32)
        expert_no, tile_no = sb("expert_no", [P, E], F32), sb("tile_no", [P, TILES], F32)
        before, ones = sb("before", [P, P], F32), sb("ones", [P, P], F32)
        before_h, ones_h, both = sb("before_h", [P, P], F16), sb("ones_h", [P, P], F16), sb("both", [P, TT, E], F16)
        up_to = sb("up_to", [P, E, E], F32)
        gap, gap_exp = sb("gap", [P, TT], F32), sb("gap_exp", [P, TT], F32)
        share = sb("share", [P, 2, TT], F32)
        count_i, tiles_i = sb("count_i", [P, E], I32), sb("tiles_i", [P, E], I32)
        tiles_f = sb("tiles_f", [P, E], F32)
        run_end, run_start = sb("run_end", [P, E], F32), sb("run_start", [P, E], F32)
        place_f, place_u = sb("place_f", [P, 2, TT], F32), sb("place_u", [P, 2, TT], U32)
        owner_f, owner = sb("owner_f", [P, TILES], F32), sb("owner", [P, TILES], I32)
        weights_at = sb("weights_at", [P, TILES], I32)
        x_in, y_out = xf[:, 0:2], xf[:, 2:4, 0:D]
        x_in_bits = xf[:].bitcast(U32)[:, 0:2]
        xt_hi = xf[:, 4, 0:D].bitcast(F16).rearrange("p (s k n) -> p s k n", s=2, k=KD)
        xt_lo = xf[:, 5, 0:D].bitcast(F16).rearrange("p (s k n) -> p s k n", s=2, k=KD)
        mix_next, token_next, token_now = sb("mix_next", [P, 2], F32), sb("token_next", [P, 2], U32), sb("token_now", [P, 2], U32)
        b1_now = sb("b1_now", [P, 2, KF], F32)
        hid = work[:, 0:1024].rearrange("p (h c) -> p h c", h=2)
        hid_hi = work[:, 1024:2048].bitcast(F16).rearrange("p (s h c) -> p s h c", s=2, h=2)
        hid_lo = work[:, 2048:3072].bitcast(F16).rearrange("p (s h c) -> p s h c", s=2, h=2)

        def gate_sum(i, shape):
            a, b = shape
            return gate_sums[:, i * TT * E:i * TT * E + a * b].rearrange("p (a b) -> p a b", b=b)

        top, top_no = (gate_sum(i, (TT, E)) for i in range(2))
        top_at = gate_sum(3, (TT, E)).bitcast(U32)
        chosen = gate_sums[:, 4 * TT * E:6 * TT * E].rearrange("p (c t e) -> p c t e", c=2, e=E)
        scratch, place, part = (gate_sum(i, (TT, E)) for i in range(6, 9))
        passed, scratch_e = gate_sum(9, (TILES, E)), gate_sum(12, (E, E))

        RANK_BANK, COUNT_BANK, BIAS_BANK = 5, 6, 7
        H_BANKS = ((0, 1), (6, 7))
        Y_BANK, X_BANK = 2, 4

        gate_in, gate_const, pool_chain, dve_chain = sem("gate_in"), sem("gate_const"), sem("e_pool_chain"), sem("e_dve_chain")
        w_loaded = [[sem(f"w_loaded{odd}{i}") for i in range(PIECES)] for odd in range(2)]

        def wait_loaded(eng, e, i):
            if e >= AHEAD:
                eng.wait_ge(w_loaded[e % 2][i], (e - AHEAD) // 2 * 16 + 16)

        w_hi_done, w_lo_done, bias_ready, bias_done = sem("e_w_hi"), sem("e_w_lo"), sem("bias_ready"), sem("bias_done")
        lnw_done = sem("lnw_done")
        gap_done, gap_exp_done, chosen_done, ranks_ready = sem("gap_done"), sem("gap_exp_done"), sem("chosen_done"), sem("ranks_ready")
        halves_done, places_done, owners_done, sorted_rows = sem("halves_done"), sem("places_done"), sem("owners_done"), sem("sorted_rows")
        row_loaded = [sem(f"row_loaded{i}") for i in range(2)]
        x_turned, x_hi_done, x_lo_done, b1_picked = sem("x_turned"), sem("x_hi_done"), sem("x_lo_done"), sem("b1_picked")
        h_ready, gelu_done, hid_hi_done, hid_done, hid_used = (
            sem("h_ready"), sem("gelu_done"), sem("hid_hi_done"), sem("hid_done"), sem("hid_used"))
        y_hi_done, y_sum_done, y_done, y_added = sem("y_hi_done"), sem("y_sum_done"), sem("y_done"), sem("y_added")
        meta_picked, row_added, stored, wait_taken = sem("meta_picked"), sem("row_added"), sem("stored"), sem("e_wait_taken")
        FREE = {gelu_done: 4, hid_done: 2, hid_used: 4, x_lo_done: 2, y_done: 2, b1_picked: 1, y_added: 2}

        block = ctx.enter_context(nc.Block())

        def tile_loop(eng, pair):
            with eng.Fori(0, (TILES - 2) // 2) as i:
                pair(i, 3)
            for i in range((TILES - 2) // 2, (TILES + 1) // 2):
                pair(i, TILES - 1 - 2 * i)

        assert TILES % 2 == 1

        @block.sync
        def _(sp):
            for e in range(AHEAD, E):
                for i in range(PIECES):
                    last = e - AHEAD if e - AHEAD < 2 else e - 2
                    sp.wait_ge(w_lo_done, last * PIECES + i + 1)
                    if i < KD:
                        sp.wait_ge(bias_ready, last * KD + i + 1)
                    load_piece(sp, A, w_in[e][:, i], e, i).then_inc(w_loaded[e % 2][i], 16)
            sp.wait_ge(sorted_rows, 2 * TT * 16)
            rows_v = rows.rearrange("(t p) d -> t p d", p=P)
            for t in range(2):
                sp.dma_start(x_in[:, t], rows_v[t]).then_inc(row_loaded[t], 16)
            for t in range(2, 4):
                sp.wait_ge(x_turned, t - 1)
                sp.wait_ge(meta_picked, t - 1)
                sp.dma_start(x_in[:, t % 2], rows_v[t]).then_inc(row_loaded[t % 2], 16)

            def load(t, parity):
                sp.wait_ge(x_turned, t - 1)
                sp.wait_ge(meta_picked, t - 1)
                src = rows_v[t] if isinstance(t, int) else rows_v[bass.ds(t, 1)].rearrange("o p d -> (o p) d")
                sp.dma_start(x_in[:, parity], src).then_inc(row_loaded[parity], 16)

            with sp.Fori(0, (TILES - 4) // 2) as i:
                for parity in range(2):
                    load(2 * i + 4 + parity, parity)
            load(TILES - 1, 0)
            sp.wait_ge(y_added, TILES + FREE[y_added])
            sp.dma_start(out.rearrange("b n d -> (b n) d").rearrange("(p r) d -> p (r d)", p=P),
                         acc[0:TT * P, :].rearrange("(p r) d -> p (r d)", p=P)).then_inc(stored, 16)
            sp.wait_ge(stored, 16)

        @block.gpsimd
        def _(pool):
            pool.iota(expert_no[:], [[1, E]], base=0, channel_multiplier=0, allow_small_or_imprecise_dtypes=True).then_inc(gate_const, 1)
            pool.iota(tile_no[:], [[1, TILES]], base=0, channel_multiplier=0, allow_small_or_imprecise_dtypes=True).then_inc(gate_const, 1)
            pool.memset(ones[:], 1.0).then_inc(gate_const, 1)
            pool.memset(up_to[:], 1.0).then_inc(pool_chain, 1)
            pool.wait_ge(pool_chain, 1)
            pool.wait_ge(gate_const, 3)
            pool.affine_select(out=before[:], in_=ones[:], compare_op=ALU.is_gt, fill=0.0, base=0,
                               pattern=[[1, P]], channel_multiplier=-1).then_inc(gate_const, 1)
            pool.affine_select(out=up_to[:], in_=up_to[:], compare_op=ALU.is_ge, fill=0.0, base=0,
                               pattern=[[1, E], [-1, E]], channel_multiplier=0).then_inc(gate_const, 1)
            pool.iota(xf[:].bitcast(I32)[:, :, ID_AT], [[P, TT]], base=0, channel_multiplier=1).then_inc(gate_const, 1)
            pool.wait_ge(gate_const, 6)
            pool.wait_ge(places_done, 1)
            for t in range(TT):
                for c in range(2):
                    pool.indirect_dma_start(rows, bass.IndirectOffsetOnAxis(ap=place_u[:, c, t:t + 1], axis=0),
                                            xf[:, t, :], None).then_inc(sorted_rows, 16)
            pool.sem_inc(y_added, FREE[y_added])

            def pair(i, more):
                for parity in range(min(more + 1, 2)):
                    t = 2 * i + parity
                    pool.wait_ge(y_done, t + 1 + FREE[y_done])
                    pool.sem_inc(wait_taken, 1)
                    pool.indirect_dma_start(acc, bass.IndirectOffsetOnAxis(ap=token_now[:, parity:parity + 1], axis=0),
                                            y_out[:, parity], None, compute_op=ALU.add).then_inc(row_added, 16)
                    pool.wait_ge(row_added, t * 16 + 16)
                    pool.sem_inc(y_added, 1)
            tile_loop(pool, pair)

        @block.scalar
        def _(act):
            act.sem_inc(gelu_done, FREE[gelu_done])
            act.dma_start(alpha[:], A["L0_ffn_alpha"].partition_broadcast(P)).then_inc(gate_in, 16)
            act.dma_start(b2_all[:], A["L0_ffn_fc2_b"].rearrange("e d -> (e d)").partition_broadcast(P)).then_inc(gate_in, 16)

            def weights_hi(pieces):
                for piece in pieces:
                    e, i = divmod(piece, PIECES)
                    wait_loaded(act, e, i)
                    if e >= AHEAD and i == 0:
                        below = 2 + (e - AHEAD) // 2
                        act.wait_ge(w_lo_done, (below + 1) * PIECES)
                        act.wait_ge(bias_ready, (below + 1) * KD)
                    if i < KD:
                        if piece == 0:
                            act.wait_ge(lnw_done, 1)
                        ins = act.activation(w1_piece(e, i, 0), w_in[e][:, i], ACT.Identity,
                                             scale=lnw_all[:, e * KD + i:e * KD + i + 1])
                    else:
                        ins = act.activation(w2_piece(e, i)[0], w_in[e][:, i].rearrange("p (f d) -> p f d", d=D),
                                             ACT.Copy, scale=F_SCALE)
                    ins.then_inc(w_hi_done, 1)

            weights_hi(range(0, 3))
            act.wait_ge(gap_done, 1)
            act.activation(gap_exp[:], gap[:], ACT.Exp).then_inc(gap_exp_done, 1)
            weights_hi(range(3, E * PIECES))

            def x_hi(t, parity):
                act.wait_ge(x_turned, t + 1)
                act.activation(xt_hi[:, parity].rearrange("p k n -> p (k n)"), ps[:, X_BANK + parity, 0:KD * P],
                               ACT.Copy).then_inc(x_hi_done, 1)

            def gelu(t, parity, half):
                act.wait_ge(h_ready, 2 * t + half + 1)
                act.wait_ge(hid_done, 2 * t + half + 1)
                if half == 0:
                    act.wait_ge(b1_picked, t + 1 + FREE[b1_picked])
                for f in range(4):
                    c = slice(f * P, (f + 1) * P)
                    ins = act.activation(hid[:, half, c], ps[:, H_BANKS[parity][half], c], ACT.Gelu_apprx_tanh,
                                         bias=b1_now[:, parity, half * 4 + f:half * 4 + f + 1], scale=1 / F_SCALE)
                ins.then_inc(gelu_done, 1)

            act.activation(gap_exp[:], gap[:], ACT.Gelu_apprx_tanh)
            x_hi(0, 0)
            x_hi(1, 1)
            for half in range(2):
                gelu(0, 0, half)

            def pair(i, more):
                for parity in range(min(more, 2)):
                    t = 2 * i + parity
                    gelu(t + 1, 1 - parity, 0)
                    if more >= 2 + parity:
                        x_hi(t + 2, parity)
                    gelu(t + 1, 1 - parity, 1)
            tile_loop(act, pair)

        @block.vector
        def _(dve):
            for s in (hid_done, x_lo_done, y_done, b1_picked):
                dve.sem_inc(s, FREE[s])
            chain = [0]

            def link(ins):
                chain[0] += 1
                ins.then_inc(dve_chain, 1)
                dve.wait_ge(dve_chain, chain[0])

            def weights_lo(pieces):
                for piece in pieces:
                    e, i = divmod(piece, PIECES)
                    dve.wait_ge(w_hi_done, piece + 1)
                    if i < KD:
                        full, w_hi, w_lo, scale = w_in[e][:, i], w1_piece(e, i, 0), w1_piece(e, i, 1), lnw_all[:, e * KD + i:e * KD + i + 1]
                    else:
                        full, scale = w_in[e][:, i].rearrange("p (f d) -> p f d", d=D), F_SCALE
                        w_hi, w_lo = w2_piece(e, i)
                    dve.scalar_tensor_tensor(out=w_lo, in0=full, scalar=scale, in1=w_hi,
                                             op0=ALU.mult, op1=ALU.subtract).then_inc(w_lo_done, 1)

            dve.tensor_scalar(lnw_all[:], vec_t[:, ROW_LNW:ROW_LNW + E * KD], F_SCALE, None, ALU.mult).then_inc(lnw_done, 1)
            dve.wait_ge(gate_const, 4)
            dve.tensor_copy(ones_h[:], ones[:]).then_inc(halves_done, 1)
            dve.tensor_copy(before_h[:], before[:]).then_inc(halves_done, 1)
            for t in range(TT):
                ins = dve.max(top[:, t, :], logits[:, t, :])
            link(ins)
            for t in range(TT):
                ins = dve.max_index(top_at[:, t, :], top[:, t, :], logits[:, t, :])
            link(ins)
            dve.tensor_tensor(gap[:], top[:, :, 1], top[:, :, 0], ALU.subtract).then_inc(gap_done, 1)
            link(dve.tensor_copy(top_no, top_at))
            dve.wait_ge(gate_const, 5)
            wide = [P, TT, E]
            for c in range(2):
                ins = dve.tensor_tensor(chosen[:, c], expert_no[:].unsqueeze(1).broadcast_to(wide),
                                        top_no[:, :, c:c + 1].broadcast_to(wide), ALU.is_equal)
            link(ins)
            dve.tensor_tensor(both[:], chosen[:, 0], chosen[:, 1], ALU.add).then_inc(chosen_done, 1)
            dve.wait_ge(gap_exp_done, 1)
            link(dve.tensor_scalar(gap[:], gap_exp[:], 1.0, None, ALU.add))
            link(dve.reciprocal(share[:, 0], gap[:]))
            link(dve.tensor_tensor(share[:, 1], gap_exp[:], share[:, 0], ALU.mult))
            dve.wait_ge(gate_in, 32)
            for c, dst in enumerate((scratch, part)):
                ins = dve.tensor_tensor(dst, chosen[:, c], share[:, c].unsqueeze(2).broadcast_to(wide), ALU.mult)
            link(ins)
            link(dve.tensor_tensor(scratch, scratch, part, ALU.add))
            link(dve.tensor_tensor(xf[:, :, MIX_AT:MIX_AT + E], scratch, alpha[:].unsqueeze(1).broadcast_to(wide), ALU.mult))
            dve.wait_ge(lnw_done, 1)
            weights_lo(range(2))
            dve.wait_ge(ranks_ready, 1)
            link(dve.tensor_scalar(count_i[:], ps[:, COUNT_BANK, 0:E], float(P - 1), None, ALU.add))
            link(dve.tensor_scalar(tiles_i[:], count_i[:], P.bit_length() - 1, None, ALU.logical_shift_right))
            link(dve.tensor_copy(tiles_f[:], tiles_i[:]))
            link(dve.tensor_tensor(scratch_e, tiles_f[:].unsqueeze(1).broadcast_to([P, E, E]), up_to[:], ALU.mult))
            link(dve.tensor_reduce(run_end[:], scratch_e, AX.X, ALU.add))
            link(dve.tensor_tensor(run_start[:], run_end[:], tiles_f[:], ALU.subtract))
            link(dve.tensor_scalar(run_start[:], run_start[:], float(P), None, ALU.mult))
            link(dve.tensor_tensor(place, ps[:, RANK_BANK, 0:TT * E].rearrange("p (t e) -> p t e", e=E),
                                   run_start[:].unsqueeze(1).broadcast_to(wide), ALU.add))
            for c in range(2):
                link(dve.tensor_tensor(scratch, chosen[:, c], place, ALU.mult))
                link(dve.tensor_reduce(place_f[:, c], scratch, AX.X, ALU.add))
            dve.tensor_copy(place_u[:], place_f[:]).then_inc(places_done, 1)
            tiles_wide = [P, TILES, E]
            link(dve.tensor_tensor(passed, tile_no[:].unsqueeze(2).broadcast_to(tiles_wide),
                                   run_end[:].unsqueeze(1).broadcast_to(tiles_wide), ALU.is_ge))
            link(dve.tensor_reduce(owner_f[:], passed, AX.X, ALU.add))
            link(dve.tensor_scalar(owner_f[:], owner_f[:], float(E - 1), None, ALU.min))
            dve.tensor_copy(owner[:], owner_f[:]).then_inc(owners_done, 1)
            dve.tensor_scalar(weights_at[:], owner_f[:], float(2 * KD * F), None, ALU.mult).then_inc(owners_done, 1)
            weights_lo(range(2, E * PIECES))
            dve.wait_ge(bias_ready, E * KD)
            dve.tensor_tensor(b1_all[:], ps[:, BIAS_BANK, 0:E * KF], vec_t[:, ROW_B1:ROW_B1 + E * KF], ALU.add).then_inc(bias_done, 1)
            dve.wait_ge(bias_done, 1)
            dve.wait_ge(owners_done, 2)

            def owner_of(t):
                return dve.value_load(owner[0:1, bass.ds(t, 1)], min_val=0, max_val=E - 1)

            def pick_b1(t, parity):
                dve.tensor_copy(b1_now[:, parity], b1_all[:, bass.ds(owner_of(t) * KF, KF)]).then_inc(b1_picked, 1)

            def x_lo(t, parity):
                dve.wait_ge(x_hi_done, t + 1)
                dve.tensor_tensor(xt_lo[:, parity].rearrange("p k n -> p (k n)"), ps[:, X_BANK + parity, 0:KD * P],
                                  xt_hi[:, parity].rearrange("p k n -> p (k n)"), ALU.subtract).then_inc(x_lo_done, 1)

            def split(t, parity, half):
                dve.wait_ge(gelu_done, 2 * t + half + 1 + FREE[gelu_done])
                dve.wait_ge(hid_used, 2 * t + half + 1)
                dve.tensor_copy(hid_hi[:, parity, half], hid[:, half]).then_inc(hid_hi_done, 1)
                dve.wait_ge(hid_hi_done, 2 * t + half + 1)
                dve.tensor_tensor(hid_lo[:, parity, half], hid[:, half], hid_hi[:, parity, half],
                                  ALU.subtract).then_inc(hid_done, 1)

            def y(t, parity):
                e = owner_of(t)
                dve.wait_ge(hid_used, 2 * t + 2 + FREE[hid_used])
                dve.wait_ge(y_added, t + 1)
                dve.scalar_tensor_tensor(out=y_out[:, parity], in0=ps[:, Y_BANK + parity, 0:D], scalar=1 / F_SCALE,
                                         in1=b2_all[:, bass.ds(e * D, D)], op0=ALU.mult, op1=ALU.add).then_inc(y_hi_done, 1)
                dve.wait_ge(meta_picked, t + 1)
                dve.tensor_copy(token_now[:, parity:parity + 1], token_next[:, parity:parity + 1]).then_inc(y_hi_done, 1)
                dve.wait_ge(y_hi_done, 2 * t + 2)
                dve.scalar_tensor_tensor(out=y_out[:, parity], in0=ps[:, Y_BANK + parity, D:2 * D], scalar=1 / F_SCALE,
                                         in1=y_out[:, parity], op0=ALU.mult, op1=ALU.add).then_inc(y_sum_done, 1)
                dve.wait_ge(y_sum_done, t + 1)
                dve.tensor_scalar(y_out[:, parity], y_out[:, parity], mix_next[:, parity:parity + 1], None,
                                  ALU.mult).then_inc(y_done, 1)

            def pick_meta(t, parity):
                e = owner_of(t)
                dve.wait_ge(y_done, t + 1)
                dve.tensor_copy(token_next[:, parity:parity + 1], x_in_bits[:, parity, ID_AT:ID_AT + 1])
                dve.tensor_copy(mix_next[:, parity:parity + 1], x_in[:, parity, bass.ds(e + MIX_AT, 1)]).then_inc(meta_picked, 1)

            for t in range(2):
                pick_b1(t, t)
                x_lo(t, t)
                pick_meta(t, t)

            for half in range(2):
                split(0, 0, half)

            def pair(i, more):
                for parity in range(min(more + 1, 2)):
                    t = 2 * i + parity
                    if more >= 1 + parity:
                        split(t + 1, 1 - parity, 0)
                    if more >= 2 + parity:
                        x_lo(t + 2, parity)
                        pick_b1(t + 2, parity)
                    if more >= 1 + parity:
                        split(t + 1, 1 - parity, 1)
                    y(t, parity)
                    if more >= 2 + parity:
                        pick_meta(t + 2, parity)
            tile_loop(dve, pair)

        @block.tensor
        def _(pe):
            pe.sem_inc(hid_used, FREE[hid_used])

            def bias_sums(e):
                for k in range(KD):
                    wait_loaded(pe, e, k)
                    for f in range(KF):
                        c = e * KF + f
                        ins = pe.matmul(ps[:, BIAS_BANK, c:c + 1], w_in[e][:, k, f * P:(f + 1) * P],
                                        vec_t[:, ROW_LNB + e * KD + k:ROW_LNB + e * KD + k + 1],
                                        start=e == 0 and k == 0 and f == 0, stop=k == KD - 1, skip_group_check=True)
                    ins.then_inc(bias_ready, 1)

            bias_sums(0)
            pe.wait_ge(chosen_done, 1)
            pe.wait_ge(halves_done, 2)
            pe.matmul(ps[:, RANK_BANK, 0:TT * E], before_h[:], both[:].rearrange("p t e -> p (t e)"),
                      start=True, stop=False, skip_group_check=True)
            for t in range(TT):
                later = TT - 1 - t
                if later:
                    pe.matmul(ps[:, RANK_BANK, (t + 1) * E:TT * E].rearrange("p (t e) -> p t e", e=E), ones_h[:],
                              both[:, t:t + 1, :].broadcast_to([P, later, E]),
                              start=False, stop=False, skip_group_check=True)
                ins = pe.matmul(ps[:, COUNT_BANK, 0:E], ones_h[:], both[:, t, :], start=t == 0, stop=t == TT - 1,
                                skip_group_check=True)
            ins.then_inc(ranks_ready, 1)
            for e in range(1, E):
                bias_sums(e)
            pe.wait_ge(owners_done, 2)

            def weights_of(t):
                return pe.value_load(weights_at[0:1, bass.ds(t, 1)], min_val=0, max_val=(E - 1) * 2 * KD * F)

            def turn(i, t, parity):
                pe.wait_ge(row_loaded[parity], (i + 1) * 16)
                pe.wait_ge(x_lo_done, t + 1)
                for k in range(KD):
                    ins = pe.transpose(ps[:, X_BANK + parity, k * P:(k + 1) * P], x_in[:, parity, k * P:(k + 1) * P], ident[:])
                ins.then_inc(x_turned, 1)

            def fc1_ready(t, half):
                if half == 0:
                    pe.wait_ge(x_lo_done, t + 1 + FREE[x_lo_done])

            def fc1_part(e, parity, half, f):
                out = ps[:, H_BANKS[parity][half], f * P:(f + 1) * P]
                for k in range(KD):
                    w_hi, w_lo = (w1[:, bass.ds(e + w1_at(0, k, half * 4 + f, part), P)] for part in range(2))
                    pe.matmul(out, w_hi, xt_hi[:, parity, k], start=f == 0 and k == 0, stop=False, skip_group_check=True)
                    pe.matmul(out, w_hi, xt_lo[:, parity, k], start=False, stop=False, skip_group_check=True)
                    ins = pe.matmul(out, w_lo, xt_hi[:, parity, k], start=False, stop=k == KD - 1, skip_group_check=True)
                return ins

            def fc1(t, e, parity, half):
                fc1_ready(t, half)
                for f in range(4):
                    ins = fc1_part(e, parity, half, f)
                ins.then_inc(h_ready, 1)

            def fc2_ready(t, half):
                pe.wait_ge(hid_done, 2 * t + half + 1 + FREE[hid_done])

            def fc2_part(e, parity, half, f):
                c, w = slice(f * P, (f + 1) * P), w2[:, bass.ds(e + w2_at(0, half * 4 + f), 2 * D)]
                pe.matmul(ps[:, Y_BANK + parity], hid_hi[:, parity, half, c], w,
                          start=half == 0 and f == 0, stop=False, skip_group_check=True)
                return pe.matmul(ps[:, Y_BANK + parity, 0:D], hid_lo[:, parity, half, c], w[:, 0:D],
                                 start=False, stop=half == 1 and f == 3, skip_group_check=True)

            def fc2(t, e, parity, half):
                fc2_ready(t, half)
                for f in range(4):
                    ins = fc2_part(e, parity, half, f)
                ins.then_inc(hid_used, 1)

            turn(0, 0, 0)
            turn(0, 1, 1)
            pe.wait_ge(w_lo_done, E * PIECES)
            pe.wait_ge(bias_done, 1)

            first = weights_of(0)
            for half in range(2):
                fc1(0, first, 0, half)
            ahead = [pe.alloc_register("even_weights"), pe.alloc_register("odd_weights")]
            pe.reg_mov(ahead[0], first)
            pe.reg_mov(ahead[1], weights_of(1))

            def pair(i, more):
                owners = [pe.snap(r, min_val=0, max_val=(E - 1) * 2 * KD * F) for r in ahead]
                for parity in range(min(more, 2)):
                    t = 2 * i + parity
                    for half in range(2):
                        fc1_ready(t + 1, half)
                        fc2_ready(t, half)
                        for f in range(4):
                            h = fc1_part(owners[parity + 1], 1 - parity, half, f)
                            used = fc2_part(owners[parity], parity, half, f)
                        h.then_inc(h_ready, 1)
                        used.then_inc(hid_used, 1)
                        if half == 0 and more >= 2 + parity:
                            turn(i + 1, t + 2, parity)
                            owners.append(weights_of(t + 2))
                for r, owner_ahead in zip(ahead, owners[2:]):
                    pe.reg_mov(r, owner_ahead)
                if more == 0:
                    for half in range(2):
                        fc2(2 * i, owners[0], 0, half)
            tile_loop(pe, pair)


def program(nc, A, out):
    with ExitStack() as ctx:
        T = {
            "space": ctx.enter_context(nc.sbuf_tensor("space", [P, 16384], F32)),
            "xf": ctx.enter_context(nc.sbuf_tensor("xf", [P, TT, ROW_W], F32)),
            "w_even": ctx.enter_context(nc.sbuf_tensor("w_even", [P, PIECES, 1024], F32)),
            "w_odd": ctx.enter_context(nc.sbuf_tensor("w_odd", [P, PIECES, 1024], F32)),
            "logits": ctx.enter_context(nc.sbuf_tensor("logits", [P, TT * E], F32)),
            "x1": ctx.enter_context(nc.sbuf_tensor("x1", [P, TT, D], F32)),
            "ident": ctx.enter_context(nc.sbuf_tensor("ident", [P, P], F32)),
            "vec_t": ctx.enter_context(nc.sbuf_tensor("vec_t", [P, P], F32)),
            "ps": ctx.enter_context(nc.psum_tensor("ps", [P, 8, 512], F32)),
        }
        T["rows"] = nc.dram_tensor("rows_by_expert", (B * CLEARED * P, ROW_W), F32, kind="Internal").ap()
        T["acc"] = nc.dram_tensor("acc", ((TT + 1) * P, D), F32, kind="Internal").ap()
        attention_block(nc, A, T)
        experts_block(nc, A, T, out)


INPUTS = ["x", "ctx_1024", "L0_xattn_ln_l_w", "L0_xattn_ln_l_b", "L0_xattn_ln_c_w", "L0_xattn_ln_c_b",
          "L0_xattn_Wq", "L0_xattn_Wkv", "L0_xattn_Wo", "L0_xattn_bo", "L0_ffn_Wg", "L0_ffn_alpha",
          "L0_ffn_ln_w", "L0_ffn_ln_b", "L0_ffn_fc1_w", "L0_ffn_fc1_b", "L0_ffn_fc2_w", "L0_ffn_fc2_b"]


def kernel(**inputs):
    import numpy as np
    import concourse.bacc as bacc
    from concourse.bass_utils import run_bass_kernel_spmd

    nc = bacc.Bacc("TRN2", target_bir_lowering=False, num_devices=1)
    arrays, aps = {}, {}
    for name in INPUTS:
        a = np.ascontiguousarray(inputs[name])
        arrays[f"in_{name}"] = a
        aps[name] = nc.dram_tensor(f"in_{name}", a.shape, mybir.dt.from_np(a.dtype), kind="ExternalInput").ap()
    out = nc.dram_tensor("out", (B, N, D), F32, kind="ExternalOutput").ap()
    program(nc, aps, out)
    r = run_bass_kernel_spmd(nc, [arrays], core_ids=[0])
    return r.results[0]["out"]
```
